# Optimizing a Trainium2 kernel written in Bass

```python
import numpy as np
import jax
import jax.numpy as jnp

def _softmax(x, axis=-1):
    return jax.nn.softmax(x, axis=axis)

def _gelu(x):
    return jax.nn.gelu(x, approximate=True)

def _silu(x):
    return jax.nn.silu(x)

def _sigmoid(x):
    return jax.nn.sigmoid(x)

def _layernorm(x, axis=-1, eps=1e-05):
    m = jnp.mean(x, axis=axis, keepdims=True)
    v = jnp.var(x, axis=axis, keepdims=True)
    return (x - m) / jnp.sqrt(v + eps)

def _scatter_add(tgt, idx, src, axis=0):
    return tgt.at[idx].add(src)

def _segment_sum(src, seg, n):
    return jax.ops.segment_sum(src, seg, n)
kernel_name = 'mk_xattn_ffn_d2_seqx_r8_65e5ba'

def setup_inputs(seed: int=0):
    np.random.seed(seed)
    _w = jnp.asarray

    def _rec_inputs():
        import jax
        import jax.numpy as jnp
        _rk = jax.random.key(seed)
        x = 2.818e-05 + 1 * jax.random.normal(jax.random.fold_in(_rk, 1), (128, 64, 128), jnp.float32)
        _lenS = 64 - jax.random.randint(jax.random.fold_in(_rk, 7), (128,), 0, max(1, 64 // 4) + 1, jnp.int32)
        _lenS2 = 64 - jax.random.randint(jax.random.fold_in(_rk, 8), (128,), 0, max(1, 64 // 4) + 1, jnp.int32)
        _ctx_2048P = jax.random.normal(jax.random.fold_in(_rk, 11), (128, 16, 256), jnp.float32)
        _ctx_2048c = jax.random.dirichlet(jax.random.fold_in(_rk, 511), 0.3 * jnp.ones((16,), jnp.float32), (128, 64))
        _ctx_2048t = jnp.einsum('bsk,bkd->bsd', _ctx_2048c, _ctx_2048P)
        _ctx_2048t = _ctx_2048t * jax.lax.rsqrt(jnp.mean(jnp.square(_ctx_2048t)) + 1e-12) * 0.953939
        ctx_2048 = -0.000125008 + 0.999885 * (_ctx_2048t + 0.3 * jax.random.normal(jax.random.fold_in(_rk, 611), (128, 64, 256), jnp.float32))
        _validS = jnp.arange(64)[None, :] < _lenS[:, None]
        _validS2 = jnp.arange(64)[None, :] < _lenS2[:, None]
        _causal = jnp.tril(jnp.ones((64, 64), dtype=bool))
        mask_BxS2_fk1 = jnp.where(jnp.broadcast_to(_validS2[:, :], (128, 64)), 1.0, 0.0).astype(jnp.float32)
        mask_BxS2_if0 = jnp.where(jnp.ones((128, 64), dtype=bool), 4, 0).astype(jnp.int32)
        return (x, ctx_2048, mask_BxS2_fk1, mask_BxS2_if0)
    x, ctx_2048, mask_BxS2_fk1, mask_BxS2_if0 = _rec_inputs()

    def _L0_xattn_setup():
        import jax, jax.numpy as jnp
        import numpy as np
        B, S, T = (32, 64, 64)
        SRC_SIZE, TGT_SIZE, OUT_SIZE, NUM_HEAD = (256, 128, 128, 8)
        HEAD_DIM = OUT_SIZE // NUM_HEAD
        key = jax.random.key(seed)
        ks = jax.random.split(key, 12)
        src = jax.random.normal(ks[0], (B, S, SRC_SIZE), dtype=jnp.float32)
        tgt = jax.random.normal(ks[1], (B, T, TGT_SIZE), dtype=jnp.float32)
        src_mask = (jax.random.uniform(ks[2], (B, S)) > 0.3).astype(jnp.float32)
        src_mask = src_mask.at[:, 0].set(1.0)
        tgt_mask = (jax.random.uniform(ks[3], (B, T)) > 0.3).astype(jnp.float32)
        tgt_mask = tgt_mask.at[:, 0].set(1.0)

        def lin(k, out_f, in_f):
            return jax.random.normal(k, (out_f, in_f), dtype=jnp.float32) / np.sqrt(in_f)
        W_src = lin(ks[4], 2 * OUT_SIZE, SRC_SIZE)
        b_src = jnp.zeros((2 * OUT_SIZE,), jnp.float32)
        W_tgt = lin(ks[5], OUT_SIZE, TGT_SIZE)
        b_tgt = jnp.zeros((OUT_SIZE,), jnp.float32)
        W_out = lin(ks[6], OUT_SIZE, OUT_SIZE + TGT_SIZE)
        b_out = jnp.zeros((OUT_SIZE,), jnp.float32)
        return {'src': src, 'tgt': tgt, 'src_mask': src_mask, 'tgt_mask': tgt_mask, 'W_src': W_src, 'b_src': b_src, 'W_tgt': W_tgt, 'b_tgt': b_tgt, 'W_out': W_out, 'b_out': b_out}
    _L0_xattn_all = _L0_xattn_setup()
    _L0_xattn_in = {k: v for k, v in _L0_xattn_all.items() if k in ('W_src', 'b_src', 'W_tgt', 'b_tgt', 'W_out', 'b_out')}
    del _L0_xattn_all

    def _L0_ffn_setup():
        import jax, jax.numpy as jnp
        import numpy as np
        E, K, H, F = (8, 2, 128, 512)
        B, S = (2, 256)
        key = jax.random.key(seed)
        ks = jax.random.split(key, 12)
        sc = 0.02
        return {'hidden_states': jax.random.normal(ks[0], (B, S, H), jnp.float32), 'router_w': jax.random.normal(ks[1], (H, E), jnp.float32) * sc, 'router_b': jnp.zeros((E,), jnp.float32), 'up_w': jax.random.normal(ks[2], (E, H, F), jnp.float32) * sc, 'up_b': jnp.zeros((E, F), jnp.float32), 'down_w': jax.random.normal(ks[3], (E, F, H), jnp.float32) * sc, 'down_b': jnp.zeros((E, H), jnp.float32), 'sh_up_w': jax.random.normal(ks[4], (H, F), jnp.float32) * sc, 'sh_up_b': jnp.zeros((F,), jnp.float32), 'sh_down_w': jax.random.normal(ks[5], (F, H), jnp.float32) * sc, 'sh_down_b': jnp.zeros((H,), jnp.float32)}
    _L0_ffn_all = _L0_ffn_setup()
    _L0_ffn_in = {k: v for k, v in _L0_ffn_all.items() if k in ('router_w', 'router_b', 'up_w', 'up_b', 'down_w', 'down_b', 'sh_up_w', 'sh_up_b', 'sh_down_w', 'sh_down_b')}
    del _L0_ffn_all

    def _L1_xattn_setup():
        import jax, jax.numpy as jnp
        import numpy as np
        B, L, P = (4, 512, 128)
        D_MODEL = 128
        D_GLOBAL = 256
        HEADDIM = 32
        EPSILON = 0.001
        RMS_EPS = 1e-05

        def rmsnorm(x, g, eps=RMS_EPS):
            var = jnp.mean(jnp.square(x), axis=-1, keepdims=True)
            return x * jax.lax.rsqrt(var + eps) * g

        def _hnet_depool(h, h_patch_full, patch_lens):
            h_patch = h_patch_full[..., :D_MODEL]
            bsz, plen = (h_patch.shape[0], h_patch.shape[1])
            seqlen = h.shape[1]
            logp = jnp.full((bsz, plen), -EPSILON, dtype=jnp.float32)
            bidx = jnp.cumsum(patch_lens, axis=1) - 1
            boundary_mask = jnp.zeros((bsz, seqlen), dtype=jnp.int32)
            boundary_mask = boundary_mask.at[jnp.arange(bsz)[:, None], bidx].set(1)
            dt = (-jnp.log(-jnp.expm1(logp))).astype(h_patch.dtype)
            x = h_patch / dt[..., None]
            n_heads = D_MODEL // HEADDIM
            A = -jnp.ones((n_heads,), dtype=jnp.float32)
            bcoef = jnp.exp(logp).astype(h_patch.dtype)
            x4 = x.reshape(bsz, plen, n_heads, HEADDIM)
            a = jnp.exp(dt[:, :, None] * A[None, None, :])
            u = (dt * bcoef)[:, :, None, None] * x4
            a_b = jnp.broadcast_to(a[..., None], u.shape)

            def comb(lft, rgt):
                aL, uL = lft
                aR, uR = rgt
                return (aL * aR, uL * aR + uR)
            _, s = jax.lax.associative_scan(comb, (a_b, u), axis=1)
            depool = s.reshape(bsz, plen, D_MODEL)
            plug = jnp.clip(jnp.cumsum(boundary_mask, axis=1) - 1, 0, plen - 1)
            depool_out = depool[jnp.arange(bsz)[:, None], plug]
            return depool_out + h
        key = jax.random.key(seed)
        k1, k2, k3, k4 = jax.random.split(key, 4)
        embeds = jax.random.normal(k1, (B, L, D_MODEL), dtype=jnp.float32)
        patch_embeds = jax.random.normal(k2, (B, P, D_GLOBAL), dtype=jnp.float32)
        patch_lens = jnp.full((B, P), L // P, dtype=jnp.int64)
        W_in = jax.random.normal(k3, (D_MODEL, D_MODEL), dtype=jnp.float32) * 0.02
        b_in = jnp.zeros((D_MODEL,), dtype=jnp.float32)
        g_res = jnp.ones((D_MODEL,), dtype=jnp.float32)
        g_init = jnp.ones((D_GLOBAL,), dtype=jnp.float32)
        return {'embeds': embeds, 'patch_embeds': patch_embeds, 'patch_lens': patch_lens, 'W_in': W_in, 'b_in': b_in, 'g_res': g_res, 'g_init': g_init}
    _L1_xattn_all = _L1_xattn_setup()
    _L1_xattn_in = {k: v for k, v in _L1_xattn_all.items() if k in ('W_in', 'b_in', 'g_res', 'g_init')}
    del _L1_xattn_all

    def _L1_ffn_setup():
        import jax, jax.numpy as jnp
        import numpy as np
        import math
        B, S, H = (8, 512, 128)
        E, I, K = (8, 256, 2)
        CAP_FACTOR = 1.0

        def _router(x, expert_embeddings):
            dot = jnp.einsum('bsh,eh->bse', x, expert_embeddings)
            n = dot.shape[0] * dot.shape[1]
            dot2 = dot.reshape(n, E)
            vals, idx = jax.lax.top_k(dot2, K)
            rows = jnp.arange(n)[:, None]
            masked = jnp.full_like(dot2, -jnp.inf).at[rows, idx].set(vals)
            return jax.nn.softmax(masked, axis=-1)
        key = jax.random.key(seed)
        k1, k2, k3, k4 = jax.random.split(key, 4)

        def kaiming(k, shape):
            bound = math.sqrt(3.0 / shape[-1])
            return jax.random.uniform(k, shape, jnp.float32, -bound, bound)
        x = jax.random.normal(k1, (B, S, H), jnp.float32)
        expert_embeddings = kaiming(k2, (E, H))
        first_linear = kaiming(k3, (E, I, H))
        second_linear = kaiming(k4, (E, H, I))
        return {'x': x, 'expert_embeddings': expert_embeddings, 'first_linear': first_linear, 'second_linear': second_linear}
    _L1_ffn_all = _L1_ffn_setup()
    _L1_ffn_in = {k: v for k, v in _L1_ffn_all.items() if k in ('expert_embeddings', 'first_linear', 'second_linear')}
    del _L1_ffn_all
    return {'x': x, 'ctx_2048': ctx_2048, 'mask_BxS2_fk1': mask_BxS2_fk1, 'mask_BxS2_if0': mask_BxS2_if0, 'L0_xattn_W_src': _L0_xattn_in['W_src'], 'L0_xattn_b_src': _L0_xattn_in['b_src'], 'L0_xattn_W_tgt': _L0_xattn_in['W_tgt'], 'L0_xattn_b_tgt': _L0_xattn_in['b_tgt'], 'L0_xattn_W_out': _L0_xattn_in['W_out'], 'L0_xattn_b_out': _L0_xattn_in['b_out'], 'L0_ffn_router_w': _L0_ffn_in['router_w'], 'L0_ffn_router_b': _L0_ffn_in['router_b'], 'L0_ffn_up_w': _L0_ffn_in['up_w'], 'L0_ffn_up_b': _L0_ffn_in['up_b'], 'L0_ffn_down_w': _L0_ffn_in['down_w'], 'L0_ffn_down_b': _L0_ffn_in['down_b'], 'L0_ffn_sh_up_w': _L0_ffn_in['sh_up_w'], 'L0_ffn_sh_up_b': _L0_ffn_in['sh_up_b'], 'L0_ffn_sh_down_w': _L0_ffn_in['sh_down_w'], 'L0_ffn_sh_down_b': _L0_ffn_in['sh_down_b'], 'L1_xattn_W_in': _L1_xattn_in['W_in'], 'L1_xattn_b_in': _L1_xattn_in['b_in'], 'L1_xattn_g_res': _L1_xattn_in['g_res'], 'L1_xattn_g_init': _L1_xattn_in['g_init'], 'L1_ffn_expert_embeddings': _L1_ffn_in['expert_embeddings'], 'L1_ffn_first_linear': _L1_ffn_in['first_linear'], 'L1_ffn_second_linear': _L1_ffn_in['second_linear']}

def reference(x, ctx_2048, mask_BxS2_fk1, mask_BxS2_if0, L0_xattn_W_src, L0_xattn_b_src, L0_xattn_W_tgt, L0_xattn_b_tgt, L0_xattn_W_out, L0_xattn_b_out, L0_ffn_router_w, L0_ffn_router_b, L0_ffn_up_w, L0_ffn_up_b, L0_ffn_down_w, L0_ffn_down_b, L0_ffn_sh_up_w, L0_ffn_sh_up_b, L0_ffn_sh_down_w, L0_ffn_sh_down_b, L1_xattn_W_in, L1_xattn_b_in, L1_xattn_g_res, L1_xattn_g_init, L1_ffn_expert_embeddings, L1_ffn_first_linear, L1_ffn_second_linear):
    import jax
    import jax.numpy as jnp

    def _L0_xattn_ref(src, tgt, src_mask, tgt_mask, W_src, b_src, W_tgt, b_tgt, W_out, b_out):
        import jax, jax.numpy as jnp
        import numpy as np
        B, S, T = (32, 64, 64)
        SRC_SIZE, TGT_SIZE, OUT_SIZE, NUM_HEAD = (256, 128, 128, 8)
        HEAD_DIM = OUT_SIZE // NUM_HEAD
        b, s, _ = src.shape
        t = tgt.shape[1]
        src_trans = jnp.einsum('bsf,of->bso', src, W_src) + b_src
        tgt_trans = jnp.einsum('btf,of->bto', tgt, W_tgt) + b_tgt
        src_trans = src_trans * src_mask[:, :, None]
        tgt_trans = tgt_trans * tgt_mask[:, :, None]
        src_key, src_val = jnp.split(src_trans, 2, axis=2)
        k = src_key.reshape(b, s, NUM_HEAD, HEAD_DIM)
        v = src_val.reshape(b, s, NUM_HEAD, HEAD_DIM)
        q = tgt_trans.reshape(b, t, NUM_HEAD, HEAD_DIM)
        scores = jnp.einsum('bthd,bshd->bhts', q, k) / np.sqrt(HEAD_DIM)
        scores = jnp.where(src_mask[:, None, None, :] == 0, -jnp.inf, scores)
        attn = jax.nn.softmax(scores, axis=-1)
        tgt_update = jnp.einsum('bhts,bshd->bthd', attn, v).reshape(b, t, OUT_SIZE)
        cat_tgt = jnp.concatenate([tgt, tgt_update], axis=2)
        return jnp.einsum('btf,of->bto', cat_tgt, W_out) + b_out

    def _L0_ffn_ref(hidden_states, router_w, router_b, up_w, up_b, down_w, down_b, sh_up_w, sh_up_b, sh_down_w, sh_down_b):
        import jax, jax.numpy as jnp
        import numpy as np
        E, K, H, F = (8, 2, 128, 512)
        B, S = (2, 256)
        x = hidden_states
        router_logits = jnp.einsum('bsh,he->bse', x, router_w) + router_b
        expert_weights = jax.nn.softmax(router_logits, axis=-1)
        top_k_weights, top_k_indices = jax.lax.top_k(expert_weights, K)
        sh = jax.nn.gelu(jnp.einsum('bsh,hf->bsf', x, sh_up_w) + sh_up_b, approximate=False)
        shared_output = jnp.einsum('bsf,fh->bsh', sh, sh_down_w) + sh_down_b
        up = jnp.einsum('bsh,ehf->ebsf', x, up_w) + up_b[:, None, None, :]
        act = jax.nn.gelu(up, approximate=False)
        exp_out = jnp.einsum('ebsf,efh->ebsh', act, down_w) + down_b[:, None, None, :]
        combine = jnp.sum(jax.nn.one_hot(top_k_indices, E, dtype=x.dtype) * top_k_weights[..., None], axis=2)
        expert_output = jnp.einsum('ebsh,bse->bsh', exp_out, combine)
        return x + shared_output + expert_output

    def _L1_xattn_ref(embeds, patch_embeds, patch_lens, W_in, b_in, g_res, g_init):
        import jax, jax.numpy as jnp
        import numpy as np
        B, L, P = (4, 512, 128)
        D_MODEL = 128
        D_GLOBAL = 256
        HEADDIM = 32
        EPSILON = 0.001
        RMS_EPS = 1e-05

        def rmsnorm(x, g, eps=RMS_EPS):
            var = jnp.mean(jnp.square(x), axis=-1, keepdims=True)
            return x * jax.lax.rsqrt(var + eps) * g

        def _hnet_depool(h, h_patch_full, patch_lens):
            h_patch = h_patch_full[..., :D_MODEL]
            bsz, plen = (h_patch.shape[0], h_patch.shape[1])
            seqlen = h.shape[1]
            logp = jnp.full((bsz, plen), -EPSILON, dtype=jnp.float32)
            bidx = jnp.cumsum(patch_lens, axis=1) - 1
            boundary_mask = jnp.zeros((bsz, seqlen), dtype=jnp.int32)
            boundary_mask = boundary_mask.at[jnp.arange(bsz)[:, None], bidx].set(1)
            dt = (-jnp.log(-jnp.expm1(logp))).astype(h_patch.dtype)
            x = h_patch / dt[..., None]
            n_heads = D_MODEL // HEADDIM
            A = -jnp.ones((n_heads,), dtype=jnp.float32)
            bcoef = jnp.exp(logp).astype(h_patch.dtype)
            x4 = x.reshape(bsz, plen, n_heads, HEADDIM)
            a = jnp.exp(dt[:, :, None] * A[None, None, :])
            u = (dt * bcoef)[:, :, None, None] * x4
            a_b = jnp.broadcast_to(a[..., None], u.shape)

            def comb(lft, rgt):
                aL, uL = lft
                aR, uR = rgt
                return (aL * aR, uL * aR + uR)
            _, s = jax.lax.associative_scan(comb, (a_b, u), axis=1)
            depool = s.reshape(bsz, plen, D_MODEL)
            plug = jnp.clip(jnp.cumsum(boundary_mask, axis=1) - 1, 0, plen - 1)
            depool_out = depool[jnp.arange(bsz)[:, None], plug]
            return depool_out + h
        h = rmsnorm(embeds, g_res)
        h = jnp.einsum('bld,ed->ble', h, W_in) + b_in
        h_patch = rmsnorm(patch_embeds, g_init)
        return _hnet_depool(h, h_patch, patch_lens)

    def _L1_ffn_ref(x, expert_embeddings, first_linear, second_linear):
        import jax, jax.numpy as jnp
        import numpy as np
        import math
        B, S, H = (8, 512, 128)
        E, I, K = (8, 256, 2)
        CAP_FACTOR = 1.0

        def _router(x, expert_embeddings):
            dot = jnp.einsum('bsh,eh->bse', x, expert_embeddings)
            n = dot.shape[0] * dot.shape[1]
            dot2 = dot.reshape(n, E)
            vals, idx = jax.lax.top_k(dot2, K)
            rows = jnp.arange(n)[:, None]
            masked = jnp.full_like(dot2, -jnp.inf).at[rows, idx].set(vals)
            return jax.nn.softmax(masked, axis=-1)
        batch, seq, hidden = x.shape
        n_tokens = batch * seq
        expert_capacity = math.ceil(n_tokens / E * CAP_FACTOR)
        weights = _router(x, expert_embeddings)
        ones = (weights > 0).astype(weights.dtype)
        cap_ones = jnp.where(jnp.cumsum(ones, axis=0) <= expert_capacity, ones, 0.0)
        caw = weights * cap_ones
        vals, idx = jax.lax.top_k(caw.T, expert_capacity)
        index = idx.reshape(-1)
        x_flat = x.reshape(n_tokens, hidden)
        tokens = x_flat[index].reshape(E, expert_capacity, hidden)
        inter = jax.nn.relu(jnp.einsum('ech,eih->eci', tokens, first_linear))
        out = jnp.einsum('eci,ehi->ech', inter, second_linear)
        out = out * vals[:, :, None]
        final = jnp.zeros((n_tokens, hidden), x.dtype).at[index].add(out.reshape(-1, hidden))
        return final.reshape(x.shape)
    x = x + _L0_xattn_ref(ctx_2048, _layernorm(x, axis=-1), mask_BxS2_fk1, mask_BxS2_fk1, L0_xattn_W_src, L0_xattn_b_src, L0_xattn_W_tgt, L0_xattn_b_tgt, L0_xattn_W_out, L0_xattn_b_out)
    x = x + _L0_ffn_ref(_layernorm(x, axis=-1), L0_ffn_router_w, L0_ffn_router_b, L0_ffn_up_w, L0_ffn_up_b, L0_ffn_down_w, L0_ffn_down_b, L0_ffn_sh_up_w, L0_ffn_sh_up_b, L0_ffn_sh_down_w, L0_ffn_sh_down_b)
    x = x + _L1_xattn_ref(_layernorm(x, axis=-1), ctx_2048, mask_BxS2_if0, L1_xattn_W_in, L1_xattn_b_in, L1_xattn_g_res, L1_xattn_g_init)
    x = x + _L1_ffn_ref(_layernorm(x, axis=-1), L1_ffn_expert_embeddings, L1_ffn_first_linear, L1_ffn_second_linear)
    return x

_drawn_inputs = setup_inputs


def setup_inputs(seed=0):
    import zlib

    import numpy as np

    out = dict(_drawn_inputs(seed))
    spreads = {'L0_xattn_b_src': (0.0, 0.1),
     'L0_xattn_b_tgt': (0.0, 0.417),
     'L0_xattn_b_out': (0.0, 0.1),
     'L0_ffn_router_b': (0.0, 0.758),
     'L0_ffn_up_b': (0.0, 0.778),
     'L0_ffn_down_b': (0.0, 0.433),
     'L0_ffn_sh_up_b': (0.0, 0.296),
     'L0_ffn_sh_down_b': (0.0, 0.1),
     'L1_xattn_b_in': (0.0, 0.1),
     'L1_xattn_g_res': (1.0, 0.6),
     'L1_xattn_g_init': (1.0, 0.2)}
    factors = {'L0_ffn_router_w': 3.742, 'L0_ffn_up_w': 4.881, 'L0_ffn_down_w': 5.055}
    for name, (base, spread) in spreads.items():
        noise = np.random.default_rng([zlib.crc32(name.encode()), seed]).standard_normal(out[name].shape)
        drawn = base * np.exp(spread * noise) if base else spread * noise
        out[name] = jnp.asarray(drawn.astype(out[name].dtype))
    for name, factor in factors.items():
        out[name] = (out[name] * factor).astype(out[name].dtype)
    return out
```

```python
from contextlib import ExitStack

import numpy as np
import concourse.bass as bass
from concourse import mybir

F32 = mybir.dt.float32
BF16 = mybir.dt.bfloat16
I32 = mybir.dt.int32
U32 = mybir.dt.uint32
ALU = mybir.AluOpType
ACT = mybir.ActivationFunctionType
AX = mybir.AxisListType

P = 128
BATCH, SEQ, H, CTX = 128, 64, 128, 256
TOKENS = BATCH * SEQ
TILES = TOKENS // P
HEADS, HEAD_DIM = 8, 16
PAIRS = HEADS // 2
E0, F0 = 8, 512
E1, F1 = 8, 256
CHUNKS0, CHUNKS1 = F0 // P, F1 // P
CAPACITY = TOKENS // E1
BLOCK = 256
BLOCKS = 2 * TOKENS // BLOCK + E0
SLOTS = BLOCKS * BLOCK
WIDE = 512
RING = 4
SCALE = HEAD_DIM ** -0.5
NEG = -1.0e30
LN_EPS = 1e-5
PATCHES = SEQ
EPSILON = 0.001
OUT_OF_RANGE = 4 * TOKENS

C_ID, C_DECAY, C_BEFORE, C_ONES, C_PART, C_ROW, C_HALF, C_IND, C_IOTA, C_KEEP = 0, 128, 256, 384, 512, 513, 514, 516, 644, 772
C_COLS = C_KEEP + TILES * E0

W_UP, W_DOWN, W_UPB, W_DNB = 0, F0, 2 * F0, 2 * F0 + CHUNKS0
W_COLS = W_DNB + H


def constants():
    c = np.zeros((P, C_COLS), np.float32)
    i = np.arange(P)
    c[:, C_ID:C_ID + P] = np.eye(P)
    dt = -np.log(-np.expm1(np.float64(-EPSILON)))
    lag = (i[:, None] - i[None, :]).astype(np.float64)
    same = (i[:, None] // SEQ == i[None, :] // SEQ) & (lag >= 0)
    c[:, C_DECAY:C_DECAY + P] = np.where(same, np.exp(-EPSILON) * np.exp(-dt * np.maximum(lag, 0)), 0.0)
    c[:, C_BEFORE:C_BEFORE + P] = i[:, None] < i[None, :]
    c[:, C_ONES:C_ONES + P] = 1.0
    c[:, C_PART] = i
    for j in range(2):
        c[:, C_HALF + j] = (i // HEAD_DIM) % 2 == j
        c[j, C_IND:C_IND + P] = i // SEQ == j
    c[:, C_ROW] = SEQ * (i % 2)
    c[:, C_IOTA:C_IOTA + P] = i
    c[:, C_KEEP:] = (np.arange(TILES * E0) % TILES != 0)
    return c


def at_least(eng, sem, n):
    if isinstance(n, int) and n <= 0:
        return
    eng.wait_ge(sem, n)


def wait_alone(eng, sem, n, met, at):
    if isinstance(n, int) and n <= 0:
        return
    if not isinstance(n, int):
        n = eng.to_reg(n)
    eng.wait_ge(met, at)
    eng.wait_ge(sem, n)


def tile_of(a, t):
    if isinstance(t, int):
        return a[:, t, :]
    return a[:, bass.ds(t, 1), :].rearrange("p a c -> p (a c)")


def row_of(a, t):
    if isinstance(t, int):
        return a[t]
    return a[bass.ds(t, 1)].rearrange("a p c -> (a p) c")


def staggered(eng, step, steps, lag, unroll, peel=0):
    for k in range(lag):
        step(k, k % unroll)
    with eng.Fori(lag // unroll, (steps - peel) // unroll) as i:
        for v in range(unroll):
            step(i * unroll + v, v)
    for k in range(steps - peel, steps + lag):
        step(k, k % unroll)


def least(n, most):
    return min(n, most) if isinstance(n, int) else n


def exists(t):
    return not isinstance(t, int) or 0 <= t < TILES


class Mem:

    def __init__(self, nc, ctx):
        self.nc, self.ctx = nc, ctx

    def sb(self, name, shape, dt=F32):
        return self.ctx.enter_context(self.nc.sbuf_tensor(name, shape, dt))

    def ps(self, name, shape, dt=F32):
        return self.ctx.enter_context(self.nc.psum_tensor(name, shape, dt))

    def sem(self, name):
        return self.ctx.enter_context(self.nc.semaphore(name))


def attention_phase(nc, io, keep):
    X, XN, XNT, LOG, C = keep["X"], keep["XN"], keep["XNT"], keep["LOG"], keep["C"]
    with ExitStack() as ctx:
        m = Mem(nc, ctx)
        sb, ps, sem = m.sb, m.ps, m.sem
        ctxT = sb("a_ctxT", [P, RING, 2, 2, 2 * SEQ])
        mrow = sb("a_mrow", [P, RING, P])
        mpair = sb("a_mpair", [2, RING, SEQ])
        mneg = sb("a_mneg", [2, RING, SEQ], BF16)
        mhalf = sb("a_mhalf", [P, RING, 2 * P])
        maskT = sb("a_maskT", [P, BATCH])
        mvj = sb("a_mvj", [P, BATCH, 2])
        half = sb("a_half", [P, 2])
        wq = sb("a_wq", [P, P])
        wk = sb("a_wk", [P, 2 * P])
        wv = sb("a_wv", [P, 2 * P])
        wo = sb("a_wo", [P, 2 * P])
        rw = sb("a_rw", [P, E0])
        cols = sb("a_cols", [P, 3])
        rows = sb("a_rows", [P, 2 * P + E0])
        ind = sb("a_ind", [2, P], BF16)
        eps = sb("a_eps", [P, 2])
        stat = sb("a_stat", [P, RING, 6])
        mv = sb("a_mv", [P, RING, 2])
        ve = sb("a_ve", [P, RING, 1])
        rstd = sb("a_rstd", [P, RING, 1])
        stat2 = sb("a_stat2", [P, RING, 6])
        mv2 = sb("a_mv2", [P, RING, 2])
        ve2 = sb("a_ve2", [P, RING, 1])
        rstd2 = sb("a_rstd2", [P, RING, 1])
        xn = sb("a_xn", [P, RING, P])
        xn2 = sb("a_xn2", [P, RING, P])
        xT = sb("a_xT", [P, RING, 2, P])
        qT = sb("a_qT", [P, 2, P])
        kT = sb("a_kT", [P, 2, 2 * P])
        V = sb("a_V", [P, 2, 2, PAIRS, 2, HEAD_DIM + 1])
        top = sb("a_top", [P, 2, HEADS])
        D = sb("a_D", [P, 2, PAIRS, 2, SEQ])
        PR = sb("a_P", [P, 2, PAIRS, 2 * SEQ])
        PT = sb("a_PT", [P, 2, PAIRS, P])
        rin = sb("a_rin", [P, 2, HEADS])
        upd = sb("a_upd", [P, 2, P])
        updT = sb("a_updT", [P, 2, P])
        zero = sb("a_zero", [P, 2048])

        turned = ps("a_turned", [P, 4, P])
        qkv = ps("a_qkv", [P, 4, P])
        proj = qkv[:, 0, :]
        S = ps("a_S", [P, PAIRS, 512])
        PTp = ps("a_PTp", [P, PAIRS, P])
        O = ps("a_O", [P, 512])
        U = O[:, 0:HEADS * (HEAD_DIM + 1)].rearrange("p (h c) -> p h c", h=HEADS)
        lgp = O[:, 400:400 + E0]

        consts_landed = sem("a_consts_landed")
        zeros_out = sem("a_zeros_out")
        setup = sem("a_setup")
        x_landed = [sem(f"a_x_landed{u}") for u in range(RING)]
        c_landed = [sem(f"a_c_landed{u}") for u in range(RING)]
        names = ("stat mv ve rstd xn xTp xT qkv masks q k v scores top shifted probs PTp PT pv rin upd updTp updT "
                 "proj xb x1 stat2 mv2 ve2 rstd2 xn2 x2 x3 lgp lg kept keptT").split()
        s = {n: sem("a_" + n) for n in names}
        n_consts = 13
        block = ctx.enter_context(nc.Block())

        @block.sync
        def _(sp):
            for dst, src in ((C, io["consts"]), (wq, io["wqT"]), (wk, io["wkT"]), (wv, io["wvT"]), (wo, io["woT"]),
                             (rw, io["L0_ffn_router_w"])):
                sp.dma_start(dst[:], src).then_inc(consts_landed, 16)
            for j, name in enumerate(("L0_xattn_b_tgt", "b_k", "b_v")):
                sp.dma_start(cols[:, j:j + 1], io[name].rearrange("(p o) -> p o", o=1)).then_inc(consts_landed, 16)
            off = 0
            for name in ("L0_xattn_b_out", "L0_ffn_sh_down_b", "L0_ffn_router_b"):
                n = io[name].shape[0]
                sp.dma_start(rows[:, off:off + n], io[name].partition_broadcast(P)).then_inc(consts_landed, 16)
                off += n
            sp.dma_start(maskT[0:SEQ, :], io["maskT"]).then_inc(consts_landed, 16)
            sp.dma_start(maskT[SEQ:P, :], io["maskT"]).then_inc(consts_landed, 16)

            def step(t, u):
                if not exists(t):
                    return
                at_least(sp, s["stat"], t - RING + 1)
                at_least(sp, s["qkv"], t - RING + 1)
                at_least(sp, s["masks"], t - RING + 1)
                at_least(sp, s["q"], t - RING + 1)
                sp.dma_start(tile_of(X, t), row_of(io["x_tiles"], t)).then_inc(x_landed[u], 16)
                sp.dma_start(ctxT[:, u].rearrange("p c b s -> p (c b s)"), row_of(io["ctxT"], t)).then_inc(c_landed[u], 16)
                sp.dma_start(mrow[:, u, :], io["mask_rows"][bass.ds(t, 1)].rearrange("a c -> (a c)")
                             .partition_broadcast(P)).then_inc(c_landed[u], 16)
                sp.dma_start(mpair[:, u, :], row_of(io["mask_pairs"], t)).then_inc(c_landed[u], 16)
            staggered(sp, step, TILES, RING, RING)

        @block.gpsimd
        def _(pool):
            nc.gpsimd.memset(zero[:], 0.0).then_inc(zeros_out, 16)
            nc.gpsimd.memset(V[:], 0.0).then_inc(setup, 1)
            nc.gpsimd.memset(eps[:], -0.5).then_inc(setup, 1)
            nc.gpsimd.memset(half[:], 0.0).then_inc(setup, 1)
            pool.wait_ge(setup, 3)
            for b in range(2):
                for ring in range(2):
                    for j in range(2):
                        nc.gpsimd.memset(V[j * SEQ:(j + 1) * SEQ, ring, b, :, j, HEAD_DIM], 1.0).then_inc(setup, 1)
            for j in range(2):
                nc.gpsimd.memset(half[j * SEQ:(j + 1) * SEQ, j:j + 1], 1.0).then_inc(setup, 1)
            pool.wait_ge(consts_landed, 16 * (n_consts + 1))
            nc.gpsimd.tensor_copy(ind[:], C[0:2, C_IND:C_IND + P]).then_inc(setup, 1)
            pool.wait_ge(setup, 13)
            for j in range(2):
                nc.gpsimd.tensor_scalar(mvj[:, :, j], maskT[:], half[:, j:j + 1], None, ALU.mult).then_inc(setup, 1)
            pool.wait_ge(setup, 15)

            def hold(name, n):
                wait_alone(pool, s[name], n, setup, 15)

            def power(t, u, mvn, ven, mv_, ve_, out, done):
                hold(mvn, t + 1)
                nc.gpsimd.tensor_scalar(ve_[:, u, :], mv_[:, u, 1:2], LN_EPS, None, ALU.add).then_inc(s[ven], 1)
                hold(ven, t + 1)
                nc.gpsimd.tensor_tensor(out[:, u, :], ve_[:, u, :], eps[:, 0:1], ALU.pow).then_inc(s[done], 1)

            def step(k, v):
                t, u = k, v
                if exists(t):
                    power(t, u, "mv", "ve", mv, ve, rstd, "rstd")
                    wait_alone(pool, c_landed[u], 48 * (t // RING + 1) if isinstance(t, int) else (t - u) * 12 + 48,
                               setup, 15)
                    hold("k", t - RING + 1)
                    for j in range(2):
                        nc.gpsimd.tensor_scalar(mhalf[:, u, j * P:(j + 1) * P], mrow[:, u, :],
                                                C[:, C_HALF + j:C_HALF + j + 1], None, ALU.mult)
                    hold("scores", t - RING + 1)
                    nc.gpsimd.tensor_scalar(mneg[:, u, :], mpair[:, u, :], 0.0, NEG, ALU.is_equal,
                                            ALU.mult).then_inc(s["masks"], 1)
                    hold("xn", t + 1)
                    nc.gpsimd.tensor_tensor(tile_of(X, t), tile_of(X, t), rows[:, 0:P], ALU.add).then_inc(s["xb"], 1)
                t, u = k - 3, (v - 3) % RING
                if exists(t):
                    power(t, u, "mv2", "ve2", mv2, ve2, rstd2, "rstd2")
                    hold("xn2", t + 1)
                    nc.gpsimd.tensor_tensor(tile_of(X, t), tile_of(X, t), xn2[:, u, :], ALU.add).then_inc(s["x2"], 1)
                    nc.gpsimd.tensor_copy(tile_of(XN, t), xn2[:, u, :]).then_inc(s["kept"], 1)
                    hold("x2", t + 1)
                    nc.gpsimd.tensor_tensor(tile_of(X, t), tile_of(X, t), rows[:, P:2 * P],
                                            ALU.add).then_inc(s["x3"], 1)
                t, u = k - 4, v
                if exists(t):
                    hold("xT", k + 1)
                    nc.gpsimd.tensor_copy(tile_of(XNT, t), xT[:, u, 1, :]).then_inc(s["keptT"], 1)
            staggered(pool, step, TILES, RING, RING)

        @block.vector
        def _(dve):
            def stats(t, u, src, st, mv_, name, after):
                nc.vector.bn_stats(st[:, u, :], src).then_inc(s[name], 1)
                wait_alone(dve, s[name], t + 1, setup, 15)
                nc.vector.bn_aggr(mv_[:, u, :], st[:, u, :]).then_inc(s[after], 1)

            def first_stats(t, u):
                if exists(t):
                    wait_alone(dve, x_landed[u], 16 * (t // RING + 1) if isinstance(t, int) else (t - u) * 4 + 16,
                               setup, 15)
                    stats(t, u, tile_of(X, t), stat, mv, "stat", "mv")

            dve.wait_ge(setup, 15)
            dve.wait_ge(consts_landed, 16 * (n_consts + 1))
            first_stats(0, 0)

            def step(k, v):
                t, u = k - 3, (v - 3) % RING
                if exists(t):
                    dve.wait_ge(s["xb"], t + 1)
                    dve.wait_ge(s["proj"], t + 1)
                    nc.vector.tensor_tensor(tile_of(X, t), tile_of(X, t), proj, ALU.add).then_inc(s["x1"], 1)
                    wait_alone(dve, s["x1"], t + 1, setup, 15)
                    stats(t, u, tile_of(X, t), stat2, mv2, "stat2", "mv2")
                t, u = k, v
                if exists(t):
                    dve.wait_ge(s["rstd"], t + 1)
                    at_least(dve, s["xTp"], t - RING + 1)
                    nc.vector.tensor_scalar(xn[:, u, :], tile_of(X, t), mv[:, u, 0:1], rstd[:, u, :],
                                            ALU.subtract, ALU.mult).then_inc(s["xn"], 1)
                t, u, w = k - 1, (v - 1) % RING, (v - 1) % 2
                if exists(t):
                    dve.wait_ge(s["scores"], t + 1)
                    Sv = S[:, :, 0:2 * SEQ].rearrange("p g (j s) -> p g j s", j=2)
                    nc.vector.tensor_reduce(top[:, w, :].rearrange("p (g j) -> p g j", j=2), Sv, AX.X,
                                            ALU.max).then_inc(s["top"], 1)
                    dve.wait_ge(s["top"], t + 1)
                    at_least(dve, s["probs"], t - 1)
                    nc.vector.tensor_tensor(D[:, w], Sv, top[:, w, :].rearrange("p (g j) -> p g j", j=2)
                                            .unsqueeze(3).broadcast_to([P, PAIRS, 2, SEQ]),
                                            ALU.subtract).then_inc(s["shifted"], 1)
                t, u, w = k, v, v % 2
                if exists(t):
                    dve.wait_ge(s["qkv"], t + 1)
                    dve.wait_ge(s["masks"], t + 1)
                    nc.vector.scalar_tensor_tensor(qT[:, w, :], qkv[:, 0, :], cols[:, 0:1], mrow[:, u, :],
                                                   ALU.add, ALU.mult).then_inc(s["q"], 1)
                    nc.vector.scalar_tensor_tensor(kT[:, w, :].rearrange("p (j c) -> p j c", j=2),
                                                   qkv[:, 1, :].unsqueeze(1).broadcast_to([P, 2, P]),
                                                   cols[:, 1:2], mhalf[:, u, :].rearrange("p (j c) -> p j c", j=2),
                                                   ALU.add, ALU.mult).then_inc(s["k"], 1)
                    at_least(dve, s["pv"], t - 1)
                    for b in range(2):
                        nc.vector.tensor_tensor(
                            V[:, w, b, :, :, 0:HEAD_DIM],
                            qkv[:, 2 + b, :].rearrange("p (g j d) -> p g j d", g=PAIRS, j=2),
                            mvj[:, bass.ds(2 * t + b, 1), :].unsqueeze(3).broadcast_to([P, 1, 2, HEAD_DIM])
                            .broadcast_to([P, PAIRS, 2, HEAD_DIM]),
                            ALU.mult).then_inc(s["v"], 1)
                t, u, w = k - 2, (v - 2) % RING, (v - 2) % 2
                if exists(t):
                    dve.wait_ge(s["pv"], t + 1)
                    nc.vector.reciprocal(rin[:, w, :], U[:, :, HEAD_DIM]).then_inc(s["rin"], 1)
                    dve.wait_ge(s["rin"], t + 1)
                    at_least(dve, s["updTp"], t - 1)
                    nc.vector.tensor_tensor(upd[:, w, :].rearrange("p (h d) -> p h d", h=HEADS), U[:, :, 0:HEAD_DIM],
                                            rin[:, w, :].unsqueeze(2).broadcast_to([P, HEADS, HEAD_DIM]),
                                            ALU.mult).then_inc(s["upd"], 1)
                t = k - 5
                if exists(t):
                    dve.wait_ge(s["lgp"], t + 1)
                    nc.vector.tensor_tensor(tile_of(LOG, t), lgp, rows[:, 2 * P:2 * P + E0],
                                            ALU.add).then_inc(s["lg"], 1)
                first_stats(k + 1, (v + 1) % RING)
                t, u = k - 3, (v - 3) % RING
                if exists(t):
                    dve.wait_ge(s["rstd2"], t + 1)
                    at_least(dve, s["kept"], t - RING + 1)
                    nc.vector.tensor_scalar(xn2[:, u, :], tile_of(X, t), mv2[:, u, 0:1], rstd2[:, u, :],
                                            ALU.subtract, ALU.mult).then_inc(s["xn2"], 1)
            staggered(dve, step, TILES, 2 * RING, RING, peel=RING)

        @block.tensor
        def _(pe):
            ident = C[:, C_ID:C_ID + P]
            pe.wait_ge(consts_landed, 16 * (n_consts + 1))
            pe.wait_ge(setup, 15)

            def step(k, v):
                t, u = k, v
                if exists(t):
                    pe.wait_ge(s["xn"], t + 1)
                at_least(pe, s["updT"], least(k - 2, TILES))
                if exists(k - 4):
                    pe.wait_ge(s["xn2"], k - 3)
                    mm = nc.tensor.transpose(turned[:, 1, :], xn2[:, u, :], ident)
                if exists(t):
                    mm = nc.tensor.transpose(turned[:, 0, :], xn[:, u, :], ident)
                if exists(k - 4) or exists(t):
                    mm.then_inc(s["xTp"], 1)
                if exists(t):
                    at_least(pe, s["x1"], least(t - 2, TILES))
                    pe.wait_ge(c_landed[u], 48 * (t // RING + 1) if isinstance(t, int) else (t - u) * 12 + 48)
                    at_least(pe, s["q"], t)
                    at_least(pe, s["k"], t)
                    at_least(pe, s["v"], 2 * t)
                    for c in range(2):
                        nc.tensor.matmul(qkv[:, 1, :], wk[:, c * P:(c + 1) * P], ctxT[:, u, c, :, 0:SEQ],
                                         start=c == 0, stop=c == 1)
                    for b in range(2):
                        for c in range(2):
                            nc.tensor.matmul(qkv[:, 2 + b, :], ctxT[:, u, c, b, :], wv[:, c * P:(c + 1) * P], start=c == 0, stop=c == 1)
                    pe.wait_ge(s["xT"], t + 1)
                    nc.tensor.matmul(qkv[:, 0, :], wq[:], xT[:, u, 0, :], start=True, stop=True).then_inc(s["qkv"], 1)
                t, w = k - 1, (v - 1) % 2
                if exists(t):
                    pe.wait_ge(s["probs"], t + 1)
                    at_least(pe, s["PT"], t)
                    for g in range(PAIRS):
                        mm = nc.tensor.transpose(PTp[:, g, :], PR[:, w, g, :], ident)
                    mm.then_inc(s["PTp"], 1)
                t, u, w = k, v, v % 2
                if exists(t):
                    pe.wait_ge(s["masks"], t + 1)
                    at_least(pe, s["shifted"], t)
                    pe.wait_ge(s["q"], t + 1)
                    pe.wait_ge(s["k"], t + 1)
                    for g in range(PAIRS):
                        nc.tensor.matmul(S[:, g, 0:2 * SEQ], ind[:], mneg[:, u, :].unsqueeze(1)
                                         .broadcast_to([2, 2, SEQ]), start=True, stop=True)
                    for g in range(PAIRS):
                        r = slice(32 * g, 32 * g + 32)
                        for b in range(2):
                            keys = kT[r, w, :].rearrange("p (j b s) -> p j b s", j=2, b=2)[:, :, b, :]
                            mm = nc.tensor.matmul(S[b * SEQ:(b + 1) * SEQ, g, 0:2 * SEQ],
                                                  qT[r, w, b * SEQ:(b + 1) * SEQ], keys, start=False, stop=True,
                                                  skip_group_check=True)
                    mm.then_inc(s["scores"], 1)
                at_least(pe, s["upd"], least(k - 1, TILES))
                at_least(pe, s["lg"], least(k - 4, TILES))
                if exists(k - 4):
                    pe.wait_ge(s["xT"], k + 1)
                    nc.tensor.matmul(lgp, xT[:, v, 1, :], rw[:], start=True, stop=True).then_inc(s["lgp"], 1)
                t, w = k - 1, (v - 1) % 2
                if exists(t):
                    pe.wait_ge(s["PT"], t + 1)
                    pe.wait_ge(s["v"], 2 * t + 2)
                    for b in range(2):
                        for g in range(PAIRS):
                            mm = nc.tensor.matmul(O[b * SEQ:(b + 1) * SEQ, g * 34:(g + 1) * 34],
                                                  PT[:, w, g, b * SEQ:(b + 1) * SEQ],
                                                  V[:, w, b, g, :, :], start=True, stop=True)
                    mm.then_inc(s["pv"], 1)
                t, u, w = k - 2, (v - 2) % RING, (v - 2) % 2
                if exists(t):
                    pe.wait_ge(s["upd"], t + 1)
                    nc.tensor.transpose(turned[:, 2, :], upd[:, w, :], ident).then_inc(s["updTp"], 1)
                    at_least(pe, s["v"], least(2 * k + 2, 2 * TILES))
                    at_least(pe, s["q"], least(k + 1, TILES))
                    at_least(pe, s["k"], least(k + 1, TILES))
                    at_least(pe, s["x1"], t)
                    nc.tensor.matmul(proj, xT[:, u, 0, :], wo[:, 0:P], start=True, stop=False)
                    pe.wait_ge(s["updT"], t + 1)
                    nc.tensor.matmul(proj, updT[:, w, :], wo[:, P:2 * P], start=False,
                                     stop=True).then_inc(s["proj"], 1)
            staggered(pe, step, TILES, 2 * RING, RING)

        @block.scalar
        def _(act):
            act.wait_ge(zeros_out, 16)
            for dst in io["zeroed"]:
                act.dma_start(dst, zero[:]).then_inc(zeros_out, 16)
            act.wait_ge(consts_landed, 16 * (n_consts + 1))

            def step(k, v):
                lo, hi = 0 if exists(k) else 1, 2 if exists(k - 4) else 1
                if lo < hi:
                    act.wait_ge(s["xTp"], k + 1)
                    at_least(act, s["keptT"], least(k - 7, TILES))
                    at_least(act, s["lgp"], least(k - 7, TILES))
                    at_least(act, s["proj"], least(k - 3, TILES))
                    nc.scalar.copy(xT[:, v, lo:hi, :], turned[:, lo:hi, :]).then_inc(s["xT"], 1)
                t, w = k - 1, (v - 1) % 2
                if exists(t):
                    act.wait_ge(s["shifted"], t + 1)
                    at_least(act, s["PTp"], t - 1)
                    nc.scalar.activation(PR[:, w].rearrange("p g c -> p (g c)"),
                                         D[:, w].rearrange("p g j c -> p (g j c)"), ACT.Exp,
                                         scale=SCALE).then_inc(s["probs"], 1)
                    act.wait_ge(s["PTp"], t + 1)
                    at_least(act, s["pv"], t - 1)
                    nc.scalar.copy(PT[:, w], PTp[:]).then_inc(s["PT"], 1)
                t, w = k - 2, (v - 2) % 2
                if exists(t):
                    act.wait_ge(s["updTp"], t + 1)
                    at_least(act, s["proj"], t - 1)
                    nc.scalar.activation(updT[:, w, :], turned[:, 2, :], ACT.Identity,
                                         bias=cols[:, 2:3]).then_inc(s["updT"], 1)
            staggered(act, step, TILES, 2 * RING, RING)
            act.wait_ge(zeros_out, 16 + 16 * len(io["zeroed"]))


def route(nc, dve, link, LOG, C, w, rank_ps, total_ps, pe_needs, pe_done, act_needs, act_done, second):
    TE = [P, TILES, E0]

    def over_e(a):
        return a.unsqueeze(2).broadcast_to(TE)

    iota = C[:, C_IOTA:C_IOTA + E0].unsqueeze(1).broadcast_to(TE)
    rest = LOG
    for n in range(2):
        top, hot = w["top"][:, n, :], w["hot"][:, n]
        link(nc.vector.tensor_reduce(top, rest[:], AX.X, ALU.max))
        link(nc.vector.tensor_tensor(w["a"][:], rest[:], over_e(top), ALU.is_equal))
        link(nc.vector.scalar_tensor_tensor(w["b"][:], w["a"][:], -float(E0), iota, ALU.mult, ALU.add))
        link(nc.vector.tensor_reduce(w["t"][:], w["b"][:], AX.X, ALU.min))
        link(nc.vector.tensor_tensor(hot, w["b"][:], over_e(w["t"][:]), ALU.is_equal))
        if n == 0:
            link(nc.vector.scalar_tensor_tensor(w["rest"][:], hot, NEG, LOG[:], ALU.mult, ALU.add))
            rest = w["rest"]
    if second:
        link(nc.vector.tensor_tensor(w["t"][:], w["top"][:, 1, :], w["top"][:, 0, :], ALU.subtract), act_needs)
    else:
        link(nc.vector.tensor_tensor(w["a"][:], LOG[:], over_e(w["top"][:, 0, :]), ALU.subtract))
        link(nc.vector.tensor_tensor(w["t"][:], w["top"][:, 1, :], w["top"][:, 0, :], ALU.subtract), act_needs)
    dve.wait_ge(act_done, 1)
    if second:
        link(nc.vector.tensor_scalar(w["sum"][:], w["exp2"][:], 1.0, None, ALU.add))
        link(nc.vector.reciprocal(w["w"][:, 0, :], w["sum"][:]))
        link(nc.vector.tensor_tensor(w["w"][:, 1, :], w["exp2"][:], w["w"][:, 0, :], ALU.mult))
        link(nc.vector.tensor_scalar(w["t"][:], w["w"][:, 1, :], 0.0, None, ALU.is_gt))
        link(nc.vector.tensor_tensor(w["a"][:], w["hot"][:, 1], over_e(w["t"][:]), ALU.mult))
        link(nc.vector.tensor_tensor(w["chosen"][:], w["a"][:], w["hot"][:, 0], ALU.add), pe_needs)
    else:
        link(nc.vector.tensor_reduce(w["sum"][:], w["b"][:], AX.X, ALU.add))
        link(nc.vector.reciprocal(w["w"][:, 0, :], w["sum"][:]))
        link(nc.vector.tensor_tensor(w["w"][:, 1, :], w["exp2"][:], w["w"][:, 0, :], ALU.mult))
        link(nc.vector.tensor_tensor(w["chosen"][:], w["hot"][:, 0], w["hot"][:, 1], ALU.add), pe_needs)
    dve.wait_ge(pe_done, 1)
    link(nc.vector.tensor_tensor_scan(w["upto"][:], C[:, C_KEEP:C_KEEP + TILES * E0], total_ps[:], 0.0,
                                      ALU.mult, ALU.add))
    link(nc.vector.tensor_tensor(w["rank"][:], w["upto"][:], total_ps[:], ALU.subtract))
    link(nc.vector.tensor_tensor(w["rank"][:], w["rank"][:], rank_ps[:], ALU.add))
    rank = w["rank"][:].rearrange("p (e t) -> p e t", e=E0)
    if second:
        link(nc.vector.tensor_scalar(w["upto"][:], w["rank"][:], float(CAPACITY), float(OUT_OF_RANGE),
                                     ALU.is_ge, ALU.mult))
        link(nc.vector.tensor_tensor(w["rank"][:], w["rank"][:], w["upto"][:], ALU.add))
        link(nc.vector.tensor_scalar(w["base"][:], C[:, C_IOTA:C_IOTA + E0], float(CAPACITY), None, ALU.mult))
    else:
        count = w["upto"][:].rearrange("p (e t) -> p e t", e=E0)[:, :, TILES - 1]
        full = TOKENS // BLOCK
        link(nc.vector.tensor_scalar(w["steps"][:], C[:, C_IOTA:C_IOTA + full], float(BLOCK), None, ALU.mult))
        link(nc.vector.tensor_tensor(w["over"][:], count.unsqueeze(2).broadcast_to([P, E0, full]),
                                     w["steps"][:].unsqueeze(1).broadcast_to([P, E0, full]), ALU.is_gt))
        link(nc.vector.tensor_reduce(w["blocks"][:], w["over"][:], AX.X, ALU.add))
        link(nc.vector.tensor_tensor_scan(w["last"][:], C[:, C_ONES:C_ONES + E0], w["blocks"][:], 0.0,
                                          ALU.mult, ALU.add))
        link(nc.vector.tensor_tensor(w["first"][:], w["last"][:], w["blocks"][:], ALU.subtract))
        link(nc.vector.tensor_scalar(w["base"][:], w["first"][:], float(BLOCK), None, ALU.mult))
        one = [1, BLOCKS, E0]
        link(nc.vector.tensor_tensor(w["owns"][:], w["first"][0:1, :].unsqueeze(1).broadcast_to(one),
                                     C[0:1, C_IOTA:C_IOTA + BLOCKS].unsqueeze(2).broadcast_to(one), ALU.is_le))
        link(nc.vector.tensor_reduce(w["owner_f"][:], w["owns"][:], AX.X, ALU.add))
        link(nc.vector.tensor_scalar(w["owner"][:], w["owner_f"][:], -1.0, None, ALU.add))
    link(nc.vector.tensor_tensor(rank, rank, w["base"][:].unsqueeze(2).broadcast_to([P, E0, TILES]), ALU.add))
    for n in range(2):
        link(nc.vector.tensor_tensor(w["a"][:], w["hot"][:, n], rank.rearrange("p e t -> p t e"), ALU.mult))
        slot = w["slot_f"][:, n, :]
        link(nc.vector.tensor_reduce(slot, w["a"][:], AX.X, ALU.add))
        if second:
            weight = w["w"][:, n, :]
            link(nc.vector.tensor_scalar(w["t"][:], weight, 0.0, float(OUT_OF_RANGE), ALU.is_le, ALU.mult))
            link(nc.vector.tensor_tensor(slot, slot, w["t"][:], ALU.add))
            link(nc.vector.tensor_scalar(w["t"][:], slot, float(TOKENS), None, ALU.is_lt))
            link(nc.vector.tensor_tensor(weight, weight, w["t"][:], ALU.mult))
    return nc.vector.tensor_copy(w["slot"][:].rearrange("p t n -> p n t"), w["slot_f"][:])


def route_buffers(m, keep, tag):
    sb = m.sb
    w = {n: sb(tag + n, [P, TILES, E0]) for n in ("a", "b", "rest")}
    w.update({n: sb(tag + n, [P, E0 * TILES]) for n in ("upto", "rank")})
    w.update({n: sb(tag + n, [P, TILES]) for n in ("t", "sum", "exp2")})
    w.update({n: sb(tag + n, [P, E0]) for n in ("blocks", "last", "first", "base")})
    w.update(hot=sb(tag + "hot", [P, 2, TILES, E0]), chosen=sb(tag + "chosen", [P, TILES, E0], BF16),
             top=sb(tag + "top", [P, 2, TILES]), slot_f=sb(tag + "slot_f", [P, 2, TILES]),
             steps=sb(tag + "steps", [P, TOKENS // BLOCK]), over=sb(tag + "over", [P, E0, TOKENS // BLOCK]),
             owns=sb(tag + "owns", [1, BLOCKS, E0]), owner_f=sb(tag + "owner_f", [1, BLOCKS]),
             owner=keep["OWNER"], w=keep["W"], slot=keep["SLOT"],
             before=sb(tag + "before", [P, P], BF16), ones=sb(tag + "ones", [P, P], BF16))
    return w


def route_exps(nc, act, w, needs, done, second):
    act.wait_ge(needs, 1)
    if not second:
        nc.scalar.activation(w["b"][:], w["a"][:], ACT.Exp)
    nc.scalar.activation(w["exp2"][:], w["t"][:], ACT.Exp).then_inc(done, 1)


def route_counts(nc, pe, w, rank_ps, total_ps, tables, needs, done):
    pe.wait_ge(tables, 2)
    pe.wait_ge(needs, 1)
    chosen = w["chosen"][:].rearrange("p t e -> p e t")
    nc.tensor.matmul(rank_ps[:], w["before"][:], chosen, start=True, stop=True)
    nc.tensor.matmul(total_ps[:], w["ones"][:], chosen, start=True, stop=True).then_inc(done, 1)


def scatter_rows(nc, pool, keep, rows, index, slots_ready, sems, dst, most):
    copied, sent = sems["copied"], sems["sent"]
    pool.wait_ge(slots_ready, 1)

    def step(t, u):
        if not isinstance(t, int) or t >= RING:
            wait_alone(pool, sent[u], 32 * (t // RING) if isinstance(t, int) else (t - u) * 8, slots_ready, 1)
        nc.gpsimd.tensor_copy(rows[:, u, :], tile_of(keep["XN"], t)).then_inc(copied, 1)
        for n in range(2):
            nc.gpsimd.tensor_copy(index[:, n, u:u + 1], keep["SLOT"][:, bass.ds(t, 1), n]).then_inc(copied, 1)
        wait_alone(pool, copied, 3 * t + 3, slots_ready, 1)
        for n in range(2):
            nc.gpsimd.indirect_dma_start(dst, bass.IndirectOffsetOnAxis(ap=index[:, n, u:u + 1], axis=0),
                                         rows[:, u, :], None, bounds_check=most - 1,
                                         oob_is_err=False).then_inc(sent[u], 16)
    for t in range(RING):
        step(t, t)
    with pool.Fori(1, TILES // RING) as i:
        for u in range(RING):
            step(i * RING + u, u)
    for u in range(RING):
        pool.wait_ge(sent[u], 32 * (TILES // RING))


def shared_phase(nc, io, keep):
    X, XNT, C = keep["X"], keep["XNT"], keep["C"]
    GROUPS, SUB = TOKENS // WIDE, WIDE // P
    with ExitStack() as ctx:
        m = Mem(nc, ctx)
        sb, ps, sem = m.sb, m.ps, m.sem
        w = route_buffers(m, keep, "b_")
        rows, index = sb("b_rows", [P, RING, P]), sb("b_index", [P, 2, RING], U32)
        WS = sb("b_W", [P, W_COLS])
        up, upb = WS[:, W_UP:W_UP + F0], WS[:, W_UPB:W_UPB + CHUNKS0]
        down = WS[:, W_DOWN:W_DOWN + F0].rearrange("p (c h) -> p c h", c=CHUNKS0)
        G = sb("b_G", [P, 2, CHUNKS0, WIDE])
        lens_i, lens = sb("b_lens_i", [P, PATCHES], I32), sb("b_lens", [P, PATCHES])
        ends, neg, mark = sb("b_ends", [P, PATCHES]), sb("b_neg", [P, PATCHES]), sb("b_mark", [P, SEQ])
        hits, plug = sb("b_hits", [P, SEQ, PATCHES]), sb("b_plug", [P, SEQ])
        hid = ps("b_hid", [P, CHUNKS0, WIDE])
        y = ps("b_y", [P, 2, WIDE])
        rank_ps, total_ps = ps("b_rank_ps", [P, WIDE]), ps("b_total_ps", [P, WIDE])
        s = {n: sem("b_" + n) for n in ("landed chain exps_wanted exps counts_wanted counts tables slots hid gelu y "
                                        "added plugged copied").split()}
        sent = [sem(f"b_sent{u}") for u in range(RING)]
        block = ctx.enter_context(nc.Block())

        @block.sync
        def _(sp):
            sp.dma_start(WS[:], io["shared_w"]).then_inc(s["landed"], 16)
            sp.dma_start(lens_i[:], io["mask_BxS2_if0"]).then_inc(s["landed"], 16)
            sp.wait_ge(s["plugged"], 1)
            sp.dma_start(io["plug"], plug[:]).then_inc(s["landed"], 16)
            sp.wait_ge(s["landed"], 48)

        @block.gpsimd
        def _(pool):
            nc.gpsimd.tensor_copy(w["before"][:], C[:, C_BEFORE:C_BEFORE + P]).then_inc(s["tables"], 1)
            nc.gpsimd.tensor_copy(w["ones"][:], C[:, C_ONES:C_ONES + P]).then_inc(s["tables"], 1)
            scatter_rows(nc, pool, keep, rows, index, s["slots"], {"copied": s["copied"], "sent": sent},
                         io["xg0"], SLOTS)

        @block.scalar
        def _(act):
            route_exps(nc, act, w, s["exps_wanted"], s["exps"], second=False)
            act.wait_ge(s["landed"], 32)

            def step(k, v):
                for c in range(CHUNKS0):
                    act.wait_ge(s["hid"], CHUNKS0 * k + c + 1)
                    if c == 0:
                        at_least(act, s["y"], k - 1)
                    nc.scalar.activation(G[:, v, c, :], hid[:, c, :], ACT.Gelu,
                                         bias=upb[:, c:c + 1]).then_inc(s["gelu"], 1)
            step(0, 0)
            step(1, 1)
            with act.Fori(1, GROUPS // 2) as i:
                step(2 * i, 0)
                step(2 * i + 1, 1)

        @block.tensor
        def _(pe):
            pe.wait_ge(s["landed"], 32)
            xt = XNT[:].rearrange("p (g t) c -> p g (t c)", g=GROUPS)

            def step(k, v):
                if not isinstance(k, int) or k < GROUPS:
                    for c in range(CHUNKS0):
                        at_least(pe, s["gelu"], CHUNKS0 * (k - 1) + c + 1)
                        nc.tensor.matmul(hid[:, c, :], up[:, c * P:(c + 1) * P], tile_of(xt, k), start=True,
                                         stop=True).then_inc(s["hid"], 1)
                k, v = k - 1, (v - 1) % 2
                if not isinstance(k, int) or k >= 0:
                    pe.wait_ge(s["gelu"], CHUNKS0 * (k + 1))
                    at_least(pe, s["added"], k - 1)
                    for t in range(SUB):
                        for c in range(CHUNKS0):
                            mm = nc.tensor.matmul(y[:, v, t * P:(t + 1) * P], G[:, v, c, t * P:(t + 1) * P],
                                                  down[:, c, :], start=c == 0, stop=c == CHUNKS0 - 1)
                    mm.then_inc(s["y"], 1)
            step(0, 0)
            step(1, 1)
            route_counts(nc, pe, w, rank_ps, total_ps, s["tables"], s["counts_wanted"], s["counts"])
            with pe.Fori(1, GROUPS // 2) as i:
                step(2 * i, 0)
                step(2 * i + 1, 1)
            step(GROUPS, 0)

        @block.vector
        def _(dve):
            count = [0]

            def link(ins, also=None):
                count[0] += 1
                ins.then_inc(s["chain"], 1)
                dve.wait_ge(s["chain"], count[0])
                if also is not None:
                    dve.sem_inc(also, 1)

            route(nc, dve, link, keep["LOG"], C, w, rank_ps, total_ps, s["counts_wanted"], s["counts"],
                  s["exps_wanted"], s["exps"], second=False).then_inc(s["slots"], 1)
            xv = X[:].rearrange("p (g t) c -> p g (t c)", g=GROUPS)

            def step(k, v):
                dve.wait_ge(s["y"], k + 1)
                nc.vector.tensor_tensor(tile_of(xv, k), tile_of(xv, k), y[:, v, :], ALU.add).then_inc(s["added"], 1)
            with dve.Fori(0, GROUPS // 2) as i:
                step(2 * i, 0)
                step(2 * i + 1, 1)
            dve.wait_ge(s["landed"], 32)
            link(nc.vector.tensor_copy(lens[:], lens_i[:]))
            ones = C[:, C_ONES:C_ONES + PATCHES]
            link(nc.vector.tensor_tensor_scan(ends[:], ones, lens[:], 0.0, ALU.mult, ALU.add))
            link(nc.vector.tensor_scalar(ends[:], ends[:], -1.0, None, ALU.add))
            link(nc.vector.tensor_scalar(neg[:], ends[:], 0.0, float(SEQ), ALU.is_lt, ALU.mult))
            link(nc.vector.tensor_tensor(ends[:], ends[:], neg[:], ALU.add))
            box = [P, SEQ, PATCHES]
            link(nc.vector.tensor_tensor(hits[:], ends[:].unsqueeze(1).broadcast_to(box),
                                         C[:, C_IOTA:C_IOTA + SEQ].unsqueeze(2).broadcast_to(box), ALU.is_equal))
            link(nc.vector.tensor_reduce(mark[:], hits[:], AX.X, ALU.max))
            link(nc.vector.tensor_tensor_scan(plug[:], ones, mark[:], 0.0, ALU.mult, ALU.add))
            link(nc.vector.tensor_scalar(plug[:], plug[:], -1.0, 0.0, ALU.add, ALU.max))
            nc.vector.tensor_scalar(plug[:], plug[:], float(PATCHES - 1), C[:, C_ROW:C_ROW + 1], ALU.min,
                                    ALU.add).then_inc(s["plugged"], 1)


def experts_phase(nc, io, keep):
    C, OWNER = keep["C"], keep["OWNER"]
    SUB = BLOCK // P
    with ExitStack() as ctx:
        m = Mem(nc, ctx)
        sb, ps, sem = m.sb, m.ps, m.sem
        WE = sb("e_W", [P, E0, W_COLS])
        W = sb("e_w", [P, 2, W_COLS])
        rows = sb("e_rows", [P, RING, SUB, P])
        xT = sb("e_xT", [P, 2, BLOCK])
        G = sb("e_G", [P, 2, CHUNKS0, BLOCK])
        Y = sb("e_Y", [P, RING, SUB, P])
        xTp = ps("e_xTp", [P, 2, 512])
        hid = ps("e_hid", [P, 2, CHUNKS0, BLOCK])
        yp = ps("e_yp", [P, 2, 512])
        s = {n: sem("e_" + n) for n in "weights w xTp xT hid gelu yp y".split()}
        landed = [sem(f"e_landed{u}") for u in range(RING)]
        stored = [sem(f"e_stored{u}") for u in range(RING)]
        n_w = E0
        src = io["xg0"].rearrange("(k n p) c -> k p n c", p=P, n=SUB)
        dst = io["yg0"].rearrange("(k n p) c -> k p n c", p=P, n=SUB)
        block = ctx.enter_context(nc.Block())

        def blk(a, k):
            return a[k] if isinstance(k, int) else a[bass.ds(k, 1)].rearrange("a p n c -> (a p) n c")

        def real(k):
            return not isinstance(k, int) or 0 <= k < BLOCKS

        @block.sync
        def _(sp):
            for e in range(E0):
                sp.dma_start(WE[:, e, :], io["expert_w"][e]).then_inc(s["weights"], 16)

            def step(k, v):
                if real(k):
                    at_least(sp, s["xTp"], k - RING + 1)
                    sp.dma_start(rows[:, v], blk(src, k)).then_inc(landed[v], 16)
                k, v = k - 4, v
                if real(k):
                    sp.wait_ge(s["y"], k + 1)
                    sp.dma_start(blk(dst, k), Y[:, v]).then_inc(stored[v], 16)
            staggered(sp, step, BLOCKS, RING, RING)
            for u in range(RING):
                sp.wait_ge(stored[u], 16 * (BLOCKS // RING))

        @block.gpsimd
        def _(pool):
            pool.wait_ge(s["weights"], 16 * n_w)

            def step(k, v):
                wait_alone(pool, s["y"], k - 1, s["weights"], 16 * n_w)
                e = pool.value_load(OWNER[0:1, bass.ds(k, 1)], min_val=0, max_val=E0 - 1)
                nc.gpsimd.tensor_copy(W[:, v, :], tile_of(WE, e)).then_inc(s["w"], 1)
            step(0, 0)
            step(1, 1)
            with pool.Fori(1, BLOCKS // 2) as i:
                step(2 * i, 0)
                step(2 * i + 1, 1)

        @block.tensor
        def _(pe):
            ident = C[:, C_ID:C_ID + P]

            def step(k, v):
                if real(k):
                    pe.wait_ge(landed[v], 16 * (k // RING + 1) if isinstance(k, int) else (k - v) * 4 + 16)
                    at_least(pe, s["xT"], k - 1)
                    for n in range(SUB):
                        mm = nc.tensor.transpose(xTp[:, v % 2, n * P:(n + 1) * P], rows[:, v, n, :], ident)
                    mm.then_inc(s["xTp"], 1)
                k, v = k - 1, (v - 1) % 2
                if real(k):
                    pe.wait_ge(s["w"], k + 1)
                    pe.wait_ge(s["xT"], k + 1)
                    at_least(pe, s["gelu"], 2 * k - 2)
                    for c in range(CHUNKS0):
                        mm = nc.tensor.matmul(hid[:, v, c, :], W[:, v, W_UP + c * P:W_UP + (c + 1) * P], xT[:, v, :],
                                              start=True, stop=True)
                        if c % 2 == 1:
                            mm.then_inc(s["hid"], 1)
                k, v = k - 1, (v - 1) % 2
                if real(k):
                    pe.wait_ge(s["gelu"], 2 * k + 2)
                    at_least(pe, s["y"], k - 1)
                    for n in range(SUB):
                        for c in range(CHUNKS0):
                            mm = nc.tensor.matmul(yp[:, v, n * P:(n + 1) * P], G[:, v, c, n * P:(n + 1) * P],
                                                  W[:, v, W_DOWN + c * P:W_DOWN + (c + 1) * P], start=c == 0,
                                                  stop=c == CHUNKS0 - 1)
                    mm.then_inc(s["yp"], 1)
            staggered(pe, step, BLOCKS, RING, RING)

        @block.scalar
        def _(act):
            def step(k, v):
                v = v % 2
                at_least(act, s["yp"], k - 1)
                for c in range(CHUNKS0):
                    if c % 2 == 0:
                        act.wait_ge(s["hid"], 2 * k + c // 2 + 1)
                    a = nc.scalar.activation(G[:, v, c, :], hid[:, v, c, :], ACT.Gelu,
                                             bias=W[:, v, W_UPB + c:W_UPB + c + 1])
                    if c % 2 == 1:
                        a.then_inc(s["gelu"], 1)
            step(0, 0)
            step(1, 1)
            with act.Fori(1, BLOCKS // 2) as i:
                step(2 * i, 0)
                step(2 * i + 1, 1)

        @block.vector
        def _(dve):
            def step(k, v):
                if real(k):
                    dve.wait_ge(s["xTp"], k + 1)
                    at_least(dve, s["hid"], 2 * k - 2)
                    nc.vector.tensor_copy(xT[:, v % 2, :], xTp[:, v % 2, 0:BLOCK]).then_inc(s["xT"], 1)
                k, v = k - 2, (v - 2) % RING
                if real(k):
                    dve.wait_ge(s["yp"], k + 1)
                    if not isinstance(k, int) or k >= RING:
                        dve.wait_ge(stored[v], 16 * (k // RING) if isinstance(k, int) else (k - v) * 4)
                    nc.vector.tensor_tensor(Y[:, v], yp[:, v % 2, 0:BLOCK].rearrange("p (n c) -> p n c", n=SUB),
                                            W[:, v % 2, W_DNB:W_DNB + H].unsqueeze(1).broadcast_to([P, SUB, H]),
                                            ALU.add).then_inc(s["y"], 1)
            staggered(dve, step, BLOCKS, 2 * RING, RING)


def slot_wait(t, u, each):
    return each * (t // RING + 1) if isinstance(t, int) else (t - u) * (each // RING) + each


def gather_rows(nc, pool, keep, t, u, index, copied, got, Y, src, most, met):
    for n in range(2):
        nc.gpsimd.tensor_copy(index[:, n, u:u + 1], keep["SLOT"][:, bass.ds(t, 1), n]).then_inc(copied, 1)
    wait_alone(pool, copied, 2 * t + 2, *met)
    for n in range(2):
        nc.gpsimd.indirect_dma_start(Y[:, u, n, :], None, src,
                                     bass.IndirectOffsetOnAxis(ap=index[:, n, u:u + 1], axis=0),
                                     bounds_check=most - 1, oob_is_err=False).then_inc(got[u], 16)


def depool_phase(nc, io, keep):
    X, XN, LOG, C = keep["X"], keep["XN"], keep["LOG"], keep["C"]
    with ExitStack() as ctx:
        m = Mem(nc, ctx)
        sb, ps, sem = m.sb, m.ps, m.sem
        cr = sb("d_ctx", [P, RING, CTX])
        plug = sb("d_plug", [P, RING, P])
        index, Y = sb("d_index", [P, 2, RING], U32), sb("d_Y", [P, RING, 2, P])
        win, g_res = sb("d_win", [P, P]), sb("d_g_res", [P, 1])
        winG = sb("d_winG", [P, P])
        g_init, b_in = sb("d_g_init", [P, P]), sb("d_b_in", [P, P])
        rw = sb("d_rw", [P, E1])
        power_of = sb("d_power_of", [P, 1])
        square = sb("d_square", [P, CTX])
        ss, ms, rc = (sb("d_" + n, [P, RING, 1]) for n in ("ss", "ms", "rc"))
        hot, cg, GT = (sb("d_" + n, [P, RING, P]) for n in ("hot", "cg", "GT"))
        stat, mv, ve, R3 = sb("d_stat", [P, RING, 6]), sb("d_mv", [P, RING, 2]), sb("d_ve", [P, RING, 1]), sb(
            "d_R3", [P, RING, 1])
        stat2, mv2, ve2, rstd2 = sb("d_stat2", [P, RING, 6]), sb("d_mv2", [P, RING, 2]), sb(
            "d_ve2", [P, RING, 1]), sb("d_rstd2", [P, RING, 1])
        z, xn = sb("d_z", [P, RING, P]), sb("d_xn", [P, RING, P])
        xT = sb("d_xT", [P, RING, 2, P])
        turned, Gp, Hp, lgp = (ps("d_" + n, [P, 512]) for n in ("turned", "Gp", "Hp", "lgp"))
        s = {n: sem("d_" + n) for n in (
            "weights setup copied ss ms rc hot cg y1 x2 stat mv ve R3 z xTp xT Gp GT H h x3 stat2 mv2 ve2 rstd2 xn "
            "kept lgp lg").split()}
        got = [sem(f"d_got{u}") for u in range(RING)]
        c_landed = [sem(f"d_c_landed{u}") for u in range(RING)]
        n_w = 16 * 5
        met = (s["setup"], 2)
        block = ctx.enter_context(nc.Block())

        @block.sync
        def _(sp):
            sp.dma_start(win[:], io["winT"]).then_inc(s["weights"], 16)
            sp.dma_start(rw[:], io["embT"]).then_inc(s["weights"], 16)
            sp.dma_start(g_res[:], io["L1_xattn_g_res"].rearrange("(p o) -> p o", o=1)).then_inc(s["weights"], 16)
            sp.dma_start(g_init[:], io["g_init"].partition_broadcast(P)).then_inc(s["weights"], 16)
            sp.dma_start(b_in[:], io["L1_xattn_b_in"].partition_broadcast(P)).then_inc(s["weights"], 16)

            def step(t, u):
                if not exists(t):
                    return
                at_least(sp, s["ss"], t - RING + 1)
                at_least(sp, s["cg"], t - RING + 1)
                at_least(sp, s["hot"], t - RING + 1)
                sp.dma_start(cr[:, u, :], row_of(io["ctx_tiles"], t)).then_inc(c_landed[u], 16)
                sp.dma_start(plug[:, u, :], io["plug_rows"][bass.ds(t, 1)].rearrange("a c -> (a c)")
                             .partition_broadcast(P)).then_inc(c_landed[u], 16)
            staggered(sp, step, TILES, RING, RING)

        @block.gpsimd
        def _(pool):
            nc.gpsimd.memset(power_of[:], -0.5).then_inc(s["setup"], 1)
            pool.wait_ge(s["weights"], n_w)
            nc.gpsimd.tensor_scalar(winG[:], win[:], g_res[:], None, ALU.mult).then_inc(s["setup"], 1)
            pool.wait_ge(*met)

            def power(t, u, needs, between, done, src, mid, out, scale, shift):
                wait_alone(pool, s[needs], t + 1, *met)
                nc.gpsimd.tensor_scalar(mid[:, u, :], src, scale, shift, ALU.mult, ALU.add).then_inc(s[between], 1)
                wait_alone(pool, s[between], t + 1, *met)
                nc.gpsimd.tensor_tensor(out[:, u, :], mid[:, u, :], power_of[:], ALU.pow).then_inc(s[done], 1)

            def step(k, v):
                t, u = k, v
                if exists(t):
                    wait_alone(pool, s["x2"], t - RING + 1, *met)
                    gather_rows(nc, pool, keep, t, u, index, s["copied"], got, Y, io["yg0"], SLOTS, met)
                    power(t, u, "ss", "ms", "rc", ss[:, u, :], ms, rc, 1.0 / CTX, LN_EPS)
                t, u = k - 3, (v - 3) % RING
                if exists(t):
                    power(t, u, "mv2", "ve2", "rstd2", mv2[:, u, 1:2], ve2, rstd2, 1.0, LN_EPS)
                t, u = k - 1, (v - 1) % RING
                if exists(t):
                    power(t, u, "mv", "ve", "R3", mv[:, u, 1:2], ve, R3, 1.0 + LN_EPS, LN_EPS * LN_EPS)
                t, u = k - 3, (v - 3) % RING
                if exists(t):
                    wait_alone(pool, s["xn"], t + 1, *met)
                    nc.gpsimd.tensor_copy(tile_of(XN, t), xn[:, u, :]).then_inc(s["kept"], 1)
            staggered(pool, step, TILES, RING, RING)

        @block.vector
        def _(dve):
            dve.wait_ge(s["weights"], n_w)
            dve.wait_ge(*met)
            W = keep["W"]

            def stats(t, u, st, mv_, name, after):
                nc.vector.bn_stats(st[:, u, :], tile_of(X, t)).then_inc(s[name], 1)
                wait_alone(dve, s[name], t + 1, *met)
                nc.vector.bn_aggr(mv_[:, u, :], st[:, u, :]).then_inc(s[after], 1)

            def step(k, v):
                t, u = k - 3, (v - 3) % RING
                if exists(t):
                    dve.wait_ge(s["H"], t + 1)
                    nc.vector.tensor_tensor(tile_of(X, t), tile_of(X, t), Hp[:, 0:P], ALU.add).then_inc(s["h"], 1)
                    dve.wait_ge(s["h"], t + 1)
                    nc.vector.tensor_tensor(tile_of(X, t), tile_of(X, t), b_in[:], ALU.add).then_inc(s["x3"], 1)
                    wait_alone(dve, s["x3"], t + 1, *met)
                    stats(t, u, stat2, mv2, "stat2", "mv2")
                t, u = k - 1, (v - 1) % RING
                if exists(t):
                    dve.wait_ge(got[u], slot_wait(t, u, 32))
                    for n, name in ((0, "y1"), (1, "x2")):
                        nc.vector.scalar_tensor_tensor(tile_of(X, t), Y[:, u, n, :], W[:, n, bass.ds(t, 1)],
                                                       tile_of(X, t), ALU.mult, ALU.add).then_inc(s[name], 1)
                        wait_alone(dve, s[name], t + 1, *met)
                    stats(t, u, stat, mv, "stat", "mv")
                t, u = k, v
                if exists(t):
                    dve.wait_ge(c_landed[u], slot_wait(t, u, 32))
                    at_least(dve, s["Gp"], t - RING + 1)
                    nc.vector.tensor_scalar(hot[:, u, :], plug[:, u, :], C[:, C_PART:C_PART + 1], None,
                                            ALU.is_equal).then_inc(s["hot"], 1)
                    at_least(dve, s["H"], t - RING + 1)
                    nc.vector.tensor_tensor(cg[:, u, :], cr[:, u, 0:H], g_init[:], ALU.mult).then_inc(s["cg"], 1)
                t, u = k - 1, (v - 1) % RING
                if exists(t):
                    dve.wait_ge(s["R3"], t + 1)
                    nc.vector.tensor_scalar(z[:, u, :], tile_of(X, t), mv[:, u, 0:1], R3[:, u, :],
                                            ALU.subtract, ALU.mult).then_inc(s["z"], 1)
                t, u = k - 3, (v - 3) % RING
                if exists(t):
                    dve.wait_ge(s["rstd2"], t + 1)
                    at_least(dve, s["kept"], t - RING + 1)
                    nc.vector.tensor_scalar(xn[:, u, :], tile_of(X, t), mv2[:, u, 0:1], rstd2[:, u, :],
                                            ALU.subtract, ALU.mult).then_inc(s["xn"], 1)
                t = k - 5
                if exists(t):
                    dve.wait_ge(s["lgp"], t + 1)
                    nc.vector.tensor_copy(tile_of(LOG, t), lgp[:, 0:E1]).then_inc(s["lg"], 1)
            staggered(dve, step, TILES, 2 * RING, RING)

        @block.tensor
        def _(pe):
            ident, decay = C[:, C_ID:C_ID + P], C[:, C_DECAY:C_DECAY + P]
            pe.wait_ge(s["weights"], n_w)
            pe.wait_ge(*met)

            def step(k, v):
                t = k - 2
                mm = None
                at_least(pe, s["xT"], min(k - 2, TILES + 2) if isinstance(k, int) else k - 2)
                if exists(k - 4):
                    pe.wait_ge(s["xn"], k - 3)
                    mm = nc.tensor.transpose(turned[:, P:2 * P], xn[:, v, :], ident)
                if exists(t):
                    pe.wait_ge(s["z"], t + 1)
                    mm = nc.tensor.transpose(turned[:, 0:P], z[:, (v - 2) % RING, :], ident)
                if mm is not None:
                    mm.then_inc(s["xTp"], 1)
                u = (v - 2) % RING
                if exists(t):
                    pe.wait_ge(s["hot"], t + 1)
                    at_least(pe, s["GT"], t)
                    nc.tensor.matmul(Gp[:, 0:P], decay, hot[:, u, :], start=True, stop=True).then_inc(s["Gp"], 1)
                    pe.wait_ge(s["xT"], k - 1)
                    at_least(pe, s["h"], t)
                    nc.tensor.matmul(Hp[:, 0:P], xT[:, v, 0, :], winG[:], start=True, stop=False)
                    pe.wait_ge(s["cg"], t + 1)
                    pe.wait_ge(s["GT"], t + 1)
                    nc.tensor.matmul(Hp[:, 0:P], GT[:, u, :], cg[:, u, :], start=False, stop=True).then_inc(s["H"], 1)
                t = k - 4
                if exists(t):
                    pe.wait_ge(s["xT"], k - 1)
                    at_least(pe, s["lg"], t)
                    nc.tensor.matmul(lgp[:, 0:E1], xT[:, v, 1, :], rw[:], start=True, stop=True).then_inc(s["lgp"], 1)
            staggered(pe, step, TILES, 2 * RING, RING)

        @block.scalar
        def _(act):
            def step(k, v):
                t, u = k, v
                if exists(t):
                    act.wait_ge(c_landed[u], slot_wait(t, u, 32))
                    at_least(act, s["ss"], t)
                    at_least(act, s["ms"], t - RING + 1)
                    nc.scalar.activation(square[:], cr[:, u, :], ACT.Square, accum_out=ss[:, u, :]).then_inc(s["ss"], 1)
                lo, hi = 0 if exists(k - 2) else 1, 2 if exists(k - 4) else 1
                if lo < hi:
                    act.wait_ge(s["xTp"], k - 1)
                    at_least(act, s["H"], least(k - 5, TILES))
                    at_least(act, s["lgp"], least(k - 7, TILES))
                    nc.scalar.copy(xT[:, v, lo:hi, :].rearrange("p a c -> p (a c)"),
                                   turned[:, lo * P:hi * P]).then_inc(s["xT"], 1)
                t, u = k - 2, (v - 2) % RING
                if exists(t):
                    act.wait_ge(s["Gp"], t + 1)
                    act.wait_ge(s["rc"], t + 1)
                    at_least(act, s["H"], t - RING + 1)
                    nc.scalar.activation(GT[:, u, :], Gp[:, 0:P], ACT.Copy, scale=rc[:, u, :]).then_inc(s["GT"], 1)
            staggered(act, step, TILES, 2 * RING, RING)


def second_route_phase(nc, io, keep):
    C = keep["C"]
    with ExitStack() as ctx:
        m = Mem(nc, ctx)
        w = route_buffers(m, keep, "r_")
        rows, index = m.sb("r_rows", [P, RING, P]), m.sb("r_index", [P, 2, RING], U32)
        rank_ps, total_ps = m.ps("r_rank_ps", [P, WIDE]), m.ps("r_total_ps", [P, WIDE])
        s = {n: m.sem("r_" + n) for n in "chain exps_wanted exps counts_wanted counts tables slots copied".split()}
        sent = [m.sem(f"r_sent{u}") for u in range(RING)]
        block = ctx.enter_context(nc.Block())

        @block.gpsimd
        def _(pool):
            nc.gpsimd.tensor_copy(w["before"][:], C[:, C_BEFORE:C_BEFORE + P]).then_inc(s["tables"], 1)
            nc.gpsimd.tensor_copy(w["ones"][:], C[:, C_ONES:C_ONES + P]).then_inc(s["tables"], 1)
            scatter_rows(nc, pool, keep, rows, index, s["slots"], {"copied": s["copied"], "sent": sent},
                         io["xg1"], TOKENS)

        @block.scalar
        def _(act):
            route_exps(nc, act, w, s["exps_wanted"], s["exps"], second=True)

        @block.tensor
        def _(pe):
            route_counts(nc, pe, w, rank_ps, total_ps, s["tables"], s["counts_wanted"], s["counts"])

        @block.vector
        def _(dve):
            count = [0]

            def link(ins, also=None):
                count[0] += 1
                ins.then_inc(s["chain"], 1)
                dve.wait_ge(s["chain"], count[0])
                if also is not None:
                    dve.sem_inc(also, 1)
            route(nc, dve, link, keep["LOG"], C, w, rank_ps, total_ps, s["counts_wanted"], s["counts"],
                  s["exps_wanted"], s["exps"], second=True).then_inc(s["slots"], 1)


def second_experts_phase(nc, io, keep):
    C = keep["C"]
    SUB, STEPS, PER = WIDE // P, TOKENS // WIDE, CAPACITY // WIDE
    with ExitStack() as ctx:
        m = Mem(nc, ctx)
        sb, ps, sem = m.sb, m.ps, m.sem
        WE = sb("f_W", [P, E1, 2 * F1])
        W = sb("f_w", [P, 2, 2 * F1])
        rows, Y = sb("f_rows", [P, RING, SUB, P]), sb("f_Y", [P, RING, SUB, P])
        xT, G = sb("f_xT", [P, 2, WIDE]), sb("f_G", [P, 2, CHUNKS1, WIDE])
        xTp, hid, yp = ps("f_xTp", [P, 2, WIDE]), ps("f_hid", [P, 2, CHUNKS1, WIDE]), ps("f_yp", [P, 2, WIDE])
        s = {n: sem("f_" + n) for n in "weights w xTp xT hid relu yp y".split()}
        landed = [sem(f"f_landed{u}") for u in range(RING)]
        stored = [sem(f"f_stored{u}") for u in range(RING)]
        src = io["xg1"].rearrange("(k n p) c -> k p n c", p=P, n=SUB)
        dst = io["yg1"].rearrange("(k n p) c -> k p n c", p=P, n=SUB)
        block = ctx.enter_context(nc.Block())

        def blk(a, k):
            return a[k] if isinstance(k, int) else a[bass.ds(k, 1)].rearrange("a p n c -> (a p) n c")

        def real(k):
            return not isinstance(k, int) or 0 <= k < STEPS

        @block.sync
        def _(sp):
            for e in range(E1):
                sp.dma_start(WE[:, e, :], io["expert1_w"][e]).then_inc(s["weights"], 16)

            def step(k, v):
                if real(k):
                    at_least(sp, s["xTp"], k - RING + 1)
                    sp.dma_start(rows[:, v], blk(src, k)).then_inc(landed[v], 16)
                k = k - 4
                if real(k):
                    sp.wait_ge(s["y"], k + 1)
                    sp.dma_start(blk(dst, k), Y[:, v]).then_inc(stored[v], 16)
            staggered(sp, step, STEPS, RING, RING)
            for u in range(RING):
                sp.wait_ge(stored[u], 16 * (STEPS // RING))

        @block.gpsimd
        def _(pool):
            pool.wait_ge(s["weights"], 16 * E1)

            def step(e, v):
                wait_alone(pool, s["yp"], PER * (e - 1), s["weights"], 16 * E1)
                nc.gpsimd.tensor_copy(W[:, v, :], tile_of(WE, e)).then_inc(s["w"], 1)
            step(0, 0)
            step(1, 1)
            with pool.Fori(1, E1 // 2) as i:
                step(2 * i, 0)
                step(2 * i + 1, 1)

        @block.tensor
        def _(pe):
            ident = C[:, C_ID:C_ID + P]

            def step(k, v):
                if real(k):
                    pe.wait_ge(landed[v], slot_wait(k, v, 16))
                    at_least(pe, s["xT"], k - 1)
                    for n in range(SUB):
                        mm = nc.tensor.transpose(xTp[:, v % 2, n * P:(n + 1) * P], rows[:, v, n, :], ident)
                    mm.then_inc(s["xTp"], 1)
                k, v = k - 1, (v - 1) % RING
                if real(k):
                    pe.wait_ge(s["w"], k // PER + 1)
                    pe.wait_ge(s["xT"], k + 1)
                    at_least(pe, s["relu"], k - 1)
                    for c in range(CHUNKS1):
                        mm = nc.tensor.matmul(hid[:, v % 2, c, :], W[:, v // PER, c * P:(c + 1) * P], xT[:, v % 2, :],
                                              start=True, stop=True)
                    mm.then_inc(s["hid"], 1)
                k, v = k - 1, (v - 1) % RING
                if real(k):
                    pe.wait_ge(s["relu"], k + 1)
                    at_least(pe, s["y"], k - 1)
                    for n in range(SUB):
                        for c in range(CHUNKS1):
                            mm = nc.tensor.matmul(yp[:, v % 2, n * P:(n + 1) * P], G[:, v % 2, c, n * P:(n + 1) * P],
                                                  W[:, v // PER, F1 + c * P:F1 + (c + 1) * P], start=c == 0,
                                                  stop=c == CHUNKS1 - 1)
                    mm.then_inc(s["yp"], 1)
            for k in range(STEPS + 2):
                step(k, k % RING)

        @block.scalar
        def _(act):
            for k in range(STEPS):
                v = k % 2
                at_least(act, s["yp"], k - 1)
                act.wait_ge(s["hid"], k + 1)
                nc.scalar.activation(G[:, v], hid[:, v], ACT.Relu).then_inc(s["relu"], 1)

        @block.vector
        def _(dve):
            def step(k, v):
                if real(k):
                    dve.wait_ge(s["xTp"], k + 1)
                    at_least(dve, s["hid"], k - 1)
                    nc.vector.tensor_copy(xT[:, v % 2, :], xTp[:, v % 2, :]).then_inc(s["xT"], 1)
                k, v = k - 2, (v - 2) % RING
                if real(k):
                    dve.wait_ge(s["yp"], k + 1)
                    if k >= RING:
                        dve.wait_ge(stored[v], 16 * (k // RING))
                    nc.vector.tensor_copy(Y[:, v].rearrange("p n c -> p (n c)"), yp[:, v % 2, :]).then_inc(s["y"], 1)
            for k in range(STEPS + 2):
                step(k, k % RING)


def output_phase(nc, io, keep):
    X, W = keep["X"], keep["W"]
    with ExitStack() as ctx:
        m = Mem(nc, ctx)
        index, Y = m.sb("o_index", [P, 2, RING], U32), m.sb("o_Y", [P, RING, 2, P])
        copied, added, setup = m.sem("o_copied"), m.sem("o_added"), m.sem("o_setup")
        got = [m.sem(f"o_got{u}") for u in range(RING)]
        out_done = m.sem("o_out_done")
        block = ctx.enter_context(nc.Block())

        @block.gpsimd
        def _(pool):
            nc.gpsimd.memset(Y[:], 0.0).then_inc(setup, 1)
            pool.wait_ge(setup, 1)

            def step(t, u):
                wait_alone(pool, added, 2 * (t - RING + 1), setup, 1)
                gather_rows(nc, pool, keep, t, u, index, copied, got, Y, io["yg1"], TOKENS, (setup, 1))
            staggered(pool, lambda t, u: step(t, u) if exists(t) else None, TILES, RING, RING)

        @block.vector
        def _(dve):
            dve.wait_ge(setup, 1)

            def step(t, u):
                dve.wait_ge(got[u], slot_wait(t, u, 32))
                for n in range(2):
                    nc.vector.scalar_tensor_tensor(tile_of(X, t), Y[:, u, n, :], W[:, n, bass.ds(t, 1)],
                                                   tile_of(X, t), ALU.mult, ALU.add).then_inc(added, 1)
                    if n == 0:
                        wait_alone(dve, added, 2 * t + 1, setup, 1)
            staggered(dve, lambda t, u: step(t, u) if exists(t) else None, TILES, RING, RING)

        @block.sync
        def _(sp):
            def step(t, u):
                sp.wait_ge(added, 2 * t + 2)
                sp.dma_start(row_of(io["out_tiles"], t), tile_of(X, t)).then_inc(out_done, 16)
            staggered(sp, lambda t, u: step(t, u) if exists(t) else None, TILES, RING, RING)
            sp.wait_ge(out_done, 16 * TILES)


def build(nc, io, out):
    zeroed = []
    io = dict(io)
    xg0 = nc.dram_tensor("xg0", [SLOTS, H], F32).ap()
    xg1 = nc.dram_tensor("xg1", [TOKENS, H], F32).ap()
    io["yg0"] = nc.dram_tensor("yg0", [SLOTS, H], F32).ap()
    io["yg1"] = nc.dram_tensor("yg1", [TOKENS, H], F32).ap()
    io["plug"] = nc.dram_tensor("plug", [BATCH, SEQ], F32).ap()
    io["xg0"], io["xg1"] = xg0, xg1
    for a, n in ((xg0, SLOTS), (xg1, TOKENS)):
        v = a.rearrange("(k p r) c -> k p (r c)", p=P, r=16)
        zeroed += [v[i] for i in range(n * H // (P * 2048))]
    io["zeroed"] = zeroed
    io["x_tiles"] = io["x"].rearrange("(t b) s d -> t (b s) d", b=2)
    io["out_tiles"] = out.rearrange("(t b) s d -> t (b s) d", b=2)
    io["plug_rows"] = io["plug"].rearrange("(t b) s -> t (b s)", b=2)
    io["ctx_tiles"] = io["ctx_2048"].rearrange("(t b) s d -> t (b s) d", b=2)
    io["mask_rows"] = io["mask_BxS2_fk1"].rearrange("(t b) s -> t (b s)", b=2)
    io["mask_pairs"] = io["mask_BxS2_fk1"].rearrange("(t b) s -> t b s", b=2)
    with ExitStack() as ctx:
        m = Mem(nc, ctx)
        keep = {
            "X": m.sb("X", [P, TILES, H]), "XN": m.sb("XN", [P, TILES, H]),
            "LOG": m.sb("LOG", [P, TILES, E0]), "C": m.sb("C", [P, C_COLS]),
            "W": m.sb("WEIGHT", [P, 2, TILES]), "SLOT": m.sb("SLOT", [P, TILES, 2], U32),
            "OWNER": m.sb("OWNER", [1, BLOCKS], I32),
        }
        with ExitStack() as inner:
            keep["XNT"] = Mem(nc, inner).sb("XNT", [P, TILES, P])
            attention_phase(nc, io, keep)
            shared_phase(nc, io, keep)
        experts_phase(nc, io, keep)
        depool_phase(nc, io, keep)
        second_route_phase(nc, io, keep)
        second_experts_phase(nc, io, keep)
        output_phase(nc, io, keep)


def kernel(**inputs):
    import numpy as _np
    import concourse.bacc as _bacc
    from concourse import mybir as _mybir
    from concourse.bass_utils import run_bass_kernel_spmd as _run

    a = {k: _np.asarray(v) for k, v in inputs.items()}
    T, ctx = _np.transpose, a["ctx_2048"].reshape(TILES, P, 2, P)
    a["consts"] = constants()
    ctx = T(ctx, (0, 3, 2, 1)).reshape(TILES, P, 2, 2, 1, SEQ)
    a["ctxT"] = _np.broadcast_to(ctx, (TILES, P, 2, 2, 2, SEQ)).reshape(TILES, P, 4 * P)
    a["maskT"] = a["mask_BxS2_fk1"].T
    wsrc = a["L0_xattn_W_src"].reshape(2, H, 2, P)
    a["wkT"] = T(wsrc[0], (2, 1, 0)).reshape(P, 2 * P)
    a["wvT"] = T(wsrc[1], (2, 1, 0)).reshape(P, 2 * P)
    a["b_k"], a["b_v"] = a["L0_xattn_b_src"][:H], a["L0_xattn_b_src"][H:]
    a["wqT"] = a["L0_xattn_W_tgt"].T
    a["woT"] = T(a["L0_xattn_W_out"].reshape(H, 2, P), (2, 1, 0)).reshape(P, 2 * P)

    def ffn(up, down, up_b, down_b):
        n = up.shape[0]
        return _np.concatenate([up, T(down.reshape(n, CHUNKS0, P, H), (0, 2, 1, 3)).reshape(n, P, F0),
                                T(up_b.reshape(n, CHUNKS0, P), (0, 2, 1)),
                                _np.broadcast_to(down_b[:, None, :], (n, P, H))], axis=2)
    a["expert_w"] = ffn(a["L0_ffn_up_w"], a["L0_ffn_down_w"], a["L0_ffn_up_b"], a["L0_ffn_down_b"])
    a["shared_w"] = ffn(a["L0_ffn_sh_up_w"][None], a["L0_ffn_sh_down_w"][None], a["L0_ffn_sh_up_b"][None],
                        a["L0_ffn_sh_down_b"][None])[0]
    a["winT"] = a["L1_xattn_W_in"].T
    a["embT"] = a["L1_ffn_expert_embeddings"].T
    a["g_init"] = a["L1_xattn_g_init"][:H]
    first, second = a["L1_ffn_first_linear"], a["L1_ffn_second_linear"]
    a["expert1_w"] = _np.concatenate([T(first, (0, 2, 1)),
                                      T(second.reshape(E1, H, CHUNKS1, P), (0, 3, 2, 1)).reshape(E1, P, F1)], axis=2)
    names = ["ctx_2048", "winT", "embT", "g_init", "L1_xattn_g_res", "L1_xattn_b_in", "expert1_w", "x", "mask_BxS2_fk1", "consts", "ctxT", "maskT", "wkT", "wvT", "b_k", "b_v", "wqT", "woT",
             "L0_xattn_b_tgt", "L0_xattn_b_out", "L0_ffn_sh_down_b", "L0_ffn_router_b", "L0_ffn_router_w",
             "mask_BxS2_if0", "expert_w", "shared_w"]
    nc = _bacc.Bacc("TRN2", target_bir_lowering=False, num_devices=1)
    arrays, io = {}, {}
    for name in names:
        v = _np.ascontiguousarray(a[name])
        arrays["in_" + name] = v
        io[name] = nc.dram_tensor("in_" + name, v.shape, _mybir.dt.from_np(v.dtype), kind="ExternalInput").ap()
    out = nc.dram_tensor("out_0", (BATCH, SEQ, H), _mybir.dt.float32, kind="ExternalOutput").ap()
    build(nc, io, out)
    r = _run(nc, [arrays], core_ids=[0])
    return r.results[0]["out_0"]
```

```python
from contextlib import ExitStack

import numpy as np
import concourse.bass as bass
from concourse import mybir

F32 = mybir.dt.float32
BF16 = mybir.dt.bfloat16
I32 = mybir.dt.int32
U32 = mybir.dt.uint32
ALU = mybir.AluOpType
ACT = mybir.ActivationFunctionType
AX = mybir.AxisListType

P = 128
BATCH, SEQ, H, CTX = 128, 64, 128, 256
TOKENS = BATCH * SEQ
TILES = TOKENS // P
HEADS, HEAD_DIM = 8, 16
PAIRS = HEADS // 2
E0, F0 = 8, 512
E1, F1 = 8, 256
CHUNKS0, CHUNKS1 = F0 // P, F1 // P
CAPACITY = TOKENS // E1
BLOCK = 256
BLOCKS = 2 * TOKENS // BLOCK + E0
SLOTS = BLOCKS * BLOCK
WIDE = 512
RING = 4
SCALE = HEAD_DIM ** -0.5
NEG = -1.0e30
LN_EPS = 1e-5
PATCHES = SEQ
EPSILON = 0.001
OUT_OF_RANGE = 4 * TOKENS

C_ID, C_DECAY, C_BEFORE, C_ONES, C_PART, C_ROW, C_HALF, C_IND, C_IOTA, C_KEEP = 0, 128, 256, 384, 512, 513, 514, 516, 644, 772
C_COLS = C_KEEP + TILES * E0

W_UP, W_DOWN, W_UPB, W_DNB = 0, F0, 2 * F0, 2 * F0 + CHUNKS0
W_COLS = W_DNB + H


def constants():
    c = np.zeros((P, C_COLS), np.float32)
    i = np.arange(P)
    c[:, C_ID:C_ID + P] = np.eye(P)
    dt = -np.log(-np.expm1(np.float64(-EPSILON)))
    lag = (i[:, None] - i[None, :]).astype(np.float64)
    same = (i[:, None] // SEQ == i[None, :] // SEQ) & (lag >= 0)
    c[:, C_DECAY:C_DECAY + P] = np.where(same, np.exp(-EPSILON) * np.exp(-dt * np.maximum(lag, 0)), 0.0)
    c[:, C_BEFORE:C_BEFORE + P] = i[:, None] < i[None, :]
    c[:, C_ONES:C_ONES + P] = 1.0
    c[:, C_PART] = i
    for j in range(2):
        c[:, C_HALF + j] = (i // HEAD_DIM) % 2 == j
        c[j, C_IND:C_IND + P] = i // SEQ == j
    c[:, C_ROW] = SEQ * (i % 2)
    c[:, C_IOTA:C_IOTA + P] = i
    c[:, C_KEEP:] = (np.arange(TILES * E0) % TILES != 0)
    return c


def at_least(eng, sem, n):
    if isinstance(n, int) and n <= 0:
        return
    eng.wait_ge(sem, n)


def wait_alone(eng, sem, n, met, at):
    if isinstance(n, int) and n <= 0:
        return
    if not isinstance(n, int):
        n = eng.to_reg(n)
    eng.wait_ge(met, at)
    eng.wait_ge(sem, n)


def slot_wait(t, u, each):
    return each * (t // RING + 1) if isinstance(t, int) else (t - u) * (each // RING) + each


def tile_of(a, t):
    if isinstance(t, int):
        return a[:, t, :]
    return a[:, bass.ds(t, 1), :].rearrange("p a c -> p (a c)")


def row_of(a, t):
    if isinstance(t, int):
        return a[t]
    return a[bass.ds(t, 1)].rearrange("a p c -> (a p) c")


def staggered(eng, step, steps, lag, unroll, peel=0):
    for k in range(lag):
        step(k, k % unroll)
    with eng.Fori(lag // unroll, (steps - peel) // unroll) as i:
        for v in range(unroll):
            step(i * unroll + v, v)
    for k in range(steps - peel, steps + lag):
        step(k, k % unroll)


def least(n, most):
    return min(n, most) if isinstance(n, int) else n


def exists(t):
    return not isinstance(t, int) or 0 <= t < TILES


class Mem:

    def __init__(self, nc, ctx):
        self.nc, self.ctx = nc, ctx

    def sb(self, name, shape, dt=F32):
        return self.ctx.enter_context(self.nc.sbuf_tensor(name, shape, dt))

    def ps(self, name, shape, dt=F32):
        return self.ctx.enter_context(self.nc.psum_tensor(name, shape, dt))

    def sem(self, name):
        return self.ctx.enter_context(self.nc.semaphore(name))


def attention_phase(nc, io, keep):
    X, XN, XNT, LOG, C = keep["X"], keep["XN"], keep["XNT"], keep["LOG"], keep["C"]
    with ExitStack() as ctx:
        m = Mem(nc, ctx)
        sb, ps, sem = m.sb, m.ps, m.sem
        ctxT = sb("a_ctxT", [P, RING, 2, 2, 2 * SEQ])
        mrow = sb("a_mrow", [P, RING, P])
        mpair = sb("a_mpair", [2, RING, SEQ])
        mneg = sb("a_mneg", [2, RING, SEQ], BF16)
        mhalf = sb("a_mhalf", [P, RING, 2 * P])
        maskT = sb("a_maskT", [P, BATCH])
        mvj = sb("a_mvj", [P, BATCH, 2])
        half = sb("a_half", [P, 2])
        wq = sb("a_wq", [P, P])
        wk = sb("a_wk", [P, 2 * P])
        wv = sb("a_wv", [P, 2 * P])
        wo = sb("a_wo", [P, 2 * P])
        rw = sb("a_rw", [P, E0])
        cols = sb("a_cols", [P, 3])
        rows = sb("a_rows", [P, P + E0])
        ind = sb("a_ind", [2, P], BF16)
        eps = sb("a_eps", [P, 2])
        stat = sb("a_stat", [P, RING, 6])
        stat2 = sb("a_stat2", [P, RING, 6])
        mv = sb("a_mv", [P, RING, 2, 2])
        ve = sb("a_ve", [P, RING, 2])
        rstd = sb("a_rstd", [P, RING, 2])
        xn = sb("a_xn", [P, RING, P])
        xn2 = sb("a_xn2", [P, RING, P])
        xT = sb("a_xT", [P, RING, 2, P])
        qT = sb("a_qT", [P, 2, P])
        kT = sb("a_kT", [P, 2, 2 * P])
        V = sb("a_V", [P, 2, 2, PAIRS, 2, HEAD_DIM + 1])
        top = sb("a_top", [P, 2, HEADS])
        D = sb("a_D", [P, 2, PAIRS, 2, SEQ])
        PR = sb("a_P", [P, 2, PAIRS, 2 * SEQ])
        PT = sb("a_PT", [P, 2, PAIRS, P])
        rin = sb("a_rin", [P, 2, HEADS])
        upd = sb("a_upd", [P, 2, P])
        updT = sb("a_updT", [P, 2, P])
        zero = sb("a_zero", [P, 2048])

        turned = ps("a_turned", [P, 4, P])
        qkv = ps("a_qkv", [P, 4, P])
        S = ps("a_S", [P, PAIRS, 512])
        PTp = ps("a_PTp", [P, PAIRS, P])
        O = ps("a_O", [P, 512])
        U = O[:, 0:HEADS * (HEAD_DIM + 1)].rearrange("p (h c) -> p h c", h=HEADS)
        proj = O[:, 256:256 + P]
        lgp = O[:, 400:400 + E0]

        consts_landed = sem("a_consts_landed")
        zeros_out = sem("a_zeros_out")
        setup = sem("a_setup")
        x_landed = [sem(f"a_x_landed{u}") for u in range(RING)]
        c_landed = [sem(f"a_c_landed{u}") for u in range(RING)]
        names = ("stat mv ve rstd xn xTp xT qkv masks halves q k v scores top shifted probs PTp PT pv rin upd updTp "
                 "updT proj xb x1 stat2 mv2 xn2 x2 lgp lg kept keptT").split()
        s = {n: sem("a_" + n) for n in names}
        n_consts = 12
        block = ctx.enter_context(nc.Block())

        @block.sync
        def _(sp):
            for dst, src in ((C, io["consts"]), (wq, io["wqT"]), (wk, io["wkT"]), (wv, io["wvT"]), (wo, io["woT"]),
                             (rw, io["L0_ffn_router_w"])):
                sp.dma_start(dst[:], src).then_inc(consts_landed, 16)
            for j, name in enumerate(("L0_xattn_b_tgt", "b_k", "b_v")):
                sp.dma_start(cols[:, j:j + 1], io[name].rearrange("(p o) -> p o", o=1)).then_inc(consts_landed, 16)
            off = 0
            for name in ("L0_xattn_b_out", "L0_ffn_router_b"):
                n = io[name].shape[0]
                sp.dma_start(rows[:, off:off + n], io[name].partition_broadcast(P)).then_inc(consts_landed, 16)
                off += n
            sp.dma_start(maskT[0:SEQ, :], io["maskT"]).then_inc(consts_landed, 16)
            sp.dma_start(maskT[SEQ:P, :], io["maskT"]).then_inc(consts_landed, 16)

            def step(t, u):
                if not exists(t):
                    return
                at_least(sp, s["stat"], t - RING + 1)
                at_least(sp, s["qkv"], t - RING + 1)
                at_least(sp, s["masks"], t - RING + 1)
                at_least(sp, s["halves"], t - RING + 1)
                at_least(sp, s["q"], t - RING + 1)
                sp.dma_start(tile_of(X, t), row_of(io["x_tiles"], t)).then_inc(x_landed[u], 16)
                sp.dma_start(ctxT[:, u].rearrange("p c b s -> p (c b s)"), row_of(io["ctxT"], t)).then_inc(c_landed[u], 16)
                sp.dma_start(mrow[:, u, :], io["mask_rows"][bass.ds(t, 1)].rearrange("a c -> (a c)")
                             .partition_broadcast(P)).then_inc(c_landed[u], 16)
                sp.dma_start(mpair[:, u, :], row_of(io["mask_pairs"], t)).then_inc(c_landed[u], 16)
            staggered(sp, step, TILES, RING, RING)

        @block.gpsimd
        def _(pool):
            nc.gpsimd.memset(zero[:], 0.0).then_inc(zeros_out, 16)
            nc.gpsimd.memset(V[:], 0.0).then_inc(setup, 1)
            nc.gpsimd.memset(eps[:], -0.5).then_inc(setup, 1)
            nc.gpsimd.memset(half[:], 0.0).then_inc(setup, 1)
            pool.wait_ge(setup, 3)
            for b in range(2):
                for ring in range(2):
                    for j in range(2):
                        nc.gpsimd.memset(V[j * SEQ:(j + 1) * SEQ, ring, b, :, j, HEAD_DIM], 1.0).then_inc(setup, 1)
            for j in range(2):
                nc.gpsimd.memset(half[j * SEQ:(j + 1) * SEQ, j:j + 1], 1.0).then_inc(setup, 1)
            pool.wait_ge(consts_landed, 16 * (n_consts + 1))
            nc.gpsimd.tensor_copy(ind[:], C[0:2, C_IND:C_IND + P]).then_inc(setup, 1)
            pool.wait_ge(setup, 13)
            for j in range(2):
                nc.gpsimd.tensor_scalar(mvj[:, :, j], maskT[:], half[:, j:j + 1], None, ALU.mult).then_inc(setup, 1)
            pool.wait_ge(setup, 15)

            def hold(name, n):
                wait_alone(pool, s[name], n, setup, 15)

            def step(k, v):
                t, u = k, v
                if exists(t):
                    wait_alone(pool, c_landed[u], slot_wait(t, u, 48), setup, 15)
                    hold("scores", t - RING + 1)
                    nc.gpsimd.tensor_scalar(mneg[:, u, :], mpair[:, u, :], 0.0, NEG, ALU.is_equal,
                                            ALU.mult).then_inc(s["masks"], 1)
                    hold("xn", t + 1)
                    nc.gpsimd.tensor_tensor(tile_of(X, t), tile_of(X, t), rows[:, 0:P], ALU.add).then_inc(s["xb"], 1)
                t, u = k - 5, (v - 5) % RING
                if exists(t):
                    hold("xn2", t + 1)
                    nc.gpsimd.tensor_tensor(tile_of(X, t), tile_of(X, t), xn2[:, u, :], ALU.add).then_inc(s["x2"], 1)
                    nc.gpsimd.tensor_copy(tile_of(XN, t), xn2[:, u, :]).then_inc(s["kept"], 1)
                    hold("xT", k)
                    nc.gpsimd.tensor_copy(tile_of(XNT, t), xT[:, u, 1, :]).then_inc(s["keptT"], 1)
                lo, hi = 0 if exists(k + 1) else 1, 2 if exists(k - 3) else 1
                if lo < hi:
                    hold("mv", least(k + 2, TILES))
                    hold("mv2", least(k - 2, TILES))
                    nc.gpsimd.tensor_scalar(ve[:, v, lo:hi], mv[:, v, lo:hi, 1], LN_EPS, None,
                                            ALU.add).then_inc(s["ve"], 1)
                    hold("ve", k + 2)
                    nc.gpsimd.tensor_tensor(rstd[:, v, lo:hi], ve[:, v, lo:hi], eps[:, lo:hi],
                                            ALU.pow).then_inc(s["rstd"], 1)
            hold("mv", 1)
            nc.gpsimd.tensor_scalar(ve[:, RING - 1, 0:1], mv[:, RING - 1, 0, 1:2], LN_EPS, None,
                                    ALU.add).then_inc(s["ve"], 1)
            hold("ve", 1)
            nc.gpsimd.tensor_tensor(rstd[:, RING - 1, 0:1], ve[:, RING - 1, 0:1], eps[:, 0:1],
                                    ALU.pow).then_inc(s["rstd"], 1)
            staggered(pool, step, TILES, 2 * RING, RING, peel=RING)

        @block.vector
        def _(dve):
            def gather_stats(t, u, st, name):
                nc.vector.bn_stats(st[:, u, :], tile_of(X, t)).then_inc(s[name], 1)

            def mean_and_variance(t, u, which, at, st, name, after):
                wait_alone(dve, s[name], t + 1, setup, 15)
                nc.vector.bn_aggr(mv[:, at, which, :], st[:, u, :]).then_inc(s[after], 1)

            def first_stats(t, u):
                if exists(t):
                    wait_alone(dve, x_landed[u], slot_wait(t, u, 16), setup, 15)
                    gather_stats(t, u, stat, "stat")

            def first_mean(t, u):
                if exists(t):
                    mean_and_variance(t, u, 0, (u - 1) % RING, stat, "stat", "mv")

            dve.wait_ge(setup, 15)
            dve.wait_ge(consts_landed, 16 * (n_consts + 1))
            first_stats(0, 0)
            first_mean(0, 0)

            def step(k, v):
                w = (v - 1) % RING
                if exists(k) or exists(k - 4):
                    dve.wait_ge(s["rstd"], k + 1)
                    at_least(dve, s["xTp"], k - RING + 1)
                if exists(k):
                    nc.vector.tensor_scalar(xn[:, v, :], tile_of(X, k), mv[:, w, 0, 0:1], rstd[:, w, 0:1],
                                            ALU.subtract, ALU.mult).then_inc(s["xn"], 1)
                t, u = k - 4, v
                if exists(t):
                    at_least(dve, s["kept"], t - RING + 1)
                    at_least(dve, s["x2"], t - RING + 1)
                    nc.vector.tensor_scalar(xn2[:, u, :], tile_of(X, t), mv[:, w, 1, 0:1], rstd[:, w, 1:2],
                                            ALU.subtract, ALU.mult).then_inc(s["xn2"], 1)
                t, w = k - 1, (v - 1) % 2
                Sv = S[:, :, 0:2 * SEQ].rearrange("p g (j s) -> p g j s", j=2)
                tops = top[:, w, :].rearrange("p (g j) -> p g j", j=2)
                if exists(t):
                    dve.wait_ge(s["scores"], t + 1)
                    nc.vector.tensor_reduce(tops, Sv, AX.X, ALU.max).then_inc(s["top"], 1)
                if exists(k - 2):
                    dve.wait_ge(s["pv"], k - 1)
                    nc.vector.reciprocal(rin[:, v % 2, :], U[:, :, HEAD_DIM]).then_inc(s["rin"], 1)
                if exists(t):
                    dve.wait_ge(s["top"], t + 1)
                    at_least(dve, s["probs"], t - 1)
                    nc.vector.tensor_tensor(D[:, w], Sv, tops.unsqueeze(3).broadcast_to([P, PAIRS, 2, SEQ]),
                                            ALU.subtract).then_inc(s["shifted"], 1)
                t, u = k - 3, (v - 3) % RING
                if exists(t):
                    dve.wait_ge(s["xb"], t + 1)
                    dve.wait_ge(s["proj"], t + 1)
                    nc.vector.tensor_tensor(tile_of(X, t), tile_of(X, t), proj, ALU.add).then_inc(s["x1"], 1)
                t, w = k - 2, v % 2
                if exists(t):
                    dve.wait_ge(s["rin"], t + 1)
                    at_least(dve, s["updTp"], t - 1)
                    nc.vector.tensor_tensor(upd[:, w, :].rearrange("p (h d) -> p h d", h=HEADS), U[:, :, 0:HEAD_DIM],
                                            rin[:, w, :].unsqueeze(2).broadcast_to([P, HEADS, HEAD_DIM]),
                                            ALU.mult).then_inc(s["upd"], 1)
                first_stats(k + 1, (v + 1) % RING)
                t, u = k - 3, (v - 3) % RING
                if exists(t):
                    wait_alone(dve, s["x1"], t + 1, setup, 15)
                    gather_stats(t, u, stat2, "stat2")
                first_mean(k + 1, (v + 1) % RING)
                if exists(k - 5):
                    dve.wait_ge(s["lgp"], k - 4)
                    nc.vector.tensor_tensor(tile_of(LOG, k - 5), lgp, rows[:, P:P + E0],
                                            ALU.add).then_inc(s["lg"], 1)
                if exists(t):
                    mean_and_variance(t, u, 1, v, stat2, "stat2", "mv2")
                t, u, w = k, v, v % 2
                if exists(t):
                    dve.wait_ge(s["qkv"], t + 1)
                    dve.wait_ge(s["halves"], t + 1)
                    nc.vector.scalar_tensor_tensor(qT[:, w, :], qkv[:, 0, :], cols[:, 0:1], mrow[:, u, :],
                                                   ALU.add, ALU.mult).then_inc(s["q"], 1)
                    nc.vector.scalar_tensor_tensor(kT[:, w, :].rearrange("p (j c) -> p j c", j=2),
                                                   qkv[:, 1, :].unsqueeze(1).broadcast_to([P, 2, P]),
                                                   cols[:, 1:2], mhalf[:, u, :].rearrange("p (j c) -> p j c", j=2),
                                                   ALU.add, ALU.mult).then_inc(s["k"], 1)
                    at_least(dve, s["pv"], t - 1)
                    for b in range(2):
                        nc.vector.tensor_tensor(
                            V[:, w, b, :, :, 0:HEAD_DIM],
                            qkv[:, 2 + b, :].rearrange("p (g j d) -> p g j d", g=PAIRS, j=2),
                            mvj[:, bass.ds(2 * t + b, 1), :].unsqueeze(3).broadcast_to([P, 1, 2, HEAD_DIM])
                            .broadcast_to([P, PAIRS, 2, HEAD_DIM]),
                            ALU.mult).then_inc(s["v"], 1)
            staggered(dve, step, TILES, 2 * RING, RING, peel=RING)

        @block.tensor
        def _(pe):
            ident = C[:, C_ID:C_ID + P]
            pe.wait_ge(consts_landed, 16 * (n_consts + 1))
            pe.wait_ge(setup, 15)

            def step(k, v):
                t, u = k, v
                if exists(t):
                    pe.wait_ge(s["xn"], t + 1)
                at_least(pe, s["updT"], least(k - 2, TILES))
                if exists(k - 4):
                    pe.wait_ge(s["xn2"], k - 3)
                    mm = nc.tensor.transpose(turned[:, 1, :], xn2[:, u, :], ident)
                if exists(t):
                    mm = nc.tensor.transpose(turned[:, 0, :], xn[:, u, :], ident)
                if exists(k - 4) or exists(t):
                    mm.then_inc(s["xTp"], 1)
                if exists(t):
                    pe.wait_ge(c_landed[u], 48 * (t // RING + 1) if isinstance(t, int) else (t - u) * 12 + 48)
                    at_least(pe, s["q"], t)
                    at_least(pe, s["k"], t)
                    at_least(pe, s["v"], 2 * t)
                    for c in range(2):
                        nc.tensor.matmul(qkv[:, 1, :], wk[:, c * P:(c + 1) * P], ctxT[:, u, c, :, 0:SEQ],
                                         start=c == 0, stop=c == 1)
                    for b in range(2):
                        for c in range(2):
                            nc.tensor.matmul(qkv[:, 2 + b, :], ctxT[:, u, c, b, :], wv[:, c * P:(c + 1) * P], start=c == 0, stop=c == 1)
                    pe.wait_ge(s["xT"], t + 1)
                    nc.tensor.matmul(qkv[:, 0, :], wq[:], xT[:, u, 0, :], start=True, stop=True).then_inc(s["qkv"], 1)
                t, w = k - 1, (v - 1) % 2
                if exists(t):
                    pe.wait_ge(s["probs"], t + 1)
                    at_least(pe, s["PT"], t)
                    for g in range(PAIRS):
                        mm = nc.tensor.transpose(PTp[:, g, :], PR[:, w, g, :], ident)
                    mm.then_inc(s["PTp"], 1)
                if exists(k) or exists(k - 4):
                    pe.wait_ge(s["xT"], k + 1)
                at_least(pe, s["upd"], least(k - 1, TILES))
                at_least(pe, s["x1"], least(k - 2, TILES))
                at_least(pe, s["lg"], least(k - 4, TILES))
                if exists(k - 4):
                    nc.tensor.matmul(lgp, xT[:, v, 1, :], rw[:], start=True, stop=True).then_inc(s["lgp"], 1)
                t, u, w = k - 2, (v - 2) % RING, (v - 2) % 2
                if exists(t):
                    nc.tensor.transpose(turned[:, 2, :], upd[:, w, :], ident).then_inc(s["updTp"], 1)
                    nc.tensor.matmul(proj, xT[:, u, 0, :], wo[:, 0:P], start=True, stop=False)
                t, u, w = k, v, v % 2
                if exists(t):
                    pe.wait_ge(s["q"], t + 1)
                    pe.wait_ge(s["k"], t + 1)
                    pe.wait_ge(s["masks"], t + 1)
                    at_least(pe, s["shifted"], t)
                    for g in range(PAIRS):
                        nc.tensor.matmul(S[:, g, 0:2 * SEQ], ind[:], mneg[:, u, :].unsqueeze(1)
                                         .broadcast_to([2, 2, SEQ]), start=True, stop=True)
                    for g in range(PAIRS):
                        r = slice(32 * g, 32 * g + 32)
                        for b in range(2):
                            keys = kT[r, w, :].rearrange("p (j b s) -> p j b s", j=2, b=2)[:, :, b, :]
                            mm = nc.tensor.matmul(S[b * SEQ:(b + 1) * SEQ, g, 0:2 * SEQ],
                                                  qT[r, w, b * SEQ:(b + 1) * SEQ], keys, start=False, stop=True,
                                                  skip_group_check=True)
                    mm.then_inc(s["scores"], 1)
                t, w = k - 2, (v - 2) % 2
                if exists(t):
                    pe.wait_ge(s["updT"], t + 1)
                    nc.tensor.matmul(proj, updT[:, w, :], wo[:, P:2 * P], start=False,
                                     stop=True).then_inc(s["proj"], 1)
                t, w = k - 1, (v - 1) % 2
                if exists(t):
                    pe.wait_ge(s["PT"], t + 1)
                    pe.wait_ge(s["v"], 2 * t + 2)
                    for b in range(2):
                        for g in range(PAIRS):
                            mm = nc.tensor.matmul(O[b * SEQ:(b + 1) * SEQ, g * 34:(g + 1) * 34],
                                                  PT[:, w, g, b * SEQ:(b + 1) * SEQ],
                                                  V[:, w, b, g, :, :], start=True, stop=True)
                    mm.then_inc(s["pv"], 1)
            staggered(pe, step, TILES, 2 * RING, RING)

        @block.scalar
        def _(act):
            act.wait_ge(zeros_out, 16)
            for dst in io["zeroed"]:
                act.dma_start(dst, zero[:]).then_inc(zeros_out, 16)
            act.wait_ge(consts_landed, 16 * (n_consts + 1))

            def step(k, v):
                lo, hi = 0 if exists(k) else 1, 2 if exists(k - 4) else 1
                if lo < hi:
                    act.wait_ge(s["xTp"], k + 1)
                    at_least(act, s["keptT"], least(k - 7, TILES))
                    at_least(act, s["lgp"], least(k - 7, TILES))
                    at_least(act, s["proj"], least(k - 3, TILES))
                    nc.scalar.copy(xT[:, v, lo:hi, :], turned[:, lo:hi, :]).then_inc(s["xT"], 1)
                t, w = k - 1, (v - 1) % 2
                if exists(t):
                    act.wait_ge(s["shifted"], t + 1)
                    at_least(act, s["PTp"], t - 1)
                    nc.scalar.activation(PR[:, w].rearrange("p g c -> p (g c)"),
                                         D[:, w].rearrange("p g j c -> p (g j c)"), ACT.Exp,
                                         scale=SCALE).then_inc(s["probs"], 1)
                if exists(k):
                    act.wait_ge(c_landed[v], slot_wait(k, v, 48))
                    at_least(act, s["k"], k - RING + 1)
                    for j in range(2):
                        a = nc.scalar.activation(mhalf[:, v, j * P:(j + 1) * P], mrow[:, v, :], ACT.Copy,
                                                 scale=C[:, C_HALF + j:C_HALF + j + 1])
                    a.then_inc(s["halves"], 1)
                if exists(t):
                    act.wait_ge(s["PTp"], t + 1)
                    at_least(act, s["pv"], t - 1)
                    nc.scalar.copy(PT[:, w], PTp[:]).then_inc(s["PT"], 1)
                t, w = k - 2, (v - 2) % 2
                if exists(t):
                    act.wait_ge(s["updTp"], t + 1)
                    at_least(act, s["proj"], t - 1)
                    nc.scalar.activation(updT[:, w, :], turned[:, 2, :], ACT.Identity,
                                         bias=cols[:, 2:3]).then_inc(s["updT"], 1)
            staggered(act, step, TILES, 2 * RING, RING)
            act.wait_ge(zeros_out, 16 + 16 * len(io["zeroed"]))


def route(nc, dve, link, LOG, C, w, rank_ps, total_ps, pe_needs, pe_done, act_needs, act_done, second):
    TE = [P, TILES, E0]

    def over_e(a):
        return a.unsqueeze(2).broadcast_to(TE)

    iota = C[:, C_IOTA:C_IOTA + E0].unsqueeze(1).broadcast_to(TE)
    rest = LOG
    for n in range(2):
        top, hot = w["top"][:, n, :], w["hot"][:, n]
        link(nc.vector.tensor_reduce(top, rest[:], AX.X, ALU.max))
        link(nc.vector.tensor_tensor(w["a"][:], rest[:], over_e(top), ALU.is_equal))
        link(nc.vector.scalar_tensor_tensor(w["b"][:], w["a"][:], -float(E0), iota, ALU.mult, ALU.add))
        link(nc.vector.tensor_reduce(w["t"][:], w["b"][:], AX.X, ALU.min))
        link(nc.vector.tensor_tensor(hot, w["b"][:], over_e(w["t"][:]), ALU.is_equal))
        if n == 0:
            link(nc.vector.scalar_tensor_tensor(w["rest"][:], hot, NEG, LOG[:], ALU.mult, ALU.add))
            rest = w["rest"]
    if second:
        link(nc.vector.tensor_tensor(w["t"][:], w["top"][:, 1, :], w["top"][:, 0, :], ALU.subtract), act_needs)
    else:
        link(nc.vector.tensor_tensor(w["a"][:], LOG[:], over_e(w["top"][:, 0, :]), ALU.subtract))
        link(nc.vector.tensor_tensor(w["t"][:], w["top"][:, 1, :], w["top"][:, 0, :], ALU.subtract), act_needs)
    dve.wait_ge(act_done, 1)
    if second:
        link(nc.vector.tensor_scalar(w["sum"][:], w["exp2"][:], 1.0, None, ALU.add))
        link(nc.vector.reciprocal(w["w"][:, 0, :], w["sum"][:]))
        link(nc.vector.tensor_tensor(w["w"][:, 1, :], w["exp2"][:], w["w"][:, 0, :], ALU.mult))
        link(nc.vector.tensor_scalar(w["t"][:], w["w"][:, 1, :], 0.0, None, ALU.is_gt))
        link(nc.vector.tensor_tensor(w["a"][:], w["hot"][:, 1], over_e(w["t"][:]), ALU.mult))
        link(nc.vector.tensor_tensor(w["chosen"][:], w["a"][:], w["hot"][:, 0], ALU.add), pe_needs)
    else:
        link(nc.vector.tensor_reduce(w["sum"][:], w["b"][:], AX.X, ALU.add))
        link(nc.vector.reciprocal(w["w"][:, 0, :], w["sum"][:]))
        link(nc.vector.tensor_tensor(w["w"][:, 1, :], w["exp2"][:], w["w"][:, 0, :], ALU.mult))
        link(nc.vector.tensor_tensor(w["chosen"][:], w["hot"][:, 0], w["hot"][:, 1], ALU.add), pe_needs)
    dve.wait_ge(pe_done, 1)
    link(nc.vector.tensor_tensor_scan(w["upto"][:], C[:, C_KEEP:C_KEEP + TILES * E0], total_ps[:], 0.0,
                                      ALU.mult, ALU.add))
    link(nc.vector.tensor_tensor(w["rank"][:], w["upto"][:], total_ps[:], ALU.subtract))
    link(nc.vector.tensor_tensor(w["rank"][:], w["rank"][:], rank_ps[:], ALU.add))
    rank = w["rank"][:].rearrange("p (e t) -> p e t", e=E0)
    if second:
        link(nc.vector.tensor_scalar(w["upto"][:], w["rank"][:], float(CAPACITY), float(OUT_OF_RANGE),
                                     ALU.is_ge, ALU.mult))
        link(nc.vector.tensor_tensor(w["rank"][:], w["rank"][:], w["upto"][:], ALU.add))
        link(nc.vector.tensor_scalar(w["base"][:], C[:, C_IOTA:C_IOTA + E0], float(CAPACITY), None, ALU.mult))
    else:
        count = w["upto"][:].rearrange("p (e t) -> p e t", e=E0)[:, :, TILES - 1]
        full = TOKENS // BLOCK
        link(nc.vector.tensor_scalar(w["steps"][:], C[:, C_IOTA:C_IOTA + full], float(BLOCK), None, ALU.mult))
        link(nc.vector.tensor_tensor(w["over"][:], count.unsqueeze(2).broadcast_to([P, E0, full]),
                                     w["steps"][:].unsqueeze(1).broadcast_to([P, E0, full]), ALU.is_gt))
        link(nc.vector.tensor_reduce(w["blocks"][:], w["over"][:], AX.X, ALU.add))
        link(nc.vector.tensor_tensor_scan(w["last"][:], C[:, C_ONES:C_ONES + E0], w["blocks"][:], 0.0,
                                          ALU.mult, ALU.add))
        link(nc.vector.tensor_tensor(w["first"][:], w["last"][:], w["blocks"][:], ALU.subtract))
        link(nc.vector.tensor_scalar(w["base"][:], w["first"][:], float(BLOCK), None, ALU.mult))
        one = [1, BLOCKS, E0]
        link(nc.vector.tensor_tensor(w["owns"][:], w["first"][0:1, :].unsqueeze(1).broadcast_to(one),
                                     C[0:1, C_IOTA:C_IOTA + BLOCKS].unsqueeze(2).broadcast_to(one), ALU.is_le))
        link(nc.vector.tensor_reduce(w["owner_f"][:], w["owns"][:], AX.X, ALU.add))
        link(nc.vector.tensor_scalar(w["owner"][:], w["owner_f"][:], -1.0, None, ALU.add))
    link(nc.vector.tensor_tensor(rank, rank, w["base"][:].unsqueeze(2).broadcast_to([P, E0, TILES]), ALU.add))
    for n in range(2):
        link(nc.vector.tensor_tensor(w["a"][:], w["hot"][:, n], rank.rearrange("p e t -> p t e"), ALU.mult))
        slot = w["slot_f"][:, n, :]
        link(nc.vector.tensor_reduce(slot, w["a"][:], AX.X, ALU.add))
        if second:
            weight = w["w"][:, n, :]
            link(nc.vector.tensor_scalar(w["t"][:], weight, 0.0, float(OUT_OF_RANGE), ALU.is_le, ALU.mult))
            link(nc.vector.tensor_tensor(slot, slot, w["t"][:], ALU.add))
            link(nc.vector.tensor_scalar(w["t"][:], slot, float(TOKENS), None, ALU.is_lt))
            link(nc.vector.tensor_tensor(weight, weight, w["t"][:], ALU.mult))
    return nc.vector.tensor_copy(w["slot"][:].rearrange("p t n -> p n t"), w["slot_f"][:])


def route_buffers(m, keep, tag):
    sb = m.sb
    w = {n: sb(tag + n, [P, TILES, E0]) for n in ("a", "b", "rest")}
    w.update({n: sb(tag + n, [P, E0 * TILES]) for n in ("upto", "rank")})
    w.update({n: sb(tag + n, [P, TILES]) for n in ("t", "sum", "exp2")})
    w.update({n: sb(tag + n, [P, E0]) for n in ("blocks", "last", "first", "base")})
    w.update(hot=sb(tag + "hot", [P, 2, TILES, E0]), chosen=sb(tag + "chosen", [P, TILES, E0], BF16),
             top=sb(tag + "top", [P, 2, TILES]), slot_f=sb(tag + "slot_f", [P, 2, TILES]),
             steps=sb(tag + "steps", [P, TOKENS // BLOCK]), over=sb(tag + "over", [P, E0, TOKENS // BLOCK]),
             owns=sb(tag + "owns", [1, BLOCKS, E0]), owner_f=sb(tag + "owner_f", [1, BLOCKS]),
             owner=keep["OWNER"], w=keep["W"], slot=keep["SLOT"],
             before=sb(tag + "before", [P, P], BF16), ones=sb(tag + "ones", [P, P], BF16))
    return w


def route_exps(nc, act, w, needs, done, second):
    act.wait_ge(needs, 1)
    if not second:
        nc.scalar.activation(w["b"][:], w["a"][:], ACT.Exp)
    nc.scalar.activation(w["exp2"][:], w["t"][:], ACT.Exp).then_inc(done, 1)


def route_counts(nc, pe, w, rank_ps, total_ps, tables, needs, done):
    pe.wait_ge(tables, 2)
    pe.wait_ge(needs, 1)
    chosen = w["chosen"][:].rearrange("p t e -> p e t")
    nc.tensor.matmul(rank_ps[:], w["before"][:], chosen, start=True, stop=True)
    nc.tensor.matmul(total_ps[:], w["ones"][:], chosen, start=True, stop=True).then_inc(done, 1)


GROUP = 4
GROUPS = TILES // GROUP


def group_wait(g, v, each):
    return each * (g // 2 + 1) if isinstance(g, int) else (g - v) * (each // 2) + each


def copy_group(nc, dve, keep, rows, index, g, v, copied, sent):
    if not isinstance(g, int) or g >= 2:
        dve.wait_ge(sent[v], group_wait(g - 2, v, 32 * GROUP) if isinstance(g, int) else (g - v) * 16 * GROUP)
    nc.vector.tensor_copy(rows[:, v], tile_of(keep["XN"][:].rearrange("p (g t) c -> p g (t c)", t=GROUP), g)
                          ).then_inc(copied, 1)
    nc.vector.tensor_copy(index[:, v], tile_of(keep["SLOT"][:].rearrange("p (g t) n -> p g (t n)", t=GROUP), g)
                          ).then_inc(copied, 1)


def scatter_rows(nc, pool, rows, index, copied, sent, dst, most):
    def step(g, v):
        wait_alone(pool, copied, 2 * g + 2, copied, 2)
        for t in range(GROUP):
            for n in range(2):
                slot = index[:, v, 2 * t + n:2 * t + n + 1]
                nc.gpsimd.indirect_dma_start(dst, bass.IndirectOffsetOnAxis(ap=slot, axis=0),
                                             rows[:, v, t * P:(t + 1) * P], None, bounds_check=most - 1,
                                             oob_is_err=False).then_inc(sent[v], 16)
    with pool.Fori(0, GROUPS // 2) as i:
        step(2 * i, 0)
        step(2 * i + 1, 1)
    for v in range(2):
        pool.wait_ge(sent[v], 16 * GROUP * GROUPS)


def shared_phase(nc, io, keep):
    X, XNT, C = keep["X"], keep["XNT"], keep["C"]
    SUB = WIDE // P
    assert WIDE == GROUP * P
    with ExitStack() as ctx:
        m = Mem(nc, ctx)
        sb, ps, sem = m.sb, m.ps, m.sem
        w = route_buffers(m, keep, "b_")
        rows, index = sb("b_rows", [P, 2, GROUP * P]), sb("b_index", [P, 2, 2 * GROUP], U32)

        WS = sb("b_W", [P, W_COLS])
        up, upb = WS[:, W_UP:W_UP + F0], WS[:, W_UPB:W_UPB + CHUNKS0]
        down = WS[:, W_DOWN:W_DOWN + F0].rearrange("p (c h) -> p c h", c=CHUNKS0)
        G = sb("b_G", [P, 2, CHUNKS0, WIDE])
        lens_i, lens = sb("b_lens_i", [P, PATCHES], I32), sb("b_lens", [P, PATCHES])
        ends, neg, mark = sb("b_ends", [P, PATCHES]), sb("b_neg", [P, PATCHES]), sb("b_mark", [P, SEQ])
        hits, plug = sb("b_hits", [P, SEQ, PATCHES]), sb("b_plug", [P, SEQ])
        hid = ps("b_hid", [P, CHUNKS0, WIDE])
        y = ps("b_y", [P, 2, WIDE])
        rank_ps, total_ps = ps("b_rank_ps", [P, WIDE]), ps("b_total_ps", [P, WIDE])
        s = {n: sem("b_" + n) for n in ("landed chain exps_wanted exps counts_wanted counts tables slots hid gelu y "
                                        "biased added plugged copied experts_landed").split()}
        sent = [sem(f"b_sent{v}") for v in range(2)]
        block = ctx.enter_context(nc.Block())

        @block.sync
        def _(sp):
            sp.dma_start(WS[:], io["shared_w"]).then_inc(s["landed"], 16)
            for e in range(E0):
                sp.dma_start(keep["WE"][:, e, :], io["expert_w"][e]).then_inc(s["experts_landed"], 16)
            sp.wait_ge(s["experts_landed"], 16 * E0)
            sp.dma_start(lens_i[:], io["mask_BxS2_if0"]).then_inc(s["landed"], 16)
            sp.wait_ge(s["plugged"], 1)
            sp.dma_start(io["plug"], plug[:]).then_inc(s["landed"], 16)
            sp.wait_ge(s["landed"], 48)

        @block.gpsimd
        def _(pool):
            nc.gpsimd.tensor_copy(w["before"][:], C[:, C_BEFORE:C_BEFORE + P]).then_inc(s["tables"], 1)
            nc.gpsimd.tensor_copy(w["ones"][:], C[:, C_ONES:C_ONES + P]).then_inc(s["tables"], 1)
            scatter_rows(nc, pool, rows, index, s["copied"], sent, io["xg0"], SLOTS)

        @block.scalar
        def _(act):
            route_exps(nc, act, w, s["exps_wanted"], s["exps"], second=False)
            act.wait_ge(s["landed"], 32)

            def step(k, v):
                for c in range(CHUNKS0):
                    act.wait_ge(s["hid"], CHUNKS0 * k + c + 1)
                    if c == 0:
                        at_least(act, s["y"], k - 1)
                    nc.scalar.activation(G[:, v, c, :], hid[:, c, :], ACT.Gelu,
                                         bias=upb[:, c:c + 1]).then_inc(s["gelu"], 1)
            step(0, 0)
            step(1, 1)
            with act.Fori(1, GROUPS // 2) as i:
                step(2 * i, 0)
                step(2 * i + 1, 1)

        @block.tensor
        def _(pe):
            pe.wait_ge(s["landed"], 32)
            xt = XNT[:].rearrange("p (g t) c -> p g (t c)", g=GROUPS)

            def step(k, v):
                if not isinstance(k, int) or k < GROUPS:
                    for c in range(CHUNKS0):
                        at_least(pe, s["gelu"], CHUNKS0 * (k - 1) + c + 1)
                        nc.tensor.matmul(hid[:, c, :], up[:, c * P:(c + 1) * P], tile_of(xt, k), start=True,
                                         stop=True).then_inc(s["hid"], 1)
                k, v = k - 1, (v - 1) % 2
                if not isinstance(k, int) or k >= 0:
                    pe.wait_ge(s["gelu"], CHUNKS0 * (k + 1))
                    at_least(pe, s["added"], k - 1)
                    for t in range(SUB):
                        for c in range(CHUNKS0):
                            mm = nc.tensor.matmul(y[:, v, t * P:(t + 1) * P], G[:, v, c, t * P:(t + 1) * P],
                                                  down[:, c, :], start=c == 0, stop=c == CHUNKS0 - 1)
                    mm.then_inc(s["y"], 1)
            step(0, 0)
            step(1, 1)
            route_counts(nc, pe, w, rank_ps, total_ps, s["tables"], s["counts_wanted"], s["counts"])
            with pe.Fori(1, GROUPS // 2) as i:
                step(2 * i, 0)
                step(2 * i + 1, 1)
            step(GROUPS, 0)

        @block.vector
        def _(dve):
            count = [0]

            def link(ins, also=None):
                count[0] += 1
                ins.then_inc(s["chain"], 1)
                dve.wait_ge(s["chain"], count[0])
                if also is not None:
                    dve.sem_inc(also, 1)

            route(nc, dve, link, keep["LOG"], C, w, rank_ps, total_ps, s["counts_wanted"], s["counts"],
                  s["exps_wanted"], s["exps"], second=False).then_inc(s["slots"], 1)
            dve.wait_ge(s["slots"], 1)
            for g in range(2):
                copy_group(nc, dve, keep, rows, index, g, g, s["copied"], sent)
            xv = X[:].rearrange("p (g t) c -> p g (t c)", g=GROUPS)

            dve.wait_ge(s["landed"], 32)

            def step(k, v, more):
                bias = WS[:, W_DNB:W_DNB + H].unsqueeze(1).broadcast_to([P, SUB, H])
                x4 = tile_of(xv, k)
                nc.vector.tensor_tensor(x4.rearrange("p (t c) -> p t c", t=SUB), x4.rearrange("p (t c) -> p t c", t=SUB),
                                        bias, ALU.add).then_inc(s["biased"], 1)
                dve.wait_ge(s["biased"], k + 1)
                dve.wait_ge(s["y"], k + 1)
                nc.vector.tensor_tensor(x4, x4, y[:, v, :], ALU.add).then_inc(s["added"], 1)
                if more:
                    copy_group(nc, dve, keep, rows, index, k + 2, v, s["copied"], sent)
            with dve.Fori(0, GROUPS // 2 - 1) as i:
                step(2 * i, 0, True)
                step(2 * i + 1, 1, True)
            step(GROUPS - 2, 0, False)
            step(GROUPS - 1, 1, False)
            dve.wait_ge(s["landed"], 32)
            link(nc.vector.tensor_copy(lens[:], lens_i[:]))
            ones = C[:, C_ONES:C_ONES + PATCHES]
            link(nc.vector.tensor_tensor_scan(ends[:], ones, lens[:], 0.0, ALU.mult, ALU.add))
            link(nc.vector.tensor_scalar(ends[:], ends[:], -1.0, None, ALU.add))
            link(nc.vector.tensor_scalar(neg[:], ends[:], 0.0, float(SEQ), ALU.is_lt, ALU.mult))
            link(nc.vector.tensor_tensor(ends[:], ends[:], neg[:], ALU.add))
            box = [P, SEQ, PATCHES]
            link(nc.vector.tensor_tensor(hits[:], ends[:].unsqueeze(1).broadcast_to(box),
                                         C[:, C_IOTA:C_IOTA + SEQ].unsqueeze(2).broadcast_to(box), ALU.is_equal))
            link(nc.vector.tensor_reduce(mark[:], hits[:], AX.X, ALU.max))
            link(nc.vector.tensor_tensor_scan(plug[:], ones, mark[:], 0.0, ALU.mult, ALU.add))
            link(nc.vector.tensor_scalar(plug[:], plug[:], -1.0, 0.0, ALU.add, ALU.max))
            nc.vector.tensor_scalar(plug[:], plug[:], float(PATCHES - 1), C[:, C_ROW:C_ROW + 1], ALU.min,
                                    ALU.add).then_inc(s["plugged"], 1)


def experts_phase(nc, io, keep):
    C, OWNER = keep["C"], keep["OWNER"]
    SUB = BLOCK // P
    with ExitStack() as ctx:
        m = Mem(nc, ctx)
        sb, ps, sem = m.sb, m.ps, m.sem
        WE = keep["WE"]
        W = sb("e_w", [P, RING, W_COLS])
        rows = sb("e_rows", [P, RING, SUB, P])
        xT = sb("e_xT", [P, 2, BLOCK])
        G = sb("e_G", [P, 2, CHUNKS0, BLOCK])
        Y = sb("e_Y", [P, RING, SUB, P])
        xTp = ps("e_xTp", [P, 2, 512])
        hid = ps("e_hid", [P, 2, CHUNKS0, BLOCK])
        yp = ps("e_yp", [P, 2, 512])
        s = {n: sem("e_" + n) for n in "w xTp xT hid gelu yp y".split()}
        landed = [sem(f"e_landed{u}") for u in range(RING)]
        stored = [sem(f"e_stored{u}") for u in range(RING)]
        src = io["xg0"].rearrange("(k n p) c -> k p n c", p=P, n=SUB)
        dst = io["yg0"].rearrange("(k n p) c -> k p n c", p=P, n=SUB)
        block = ctx.enter_context(nc.Block())

        def blk(a, k):
            return a[k] if isinstance(k, int) else a[bass.ds(k, 1)].rearrange("a p n c -> (a p) n c")

        def real(k):
            return not isinstance(k, int) or 0 <= k < BLOCKS

        @block.sync
        def _(sp):
            def step(k, v):
                if real(k):
                    at_least(sp, s["xTp"], k - RING + 1)
                    sp.dma_start(rows[:, v], blk(src, k)).then_inc(landed[v], 16)
                k, v = k - 4, v
                if real(k):
                    sp.wait_ge(s["y"], k + 1)
                    sp.dma_start(blk(dst, k), Y[:, v]).then_inc(stored[v], 16)
            staggered(sp, step, BLOCKS, RING, RING)
            for u in range(RING):
                sp.wait_ge(stored[u], 16 * (BLOCKS // RING))

        @block.tensor
        def _(pe):
            ident = C[:, C_ID:C_ID + P]

            def step(k, v):
                if real(k):
                    pe.wait_ge(landed[v], 16 * (k // RING + 1) if isinstance(k, int) else (k - v) * 4 + 16)
                    at_least(pe, s["xT"], k - 1)
                    for n in range(SUB):
                        mm = nc.tensor.transpose(xTp[:, v % 2, n * P:(n + 1) * P], rows[:, v, n, :], ident)
                    mm.then_inc(s["xTp"], 1)
                k, v = k - 1, (v - 1) % RING
                if real(k):
                    pe.wait_ge(s["w"], k + 1)
                    pe.wait_ge(s["xT"], k + 1)
                    at_least(pe, s["gelu"], 2 * k - 2)
                    for c in range(CHUNKS0):
                        mm = nc.tensor.matmul(hid[:, v % 2, c, :], W[:, v, W_UP + c * P:W_UP + (c + 1) * P], xT[:, v % 2, :],
                                              start=True, stop=True)
                        if c % 2 == 1:
                            mm.then_inc(s["hid"], 1)
                k, v = k - 1, (v - 1) % RING
                if real(k):
                    pe.wait_ge(s["gelu"], 2 * k + 2)
                    at_least(pe, s["y"], k - 1)
                    for n in range(SUB):
                        for c in range(CHUNKS0):
                            mm = nc.tensor.matmul(yp[:, v % 2, n * P:(n + 1) * P], G[:, v % 2, c, n * P:(n + 1) * P],
                                                  W[:, v, W_DOWN + c * P:W_DOWN + (c + 1) * P], start=c == 0,
                                                  stop=c == CHUNKS0 - 1)
                    mm.then_inc(s["yp"], 1)
            staggered(pe, step, BLOCKS, RING, RING)

        @block.scalar
        def _(act):
            def step(k, v):
                if not real(k):
                    return
                at_least(act, s["yp"], k - 1)
                for c in range(CHUNKS0):
                    if c % 2 == 0:
                        act.wait_ge(s["hid"], 2 * k + c // 2 + 1)
                    a = nc.scalar.activation(G[:, v % 2, c, :], hid[:, v % 2, c, :], ACT.Gelu,
                                             bias=W[:, v, W_UPB + c:W_UPB + c + 1])
                    if c % 2 == 1:
                        a.then_inc(s["gelu"], 1)
            staggered(act, step, BLOCKS, RING, RING)

        @block.vector
        def _(dve):
            def step(k, v):
                if real(k):
                    dve.wait_ge(s["xTp"], k + 1)
                    at_least(dve, s["hid"], 2 * k - 2)
                    nc.vector.tensor_copy(xT[:, v % 2, :], xTp[:, v % 2, 0:BLOCK]).then_inc(s["xT"], 1)
                    at_least(dve, s["y"], k - RING + 1)
                    e = dve.value_load(OWNER[0:1, bass.ds(k, 1)], min_val=0, max_val=E0 - 1)
                    nc.vector.tensor_copy(W[:, v, :], tile_of(WE, e)).then_inc(s["w"], 1)
                k, v = k - 2, (v - 2) % RING
                if real(k):
                    dve.wait_ge(s["yp"], k + 1)
                    if not isinstance(k, int) or k >= RING:
                        dve.wait_ge(stored[v], 16 * (k // RING) if isinstance(k, int) else (k - v) * 4)
                    nc.vector.tensor_tensor(Y[:, v], yp[:, v % 2, 0:BLOCK].rearrange("p (n c) -> p n c", n=SUB),
                                            W[:, v, W_DNB:W_DNB + H].unsqueeze(1).broadcast_to([P, SUB, H]),
                                            ALU.add).then_inc(s["y"], 1)
            staggered(dve, step, BLOCKS, 2 * RING, RING)


def copy_index(nc, keep, t, u, index, copied):
    if exists(t):
        nc.vector.tensor_copy(index[:, u, :], tile_of(keep["SLOT"], t)).then_inc(copied, 1)


def gather_rows(nc, pool, t, u, index, copied, got, Y, src, most, met):
    wait_alone(pool, copied, t + 1, *met)
    for n in range(2):
        nc.gpsimd.indirect_dma_start(Y[:, u, n, :], None, src,
                                     bass.IndirectOffsetOnAxis(ap=index[:, u, n:n + 1], axis=0),
                                     bounds_check=most - 1, oob_is_err=False).then_inc(got[u], 16)


def depool_phase(nc, io, keep):
    X, XN, LOG, C = keep["X"], keep["XN"], keep["LOG"], keep["C"]
    with ExitStack() as ctx:
        m = Mem(nc, ctx)
        sb, ps, sem = m.sb, m.ps, m.sem
        cr = sb("d_ctx", [P, RING, CTX])
        plug = sb("d_plug", [P, RING, P])
        index, Y = sb("d_index", [P, RING, 2], U32), sb("d_Y", [P, RING, 2, P])
        win, g_res = sb("d_win", [P, P]), sb("d_g_res", [P, 1])
        winG = sb("d_winG", [P, P])
        g_init, b_in = sb("d_g_init", [P, P]), sb("d_b_in", [1, P])
        rw = sb("d_rw", [P, E1])
        power_of = sb("d_power_of", [P, 3])
        square = sb("d_square", [P, CTX])
        hot, cg, GT = (sb("d_" + n, [P, RING, P]) for n in ("hot", "cg", "GT"))
        stat, stat2 = sb("d_stat", [P, RING, 6]), sb("d_stat2", [P, RING, 6])
        mv = sb("d_mv", [P, RING, 3, 2])
        ve = sb("d_ve", [P, RING, 3])
        factor = sb("d_factor", [P, RING, 3])
        z, xn = sb("d_z", [P, RING, P]), sb("d_xn", [P, RING, P])
        xT = sb("d_xT", [P, RING, 2, P])
        turned, Gp, Hp, lgp = (ps("d_" + n, [P, 512]) for n in ("turned", "Gp", "Hp", "lgp"))
        s = {n: sem("d_" + n) for n in (
            "weights setup copied ss hot cg y1 x2 stat mv x3 stat2 mv2 ve factor z xn xTp xT Gp GT H kept lgp "
            "lg").split()}
        got = [sem(f"d_got{u}") for u in range(RING)]
        c_landed = [sem(f"d_c_landed{u}") for u in range(RING)]
        n_w = 16 * 5
        met = (s["setup"], 2)
        block = ctx.enter_context(nc.Block())

        @block.sync
        def _(sp):
            sp.dma_start(win[:], io["winT"]).then_inc(s["weights"], 16)
            sp.dma_start(rw[:], io["embT"]).then_inc(s["weights"], 16)
            sp.dma_start(g_res[:], io["L1_xattn_g_res"].rearrange("(p o) -> p o", o=1)).then_inc(s["weights"], 16)
            sp.dma_start(g_init[:], io["g_init"].partition_broadcast(P)).then_inc(s["weights"], 16)
            sp.dma_start(b_in[:], io["L1_xattn_b_in"].rearrange("(o d) -> o d", o=1)).then_inc(s["weights"], 16)

            def step(t, u):
                if not exists(t):
                    return
                at_least(sp, s["ss"], t - RING + 1)
                at_least(sp, s["cg"], t - RING + 1)
                at_least(sp, s["hot"], t - RING + 1)
                sp.dma_start(cr[:, u, :], row_of(io["ctx_tiles"], t)).then_inc(c_landed[u], 16)
                sp.dma_start(plug[:, u, :], io["plug_rows"][bass.ds(t, 1)].rearrange("a c -> (a c)")
                             .partition_broadcast(P)).then_inc(c_landed[u], 16)
            staggered(sp, step, TILES, RING, RING)

        @block.gpsimd
        def _(pool):
            nc.gpsimd.memset(power_of[:], -0.5).then_inc(s["setup"], 1)
            pool.wait_ge(s["weights"], n_w)
            nc.gpsimd.tensor_scalar(winG[:], win[:], g_res[:], None, ALU.mult).then_inc(s["setup"], 1)
            pool.wait_ge(*met)

            def gather(t, u):
                if exists(t):
                    wait_alone(pool, s["x2"], t - RING + 1, *met)
                    gather_rows(nc, pool, t, u, index, s["copied"], got, Y, io["yg0"], SLOTS, met)

            def step(k, v):
                t, u = k - 1, (v - 1) % RING
                if exists(t):
                    wait_alone(pool, c_landed[u], slot_wait(t, u, 32), *met)
                    wait_alone(pool, s["H"], t - RING + 1, *met)
                    nc.gpsimd.tensor_tensor(cg[:, u, :], cr[:, u, 0:H], g_init[:], ALU.mult).then_inc(s["cg"], 1)
                gather(k + 1, (v + 1) % RING)
                lo, hi = 0 if exists(k - 1) else 2, 3 if exists(k - 3) else 2
                if lo < hi:
                    if lo == 0:
                        wait_alone(pool, s["mv"], k, *met)
                        nc.gpsimd.tensor_scalar(ve[:, v, 0:1], mv[:, v, 0, 1:2], 1.0 + LN_EPS, LN_EPS * LN_EPS,
                                                ALU.mult, ALU.add).then_inc(s["ve"], 1)
                        wait_alone(pool, s["ss"], k, *met)
                    wait_alone(pool, s["mv2"], least(k - 2, TILES), *met)
                    lo1 = max(lo, 1)
                    nc.gpsimd.tensor_scalar(ve[:, v, lo1:hi], mv[:, v, lo1:hi, 1], LN_EPS, None,
                                            ALU.add).then_inc(s["ve"], 1)
                    wait_alone(pool, s["ve"], 2 * k if exists(k - 1) else k + TILES, *met)
                    nc.gpsimd.tensor_tensor(factor[:, v, lo:hi], ve[:, v, lo:hi], power_of[:, lo:hi],
                                            ALU.pow).then_inc(s["factor"], 1)
            gather(0, 0)
            staggered(pool, step, TILES, RING, RING, peel=RING)

        @block.vector
        def _(dve):
            dve.wait_ge(s["weights"], n_w)
            dve.wait_ge(*met)
            W = keep["W"]
            for t in range(3):
                copy_index(nc, keep, t, t, index, s["copied"])

            def add_choice(t, u, n, name):
                nc.vector.scalar_tensor_tensor(tile_of(X, t), Y[:, u, n, :], W[:, n, bass.ds(t, 1)],
                                               tile_of(X, t), ALU.mult, ALU.add).then_inc(s[name], 1)

            def step(k, v):
                w = (v - 1) % RING
                t, u = k - 2, (v - 2) % RING
                if exists(k - 2) or exists(k - 4):
                    dve.wait_ge(s["factor"], k - 1)
                if exists(t):
                    nc.vector.tensor_scalar(z[:, u, :], tile_of(X, t), mv[:, w, 0, 0:1], factor[:, w, 0:1],
                                            ALU.subtract, ALU.mult).then_inc(s["z"], 1)
                t, u = k - 4, v
                if exists(t):
                    at_least(dve, s["kept"], t - RING + 1)
                    nc.vector.tensor_scalar(xn[:, u, :], tile_of(X, t), mv[:, w, 2, 0:1], factor[:, w, 2:3],
                                            ALU.subtract, ALU.mult).then_inc(s["xn"], 1)
                old, new = k - 3, k - 1
                uo, un = (v - 3) % RING, (v - 1) % RING
                if exists(old):
                    dve.wait_ge(s["H"], old + 1)
                    nc.vector.tensor_tensor(tile_of(X, old), tile_of(X, old), Hp[:, 0:P], ALU.add).then_inc(s["x3"], 1)
                if exists(new):
                    dve.wait_ge(got[un], slot_wait(new, un, 32))
                    add_choice(new, un, 0, "y1")
                if exists(old):
                    wait_alone(dve, s["x3"], old + 1, *met)
                    nc.vector.bn_stats(stat2[:, uo, :], tile_of(X, old)).then_inc(s["stat2"], 1)
                if exists(new):
                    wait_alone(dve, s["y1"], new + 1, *met)
                    add_choice(new, un, 1, "x2")
                if exists(old):
                    wait_alone(dve, s["stat2"], old + 1, *met)
                    nc.vector.bn_aggr(mv[:, v, 2, :], stat2[:, uo, :]).then_inc(s["mv2"], 1)
                if exists(k - 5):
                    dve.wait_ge(s["lgp"], k - 4)
                    nc.vector.tensor_copy(tile_of(LOG, k - 5), lgp[:, 0:E1]).then_inc(s["lg"], 1)
                if exists(new):
                    wait_alone(dve, s["x2"], new + 1, *met)
                    nc.vector.bn_stats(stat[:, un, :], tile_of(X, new)).then_inc(s["stat"], 1)
                    dve.wait_ge(c_landed[un], slot_wait(new, un, 32))
                    at_least(dve, s["Gp"], new - RING + 1)
                    nc.vector.tensor_scalar(hot[:, un, :], plug[:, un, :], C[:, C_PART:C_PART + 1], None,
                                            ALU.is_equal).then_inc(s["hot"], 1)
                    wait_alone(dve, s["stat"], new + 1, *met)
                    nc.vector.bn_aggr(mv[:, v, 0, :], stat[:, un, :]).then_inc(s["mv"], 1)
                    copy_index(nc, keep, k + 2, (v + 2) % RING, index, s["copied"])
            staggered(dve, step, TILES, 2 * RING, RING, peel=RING)

        @block.tensor
        def _(pe):
            ident, decay = C[:, C_ID:C_ID + P], C[:, C_DECAY:C_DECAY + P]
            pe.wait_ge(s["weights"], n_w)
            pe.wait_ge(*met)

            def step(k, v):
                t = k - 2
                mm = None
                at_least(pe, s["xT"], min(k - 2, TILES + 2) if isinstance(k, int) else k - 2)
                if exists(k - 4):
                    pe.wait_ge(s["xn"], k - 3)
                    mm = nc.tensor.transpose(turned[:, P:2 * P], xn[:, v, :], ident)
                if exists(t):
                    pe.wait_ge(s["z"], t + 1)
                    mm = nc.tensor.transpose(turned[:, 0:P], z[:, (v - 2) % RING, :], ident)
                if mm is not None:
                    mm.then_inc(s["xTp"], 1)
                u = (v - 2) % RING
                if exists(t):
                    pe.wait_ge(s["hot"], t + 1)
                    at_least(pe, s["GT"], t)
                    nc.tensor.matmul(Gp[:, 0:P], decay, hot[:, u, :], start=True, stop=True).then_inc(s["Gp"], 1)
                    pe.wait_ge(s["xT"], k - 1)
                    at_least(pe, s["x3"], t)
                    nc.tensor.matmul(Hp[:, 0:P], C[0:1, C_ONES:C_ONES + P], b_in[:], start=True, stop=False)
                    nc.tensor.matmul(Hp[:, 0:P], xT[:, v, 0, :], winG[:], start=False, stop=False)
                    pe.wait_ge(s["cg"], t + 1)
                    pe.wait_ge(s["GT"], t + 1)
                    nc.tensor.matmul(Hp[:, 0:P], GT[:, u, :], cg[:, u, :], start=False, stop=True).then_inc(s["H"], 1)
                t = k - 4
                if exists(t):
                    pe.wait_ge(s["xT"], k - 1)
                    at_least(pe, s["lg"], t)
                    nc.tensor.matmul(lgp[:, 0:E1], xT[:, v, 1, :], rw[:], start=True, stop=True).then_inc(s["lgp"], 1)
            staggered(pe, step, TILES, 2 * RING, RING)

        @block.scalar
        def _(act):
            def step(k, v):
                lo, hi = 0 if exists(k - 2) else 1, 2 if exists(k - 4) else 1
                if lo < hi:
                    act.wait_ge(s["xTp"], k - 1)
                    at_least(act, s["H"], least(k - 5, TILES))
                    at_least(act, s["lgp"], least(k - 7, TILES))
                    nc.scalar.copy(xT[:, v, lo:hi, :].rearrange("p a c -> p (a c)"),
                                   turned[:, lo * P:hi * P]).then_inc(s["xT"], 1)
                t, u = k - 2, (v - 2) % RING
                if exists(t):
                    act.wait_ge(s["Gp"], t + 1)
                    act.wait_ge(s["factor"], k - 1)
                    at_least(act, s["H"], t - RING + 1)
                    nc.scalar.activation(GT[:, u, :], Gp[:, 0:P], ACT.Copy, 
                                         scale=factor[:, (v - 1) % RING, 1:2]).then_inc(s["GT"], 1)
                t, u = k - 1, (v - 1) % RING
                if exists(t):
                    act.wait_ge(c_landed[u], slot_wait(t, u, 32))
                    at_least(act, s["ss"], t)
                    at_least(act, s["factor"], k - RING)
                    nc.scalar.activation(square[:], cr[:, u, :], ACT.Square, scale=CTX ** -0.5,
                                         accum_out=mv[:, v, 1, 1:2]).then_inc(s["ss"], 1)
                t = k - 4
                if exists(t):
                    nc.scalar.copy(tile_of(XN, t), xn[:, v, :]).then_inc(s["kept"], 1)
            staggered(act, step, TILES, 2 * RING, RING)


def second_route_phase(nc, io, keep):
    C = keep["C"]
    with ExitStack() as ctx:
        m = Mem(nc, ctx)
        w = route_buffers(m, keep, "r_")
        rows, index = m.sb("r_rows", [P, 2, GROUP * P]), m.sb("r_index", [P, 2, 2 * GROUP], U32)
        rank_ps, total_ps = m.ps("r_rank_ps", [P, WIDE]), m.ps("r_total_ps", [P, WIDE])
        s = {n: m.sem("r_" + n) for n in "chain exps_wanted exps counts_wanted counts tables slots copied".split()}
        sent = [m.sem(f"r_sent{v}") for v in range(2)]
        block = ctx.enter_context(nc.Block())

        @block.gpsimd
        def _(pool):
            nc.gpsimd.tensor_copy(w["before"][:], C[:, C_BEFORE:C_BEFORE + P]).then_inc(s["tables"], 1)
            nc.gpsimd.tensor_copy(w["ones"][:], C[:, C_ONES:C_ONES + P]).then_inc(s["tables"], 1)
            scatter_rows(nc, pool, rows, index, s["copied"], sent, io["xg1"], TOKENS)

        @block.scalar
        def _(act):
            route_exps(nc, act, w, s["exps_wanted"], s["exps"], second=True)

        @block.tensor
        def _(pe):
            route_counts(nc, pe, w, rank_ps, total_ps, s["tables"], s["counts_wanted"], s["counts"])

        @block.vector
        def _(dve):
            count = [0]

            def link(ins, also=None):
                count[0] += 1
                ins.then_inc(s["chain"], 1)
                dve.wait_ge(s["chain"], count[0])
                if also is not None:
                    dve.sem_inc(also, 1)
            route(nc, dve, link, keep["LOG"], C, w, rank_ps, total_ps, s["counts_wanted"], s["counts"],
                  s["exps_wanted"], s["exps"], second=True).then_inc(s["slots"], 1)
            dve.wait_ge(s["slots"], 1)
            for g in range(2):
                copy_group(nc, dve, keep, rows, index, g, g, s["copied"], sent)
            with dve.Fori(1, GROUPS // 2) as i:
                for v in range(2):
                    copy_group(nc, dve, keep, rows, index, 2 * i + v, v, s["copied"], sent)


def second_experts_phase(nc, io, keep):
    C = keep["C"]
    SUB, STEPS, PER = WIDE // P, TOKENS // WIDE, CAPACITY // WIDE
    with ExitStack() as ctx:
        m = Mem(nc, ctx)
        sb, ps, sem = m.sb, m.ps, m.sem
        WE = sb("f_W", [P, E1, 2 * F1])
        W = sb("f_w", [P, 2, 2 * F1])
        rows, Y = sb("f_rows", [P, RING, SUB, P]), sb("f_Y", [P, RING, SUB, P])
        xT, G = sb("f_xT", [P, 2, WIDE]), sb("f_G", [P, 2, CHUNKS1, WIDE])
        xTp, hid, yp = ps("f_xTp", [P, 2, WIDE]), ps("f_hid", [P, 2, CHUNKS1, WIDE]), ps("f_yp", [P, 2, WIDE])
        s = {n: sem("f_" + n) for n in "weights w xTp xT hid relu yp y".split()}
        landed = [sem(f"f_landed{u}") for u in range(RING)]
        stored = [sem(f"f_stored{u}") for u in range(RING)]
        src = io["xg1"].rearrange("(k n p) c -> k p n c", p=P, n=SUB)
        dst = io["yg1"].rearrange("(k n p) c -> k p n c", p=P, n=SUB)
        block = ctx.enter_context(nc.Block())

        def blk(a, k):
            return a[k] if isinstance(k, int) else a[bass.ds(k, 1)].rearrange("a p n c -> (a p) n c")

        def real(k):
            return not isinstance(k, int) or 0 <= k < STEPS

        @block.sync
        def _(sp):
            for e in range(E1):
                sp.dma_start(WE[:, e, :], io["expert1_w"][e]).then_inc(s["weights"], 16)

            def step(k, v):
                if real(k):
                    at_least(sp, s["xTp"], k - RING + 1)
                    sp.dma_start(rows[:, v], blk(src, k)).then_inc(landed[v], 16)
                k = k - 4
                if real(k):
                    sp.wait_ge(s["y"], k + 1)
                    sp.dma_start(blk(dst, k), Y[:, v]).then_inc(stored[v], 16)
            staggered(sp, step, STEPS, RING, RING)
            for u in range(RING):
                sp.wait_ge(stored[u], 16 * (STEPS // RING))

        @block.gpsimd
        def _(pool):
            pool.wait_ge(s["weights"], 16 * E1)

            def step(e, v):
                wait_alone(pool, s["yp"], PER * (e - 1), s["weights"], 16 * E1)
                nc.gpsimd.tensor_copy(W[:, v, :], tile_of(WE, e)).then_inc(s["w"], 1)
            step(0, 0)
            step(1, 1)
            with pool.Fori(1, E1 // 2) as i:
                step(2 * i, 0)
                step(2 * i + 1, 1)

        @block.tensor
        def _(pe):
            ident = C[:, C_ID:C_ID + P]

            def step(k, v):
                if real(k):
                    pe.wait_ge(landed[v], slot_wait(k, v, 16))
                    at_least(pe, s["xT"], k - 1)
                    for n in range(SUB):
                        mm = nc.tensor.transpose(xTp[:, v % 2, n * P:(n + 1) * P], rows[:, v, n, :], ident)
                    mm.then_inc(s["xTp"], 1)
                k, v = k - 1, (v - 1) % RING
                if real(k):
                    pe.wait_ge(s["w"], k // PER + 1)
                    pe.wait_ge(s["xT"], k + 1)
                    at_least(pe, s["relu"], k - 1)
                    for c in range(CHUNKS1):
                        mm = nc.tensor.matmul(hid[:, v % 2, c, :], W[:, v // PER, c * P:(c + 1) * P], xT[:, v % 2, :],
                                              start=True, stop=True)
                    mm.then_inc(s["hid"], 1)
                k, v = k - 1, (v - 1) % RING
                if real(k):
                    pe.wait_ge(s["relu"], k + 1)
                    at_least(pe, s["y"], k - 1)
                    for n in range(SUB):
                        for c in range(CHUNKS1):
                            mm = nc.tensor.matmul(yp[:, v % 2, n * P:(n + 1) * P], G[:, v % 2, c, n * P:(n + 1) * P],
                                                  W[:, v // PER, F1 + c * P:F1 + (c + 1) * P], start=c == 0,
                                                  stop=c == CHUNKS1 - 1)
                    mm.then_inc(s["yp"], 1)
            for k in range(STEPS + 2):
                step(k, k % RING)

        @block.scalar
        def _(act):
            for k in range(STEPS):
                v = k % 2
                at_least(act, s["yp"], k - 1)
                act.wait_ge(s["hid"], k + 1)
                nc.scalar.activation(G[:, v], hid[:, v], ACT.Relu).then_inc(s["relu"], 1)

        @block.vector
        def _(dve):
            def step(k, v):
                if real(k):
                    dve.wait_ge(s["xTp"], k + 1)
                    at_least(dve, s["hid"], k - 1)
                    nc.vector.tensor_copy(xT[:, v % 2, :], xTp[:, v % 2, :]).then_inc(s["xT"], 1)
                k, v = k - 2, (v - 2) % RING
                if real(k):
                    dve.wait_ge(s["yp"], k + 1)
                    if k >= RING:
                        dve.wait_ge(stored[v], 16 * (k // RING))
                    nc.vector.tensor_copy(Y[:, v].rearrange("p n c -> p (n c)"), yp[:, v % 2, :]).then_inc(s["y"], 1)
            for k in range(STEPS + 2):
                step(k, k % RING)


def output_phase(nc, io, keep):
    X, W = keep["X"], keep["W"]
    with ExitStack() as ctx:
        m = Mem(nc, ctx)
        index, Y = m.sb("o_index", [P, RING, 2], U32), m.sb("o_Y", [P, RING, 2, P])
        copied, added, setup = m.sem("o_copied"), m.sem("o_added"), m.sem("o_setup")
        got = [m.sem(f"o_got{u}") for u in range(RING)]
        out_done = m.sem("o_out_done")
        block = ctx.enter_context(nc.Block())

        @block.gpsimd
        def _(pool):
            nc.gpsimd.memset(Y[:], 0.0).then_inc(setup, 1)
            pool.wait_ge(setup, 1)

            def step(t, u):
                wait_alone(pool, added, 2 * (t - RING + 1), setup, 1)
                gather_rows(nc, pool, t, u, index, copied, got, Y, io["yg1"], TOKENS, (setup, 1))
            staggered(pool, lambda t, u: step(t, u) if exists(t) else None, TILES, RING, RING)

        @block.vector
        def _(dve):
            dve.wait_ge(setup, 1)
            for t in range(RING):
                copy_index(nc, keep, t, t, index, copied)

            def step(t, u):
                dve.wait_ge(got[u], slot_wait(t, u, 32))
                copy_index(nc, keep, t + RING, u, index, copied)
                for n in range(2):
                    nc.vector.scalar_tensor_tensor(tile_of(X, t), Y[:, u, n, :], W[:, n, bass.ds(t, 1)],
                                                   tile_of(X, t), ALU.mult, ALU.add).then_inc(added, 1)
                    if n == 0:
                        wait_alone(dve, added, 2 * t + 1, setup, 1)
            staggered(dve, lambda t, u: step(t, u) if exists(t) else None, TILES, RING, RING, peel=RING)

        @block.sync
        def _(sp):
            def step(t, u):
                sp.wait_ge(added, 2 * t + 2)
                sp.dma_start(row_of(io["out_tiles"], t), tile_of(X, t)).then_inc(out_done, 16)
            staggered(sp, lambda t, u: step(t, u) if exists(t) else None, TILES, RING, RING)
            sp.wait_ge(out_done, 16 * TILES)


def build(nc, io, out):
    zeroed = []
    io = dict(io)
    xg0 = nc.dram_tensor("xg0", [SLOTS, H], F32).ap()
    xg1 = nc.dram_tensor("xg1", [TOKENS, H], F32).ap()
    io["yg0"] = nc.dram_tensor("yg0", [SLOTS, H], F32).ap()
    io["yg1"] = nc.dram_tensor("yg1", [TOKENS, H], F32).ap()
    io["plug"] = nc.dram_tensor("plug", [BATCH, SEQ], F32).ap()
    io["xg0"], io["xg1"] = xg0, xg1
    for a, n in ((xg0, SLOTS), (xg1, TOKENS)):
        v = a.rearrange("(k p r) c -> k p (r c)", p=P, r=16)
        zeroed += [v[i] for i in range(n * H // (P * 2048))]
    io["zeroed"] = zeroed
    io["x_tiles"] = io["x"].rearrange("(t b) s d -> t (b s) d", b=2)
    io["out_tiles"] = out.rearrange("(t b) s d -> t (b s) d", b=2)
    io["plug_rows"] = io["plug"].rearrange("(t b) s -> t (b s)", b=2)
    io["ctx_tiles"] = io["ctx_2048"].rearrange("(t b) s d -> t (b s) d", b=2)
    io["mask_rows"] = io["mask_BxS2_fk1"].rearrange("(t b) s -> t (b s)", b=2)
    io["mask_pairs"] = io["mask_BxS2_fk1"].rearrange("(t b) s -> t b s", b=2)
    with ExitStack() as ctx:
        m = Mem(nc, ctx)
        keep = {
            "X": m.sb("X", [P, TILES, H]), "XN": m.sb("XN", [P, TILES, H]),
            "LOG": m.sb("LOG", [P, TILES, E0]), "C": m.sb("C", [P, C_COLS]),
            "W": m.sb("WEIGHT", [P, 2, TILES]), "SLOT": m.sb("SLOT", [P, TILES, 2], U32),
            "OWNER": m.sb("OWNER", [1, BLOCKS], I32),
        }
        with ExitStack() as weights:
            keep["WE"] = Mem(nc, weights).sb("WE", [P, E0, W_COLS])
            with ExitStack() as inner:
                keep["XNT"] = Mem(nc, inner).sb("XNT", [P, TILES, P])
                attention_phase(nc, io, keep)
                shared_phase(nc, io, keep)
            experts_phase(nc, io, keep)
        depool_phase(nc, io, keep)
        second_route_phase(nc, io, keep)
        second_experts_phase(nc, io, keep)
        output_phase(nc, io, keep)


def kernel(**inputs):
    import numpy as _np
    import concourse.bacc as _bacc
    from concourse import mybir as _mybir
    from concourse.bass_utils import run_bass_kernel_spmd as _run

    a = {k: _np.asarray(v) for k, v in inputs.items()}
    T, ctx = _np.transpose, a["ctx_2048"].reshape(TILES, P, 2, P)
    a["consts"] = constants()
    ctx = T(ctx, (0, 3, 2, 1)).reshape(TILES, P, 2, 2, 1, SEQ)
    a["ctxT"] = _np.broadcast_to(ctx, (TILES, P, 2, 2, 2, SEQ)).reshape(TILES, P, 4 * P)
    a["maskT"] = a["mask_BxS2_fk1"].T
    wsrc = a["L0_xattn_W_src"].reshape(2, H, 2, P)
    a["wkT"] = T(wsrc[0], (2, 1, 0)).reshape(P, 2 * P)
    a["wvT"] = T(wsrc[1], (2, 1, 0)).reshape(P, 2 * P)
    a["b_k"], a["b_v"] = a["L0_xattn_b_src"][:H], a["L0_xattn_b_src"][H:]
    a["wqT"] = a["L0_xattn_W_tgt"].T
    a["woT"] = T(a["L0_xattn_W_out"].reshape(H, 2, P), (2, 1, 0)).reshape(P, 2 * P)

    def ffn(up, down, up_b, down_b):
        n = up.shape[0]
        return _np.concatenate([up, T(down.reshape(n, CHUNKS0, P, H), (0, 2, 1, 3)).reshape(n, P, F0),
                                T(up_b.reshape(n, CHUNKS0, P), (0, 2, 1)),
                                _np.broadcast_to(down_b[:, None, :], (n, P, H))], axis=2)
    a["expert_w"] = ffn(a["L0_ffn_up_w"], a["L0_ffn_down_w"], a["L0_ffn_up_b"], a["L0_ffn_down_b"])
    a["shared_w"] = ffn(a["L0_ffn_sh_up_w"][None], a["L0_ffn_sh_down_w"][None], a["L0_ffn_sh_up_b"][None],
                        a["L0_ffn_sh_down_b"][None])[0]
    a["winT"] = a["L1_xattn_W_in"].T
    a["embT"] = a["L1_ffn_expert_embeddings"].T
    a["g_init"] = a["L1_xattn_g_init"][:H]
    first, second = a["L1_ffn_first_linear"], a["L1_ffn_second_linear"]
    a["expert1_w"] = _np.concatenate([T(first, (0, 2, 1)),
                                      T(second.reshape(E1, H, CHUNKS1, P), (0, 3, 2, 1)).reshape(E1, P, F1)], axis=2)
    names = ["ctx_2048", "winT", "embT", "g_init", "L1_xattn_g_res", "L1_xattn_b_in", "expert1_w", "x", "mask_BxS2_fk1", "consts", "ctxT", "maskT", "wkT", "wvT", "b_k", "b_v", "wqT", "woT",
             "L0_xattn_b_tgt", "L0_xattn_b_out", "L0_ffn_router_b", "L0_ffn_router_w",
             "mask_BxS2_if0", "expert_w", "shared_w"]
    nc = _bacc.Bacc("TRN2", target_bir_lowering=False, num_devices=1)
    arrays, io = {}, {}
    for name in names:
        v = _np.ascontiguousarray(a[name])
        arrays["in_" + name] = v
        io[name] = nc.dram_tensor("in_" + name, v.shape, _mybir.dt.from_np(v.dtype), kind="ExternalInput").ap()
    out = nc.dram_tensor("out_0", (BATCH, SEQ, H), _mybir.dt.float32, kind="ExternalOutput").ap()
    build(nc, io, out)
    r = _run(nc, [arrays], core_ids=[0])
    return r.results[0]["out_0"]
```

```python
from contextlib import ExitStack

import numpy as np
import concourse.bass as bass
from concourse import mybir

F32 = mybir.dt.float32
BF16 = mybir.dt.bfloat16
I32 = mybir.dt.int32
U32 = mybir.dt.uint32
ALU = mybir.AluOpType
ACT = mybir.ActivationFunctionType
AX = mybir.AxisListType

P = 128
BATCH, SEQ, H, CTX = 128, 64, 128, 256
TOKENS = BATCH * SEQ
TILES = TOKENS // P
HEADS, HEAD_DIM = 8, 16
PAIRS = HEADS // 2
E0, F0 = 8, 512
E1, F1 = 8, 256
CHUNKS0, CHUNKS1 = F0 // P, F1 // P
CAPACITY = TOKENS // E1
BLOCK = 256
BLOCKS = 2 * TOKENS // BLOCK + E0
SLOTS = BLOCKS * BLOCK
WIDE = 512
CHOICES = 2
ROW = H + 1
RING = 4
SCALE = HEAD_DIM ** -0.5
NEG = -1.0e30
LN_EPS = 1e-5
PATCHES = SEQ
EPSILON = 0.001
OUT_OF_RANGE = 4 * TOKENS

C_ID, C_DECAY, C_BEFORE, C_ONES, C_PART, C_ROW, C_HALF, C_IND, C_IOTA, C_KEEP = 0, 128, 256, 384, 512, 513, 514, 516, 644, 772
C_PLACE = C_KEEP + TILES * E0
C_COLS = C_PLACE + TILES * CHOICES

W_UP, W_DOWN, W_UPB, W_DNB = 0, F0, 2 * F0, 2 * F0 + CHUNKS0
W_COLS = W_DNB + H


ZEROS = P * ROW // 8


def constants():
    c = np.zeros((P, C_COLS), np.float32)
    i = np.arange(P)
    c[:, C_ID:C_ID + P] = np.eye(P)
    dt = -np.log(-np.expm1(np.float64(-EPSILON)))
    lag = (i[:, None] - i[None, :]).astype(np.float64)
    same = (i[:, None] // SEQ == i[None, :] // SEQ) & (lag >= 0)
    c[:, C_DECAY:C_DECAY + P] = np.where(same, np.exp(-EPSILON) * np.exp(-dt * np.maximum(lag, 0)), 0.0)
    c[:, C_BEFORE:C_BEFORE + P] = i[:, None] < i[None, :]
    c[:, C_ONES:C_ONES + P] = 1.0
    c[:, C_PART] = i
    for j in range(2):
        c[:, C_HALF + j] = (i // HEAD_DIM) % 2 == j
        c[j, C_IND:C_IND + P] = i // SEQ == j
    c[:, C_ROW] = SEQ * (i % 2)
    c[:, C_IOTA:C_IOTA + P] = i
    c[:, C_KEEP:C_PLACE] = (np.arange(TILES * E0) % TILES != 0)
    place = CHOICES * (P * np.arange(TILES)[None, :, None] + i[:, None, None]) + np.arange(CHOICES)
    c[:, C_PLACE:] = (place - OUT_OF_RANGE).reshape(P, -1)
    return c


def at_least(eng, sem, n):
    if isinstance(n, int) and n <= 0:
        return
    eng.wait_ge(sem, n)


def wait_alone(eng, sem, n, met, at):
    if isinstance(n, int) and n <= 0:
        return
    if not isinstance(n, int):
        n = eng.to_reg(n)
    eng.wait_ge(met, at)
    eng.wait_ge(sem, n)


def slot_wait(t, u, each):
    return each * (t // RING + 1) if isinstance(t, int) else (t - u) * (each // RING) + each


def tile_of(a, t):
    if isinstance(t, int):
        return a[:, t, :]
    return a[:, bass.ds(t, 1), :].rearrange("p a c -> p (a c)")


def row_of(a, t):
    if isinstance(t, int):
        return a[t]
    return a[bass.ds(t, 1)].rearrange("a p c -> (a p) c")


def staggered(eng, step, steps, lag, unroll, peel=0):
    for k in range(lag):
        step(k, k % unroll)
    with eng.Fori(lag // unroll, (steps - peel) // unroll) as i:
        for v in range(unroll):
            step(i * unroll + v, v)
    for k in range(steps - peel, steps + lag):
        step(k, k % unroll)


def least(n, most):
    return min(n, most) if isinstance(n, int) else n


def exists(t):
    return not isinstance(t, int) or 0 <= t < TILES


class Mem:

    def __init__(self, nc, ctx):
        self.nc, self.ctx = nc, ctx

    def sb(self, name, shape, dt=F32):
        return self.ctx.enter_context(self.nc.sbuf_tensor(name, shape, dt))

    def ps(self, name, shape, dt=F32):
        return self.ctx.enter_context(self.nc.psum_tensor(name, shape, dt))

    def sem(self, name):
        return self.ctx.enter_context(self.nc.semaphore(name))


def attention_phase(nc, io, keep):
    X, XN, XNT, LOG, C = keep["X"], keep["XN"], keep["XNT"], keep["LOG"], keep["C"]
    with ExitStack() as ctx:
        m = Mem(nc, ctx)
        sb, ps, sem = m.sb, m.ps, m.sem
        ctxT = sb("a_ctxT", [P, RING, 2, 2, 2 * SEQ])
        mrow = sb("a_mrow", [P, RING, P])
        mpair = sb("a_mpair", [2, RING, SEQ])
        mneg = sb("a_mneg", [2, RING, SEQ], BF16)
        mhalf = sb("a_mhalf", [P, RING, 2 * P])
        maskT = sb("a_maskT", [P, BATCH])
        mvj = sb("a_mvj", [P, BATCH, 2])
        half = sb("a_half", [P, 2])
        wq = sb("a_wq", [P, P])
        wk = sb("a_wk", [P, 2 * P])
        wv = sb("a_wv", [P, 2 * P])
        wo = sb("a_wo", [P, 2 * P])
        rw = sb("a_rw", [P, E0])
        cols = sb("a_cols", [P, 3])
        rows = sb("a_rows", [P, P + E0])
        ind = sb("a_ind", [2, P], BF16)
        eps = sb("a_eps", [P, 2])
        stat = sb("a_stat", [P, RING, 6])
        stat2 = sb("a_stat2", [P, RING, 6])
        mv = sb("a_mv", [P, RING, 2, 2])
        ve = sb("a_ve", [P, RING, 2])
        rstd = sb("a_rstd", [P, RING, 2])
        xn = sb("a_xn", [P, RING, P])
        xn2 = sb("a_xn2", [P, RING, P])
        xT = sb("a_xT", [P, RING, 2, P])
        qT = sb("a_qT", [P, 2, P])
        kT = sb("a_kT", [P, 2, 2 * P])
        V = sb("a_V", [P, 2, 2, PAIRS, 2, HEAD_DIM + 1])
        top = sb("a_top", [P, 2, HEADS])
        D = sb("a_D", [P, 2, PAIRS, 2, SEQ])
        PR = sb("a_P", [P, 2, PAIRS, 2 * SEQ])
        PT = sb("a_PT", [P, 2, PAIRS, P])
        rin = sb("a_rin", [P, 2, HEADS])
        upd = sb("a_upd", [P, 2, P])
        updT = sb("a_updT", [P, 2, P])
        zero = sb("a_zero", [P, ZEROS])

        turned = ps("a_turned", [P, 4, P])
        qkv = ps("a_qkv", [P, 4, P])
        S = ps("a_S", [P, PAIRS, 512])
        PTp = ps("a_PTp", [P, PAIRS, P])
        O = ps("a_O", [P, 512])
        U = O[:, 0:HEADS * (HEAD_DIM + 1)].rearrange("p (h c) -> p h c", h=HEADS)
        proj = O[:, 256:256 + P]
        lgp = O[:, 400:400 + E0]

        consts_landed = sem("a_consts_landed")
        zeros_out, experts_landed = sem("a_zeros_out"), sem("a_experts_landed")
        setup = sem("a_setup")
        x_landed = [sem(f"a_x_landed{u}") for u in range(RING)]
        c_landed = [sem(f"a_c_landed{u}") for u in range(RING)]
        names = ("stat mv ve rstd xn xTp xT qkv masks halves q k v scores top shifted probs PTp PT pv rin upd updTp "
                 "updT proj xb x1 stat2 mv2 xn2 x2 lgp lg kept keptT").split()
        s = {n: sem("a_" + n) for n in names}
        n_consts = 12
        block = ctx.enter_context(nc.Block())

        @block.sync
        def _(sp):
            for dst, src in ((C, io["consts"]), (wq, io["wqT"]), (wk, io["wkT"]), (wv, io["wvT"]), (wo, io["woT"]),
                             (rw, io["L0_ffn_router_w"])):
                sp.dma_start(dst[:], src).then_inc(consts_landed, 16)
            for j, name in enumerate(("L0_xattn_b_tgt", "b_k", "b_v")):
                sp.dma_start(cols[:, j:j + 1], io[name].rearrange("(p o) -> p o", o=1)).then_inc(consts_landed, 16)
            off = 0
            for name in ("L0_xattn_b_out", "L0_ffn_router_b"):
                n = io[name].shape[0]
                sp.dma_start(rows[:, off:off + n], io[name].partition_broadcast(P)).then_inc(consts_landed, 16)
                off += n
            sp.dma_start(maskT[0:SEQ, :], io["maskT"]).then_inc(consts_landed, 16)
            sp.dma_start(maskT[SEQ:P, :], io["maskT"]).then_inc(consts_landed, 16)

            def step(t, u):
                if not exists(t):
                    return
                at_least(sp, s["stat"], t - RING + 1)
                at_least(sp, s["qkv"], t - RING + 1)
                at_least(sp, s["masks"], t - RING + 1)
                at_least(sp, s["halves"], t - RING + 1)
                at_least(sp, s["q"], t - RING + 1)
                sp.dma_start(tile_of(X, t), row_of(io["x_tiles"], t)).then_inc(x_landed[u], 16)
                sp.dma_start(ctxT[:, u].rearrange("p c b s -> p (c b s)"), row_of(io["ctxT"], t)).then_inc(c_landed[u], 16)
                sp.dma_start(mrow[:, u, :], io["mask_rows"][bass.ds(t, 1)].rearrange("a c -> (a c)")
                             .partition_broadcast(P)).then_inc(c_landed[u], 16)
                sp.dma_start(mpair[:, u, :], row_of(io["mask_pairs"], t)).then_inc(c_landed[u], 16)
            staggered(sp, step, TILES, RING, RING)

        @block.gpsimd
        def _(pool):
            nc.gpsimd.memset(zero[:], 0.0).then_inc(zeros_out, 16)
            nc.gpsimd.memset(V[:], 0.0).then_inc(setup, 1)
            nc.gpsimd.memset(eps[:], -0.5).then_inc(setup, 1)
            nc.gpsimd.memset(half[:], 0.0).then_inc(setup, 1)
            pool.wait_ge(setup, 3)
            for b in range(2):
                for ring in range(2):
                    for j in range(2):
                        nc.gpsimd.memset(V[j * SEQ:(j + 1) * SEQ, ring, b, :, j, HEAD_DIM], 1.0).then_inc(setup, 1)
            for j in range(2):
                nc.gpsimd.memset(half[j * SEQ:(j + 1) * SEQ, j:j + 1], 1.0).then_inc(setup, 1)
            pool.wait_ge(consts_landed, 16 * (n_consts + 1))
            nc.gpsimd.tensor_copy(ind[:], C[0:2, C_IND:C_IND + P]).then_inc(setup, 1)
            pool.wait_ge(setup, 13)
            for j in range(2):
                nc.gpsimd.tensor_scalar(mvj[:, :, j], maskT[:], half[:, j:j + 1], None, ALU.mult).then_inc(setup, 1)
            pool.wait_ge(setup, 15)

            def hold(name, n):
                wait_alone(pool, s[name], n, setup, 15)

            def step(k, v):
                t, u = k, v
                if exists(t):
                    wait_alone(pool, c_landed[u], slot_wait(t, u, 48), setup, 15)
                    hold("scores", t - RING + 1)
                    nc.gpsimd.tensor_scalar(mneg[:, u, :], mpair[:, u, :], 0.0, NEG, ALU.is_equal,
                                            ALU.mult).then_inc(s["masks"], 1)
                    hold("xn", t + 1)
                    nc.gpsimd.tensor_tensor(tile_of(X, t), tile_of(X, t), rows[:, 0:P], ALU.add).then_inc(s["xb"], 1)
                t, u = k - 5, (v - 5) % RING
                if exists(t):
                    hold("xn2", t + 1)
                    nc.gpsimd.tensor_tensor(tile_of(X, t), tile_of(X, t), xn2[:, u, :], ALU.add).then_inc(s["x2"], 1)
                    nc.gpsimd.tensor_copy(tile_of(XN, t), xn2[:, u, :]).then_inc(s["kept"], 1)
                    hold("xT", k)
                    nc.gpsimd.tensor_copy(tile_of(XNT, t), xT[:, u, 1, :]).then_inc(s["keptT"], 1)
                lo, hi = 0 if exists(k + 1) else 1, 2 if exists(k - 3) else 1
                if lo < hi:
                    hold("mv", least(k + 2, TILES))
                    hold("mv2", least(k - 2, TILES))
                    nc.gpsimd.tensor_scalar(ve[:, v, lo:hi], mv[:, v, lo:hi, 1], LN_EPS, None,
                                            ALU.add).then_inc(s["ve"], 1)
                    hold("ve", k + 2)
                    nc.gpsimd.tensor_tensor(rstd[:, v, lo:hi], ve[:, v, lo:hi], eps[:, lo:hi],
                                            ALU.pow).then_inc(s["rstd"], 1)
            hold("mv", 1)
            nc.gpsimd.tensor_scalar(ve[:, RING - 1, 0:1], mv[:, RING - 1, 0, 1:2], LN_EPS, None,
                                    ALU.add).then_inc(s["ve"], 1)
            hold("ve", 1)
            nc.gpsimd.tensor_tensor(rstd[:, RING - 1, 0:1], ve[:, RING - 1, 0:1], eps[:, 0:1],
                                    ALU.pow).then_inc(s["rstd"], 1)
            staggered(pool, step, TILES, 2 * RING, RING, peel=RING)

        @block.vector
        def _(dve):
            def gather_stats(t, u, st, name):
                nc.vector.bn_stats(st[:, u, :], tile_of(X, t)).then_inc(s[name], 1)

            def mean_and_variance(t, u, which, at, st, name, after):
                wait_alone(dve, s[name], t + 1, setup, 15)
                nc.vector.bn_aggr(mv[:, at, which, :], st[:, u, :]).then_inc(s[after], 1)

            def first_stats(t, u):
                if exists(t):
                    wait_alone(dve, x_landed[u], slot_wait(t, u, 16), setup, 15)
                    gather_stats(t, u, stat, "stat")

            def first_mean(t, u):
                if exists(t):
                    mean_and_variance(t, u, 0, (u - 1) % RING, stat, "stat", "mv")

            dve.wait_ge(setup, 15)
            dve.wait_ge(consts_landed, 16 * (n_consts + 1))
            first_stats(0, 0)
            first_mean(0, 0)

            def step(k, v):
                w = (v - 1) % RING
                if exists(k) or exists(k - 4):
                    dve.wait_ge(s["rstd"], k + 1)
                    at_least(dve, s["xTp"], k - RING + 1)
                if exists(k):
                    nc.vector.tensor_scalar(xn[:, v, :], tile_of(X, k), mv[:, w, 0, 0:1], rstd[:, w, 0:1],
                                            ALU.subtract, ALU.mult).then_inc(s["xn"], 1)
                t, u = k - 4, v
                if exists(t):
                    at_least(dve, s["kept"], t - RING + 1)
                    at_least(dve, s["x2"], t - RING + 1)
                    nc.vector.tensor_scalar(xn2[:, u, :], tile_of(X, t), mv[:, w, 1, 0:1], rstd[:, w, 1:2],
                                            ALU.subtract, ALU.mult).then_inc(s["xn2"], 1)
                t, w = k - 1, (v - 1) % 2
                Sv = S[:, :, 0:2 * SEQ].rearrange("p g (j s) -> p g j s", j=2)
                tops = top[:, w, :].rearrange("p (g j) -> p g j", j=2)
                if exists(t):
                    dve.wait_ge(s["scores"], t + 1)
                    nc.vector.tensor_reduce(tops, Sv, AX.X, ALU.max).then_inc(s["top"], 1)
                if exists(k - 2):
                    dve.wait_ge(s["pv"], k - 1)
                    nc.vector.reciprocal(rin[:, v % 2, :], U[:, :, HEAD_DIM]).then_inc(s["rin"], 1)
                if exists(t):
                    dve.wait_ge(s["top"], t + 1)
                    at_least(dve, s["probs"], t - 1)
                    nc.vector.tensor_tensor(D[:, w], Sv, tops.unsqueeze(3).broadcast_to([P, PAIRS, 2, SEQ]),
                                            ALU.subtract).then_inc(s["shifted"], 1)
                t, u = k - 3, (v - 3) % RING
                if exists(t):
                    dve.wait_ge(s["xb"], t + 1)
                    dve.wait_ge(s["proj"], t + 1)
                    nc.vector.tensor_tensor(tile_of(X, t), tile_of(X, t), proj, ALU.add).then_inc(s["x1"], 1)
                t, w = k - 2, v % 2
                if exists(t):
                    dve.wait_ge(s["rin"], t + 1)
                    at_least(dve, s["updTp"], t - 1)
                    nc.vector.tensor_tensor(upd[:, w, :].rearrange("p (h d) -> p h d", h=HEADS), U[:, :, 0:HEAD_DIM],
                                            rin[:, w, :].unsqueeze(2).broadcast_to([P, HEADS, HEAD_DIM]),
                                            ALU.mult).then_inc(s["upd"], 1)
                first_stats(k + 1, (v + 1) % RING)
                t, u = k - 3, (v - 3) % RING
                if exists(t):
                    wait_alone(dve, s["x1"], t + 1, setup, 15)
                    gather_stats(t, u, stat2, "stat2")
                first_mean(k + 1, (v + 1) % RING)
                if exists(k - 5):
                    dve.wait_ge(s["lgp"], k - 4)
                    nc.vector.tensor_tensor(tile_of(LOG, k - 5), lgp, rows[:, P:P + E0],
                                            ALU.add).then_inc(s["lg"], 1)
                if exists(t):
                    mean_and_variance(t, u, 1, v, stat2, "stat2", "mv2")
                t, u, w = k, v, v % 2
                if exists(t):
                    dve.wait_ge(s["qkv"], t + 1)
                    dve.wait_ge(s["halves"], t + 1)
                    nc.vector.scalar_tensor_tensor(qT[:, w, :], qkv[:, 0, :], cols[:, 0:1], mrow[:, u, :],
                                                   ALU.add, ALU.mult).then_inc(s["q"], 1)
                    nc.vector.scalar_tensor_tensor(kT[:, w, :].rearrange("p (j c) -> p j c", j=2),
                                                   qkv[:, 1, :].unsqueeze(1).broadcast_to([P, 2, P]),
                                                   cols[:, 1:2], mhalf[:, u, :].rearrange("p (j c) -> p j c", j=2),
                                                   ALU.add, ALU.mult).then_inc(s["k"], 1)
                    at_least(dve, s["pv"], t - 1)
                    for b in range(2):
                        nc.vector.tensor_tensor(
                            V[:, w, b, :, :, 0:HEAD_DIM],
                            qkv[:, 2 + b, :].rearrange("p (g j d) -> p g j d", g=PAIRS, j=2),
                            mvj[:, bass.ds(2 * t + b, 1), :].unsqueeze(3).broadcast_to([P, 1, 2, HEAD_DIM])
                            .broadcast_to([P, PAIRS, 2, HEAD_DIM]),
                            ALU.mult).then_inc(s["v"], 1)
            staggered(dve, step, TILES, 2 * RING, RING, peel=RING)

        @block.tensor
        def _(pe):
            ident = C[:, C_ID:C_ID + P]
            pe.wait_ge(consts_landed, 16 * (n_consts + 1))
            pe.wait_ge(setup, 15)

            def step(k, v):
                t, u = k, v
                if exists(t):
                    pe.wait_ge(s["xn"], t + 1)
                at_least(pe, s["updT"], least(k - 2, TILES))
                if exists(k - 4):
                    pe.wait_ge(s["xn2"], k - 3)
                    mm = nc.tensor.transpose(turned[:, 1, :], xn2[:, u, :], ident)
                if exists(t):
                    mm = nc.tensor.transpose(turned[:, 0, :], xn[:, u, :], ident)
                if exists(k - 4) or exists(t):
                    mm.then_inc(s["xTp"], 1)
                if exists(t):
                    pe.wait_ge(c_landed[u], 48 * (t // RING + 1) if isinstance(t, int) else (t - u) * 12 + 48)
                    at_least(pe, s["q"], t)
                    at_least(pe, s["k"], t)
                    at_least(pe, s["v"], 2 * t)
                    for c in range(2):
                        nc.tensor.matmul(qkv[:, 1, :], wk[:, c * P:(c + 1) * P], ctxT[:, u, c, :, 0:SEQ],
                                         start=c == 0, stop=c == 1)
                    for b in range(2):
                        for c in range(2):
                            nc.tensor.matmul(qkv[:, 2 + b, :], ctxT[:, u, c, b, :], wv[:, c * P:(c + 1) * P], start=c == 0, stop=c == 1)
                    pe.wait_ge(s["xT"], t + 1)
                    nc.tensor.matmul(qkv[:, 0, :], wq[:], xT[:, u, 0, :], start=True, stop=True).then_inc(s["qkv"], 1)
                t, w = k - 1, (v - 1) % 2
                if exists(t):
                    pe.wait_ge(s["probs"], t + 1)
                    at_least(pe, s["PT"], t)
                    for g in range(PAIRS):
                        mm = nc.tensor.transpose(PTp[:, g, :], PR[:, w, g, :], ident)
                    mm.then_inc(s["PTp"], 1)
                if exists(k) or exists(k - 4):
                    pe.wait_ge(s["xT"], k + 1)
                at_least(pe, s["upd"], least(k - 1, TILES))
                at_least(pe, s["x1"], least(k - 2, TILES))
                at_least(pe, s["lg"], least(k - 4, TILES))
                if exists(k - 4):
                    nc.tensor.matmul(lgp, xT[:, v, 1, :], rw[:], start=True, stop=True).then_inc(s["lgp"], 1)
                t, u, w = k - 2, (v - 2) % RING, (v - 2) % 2
                if exists(t):
                    nc.tensor.transpose(turned[:, 2, :], upd[:, w, :], ident).then_inc(s["updTp"], 1)
                    nc.tensor.matmul(proj, xT[:, u, 0, :], wo[:, 0:P], start=True, stop=False)
                t, u, w = k, v, v % 2
                if exists(t):
                    pe.wait_ge(s["masks"], t + 1)
                    at_least(pe, s["shifted"], t)
                    for g in range(PAIRS):
                        nc.tensor.matmul(S[:, g, 0:2 * SEQ], ind[:], mneg[:, u, :].unsqueeze(1)
                                         .broadcast_to([2, 2, SEQ]), start=True, stop=True)
                    pe.wait_ge(s["q"], t + 1)
                    pe.wait_ge(s["k"], t + 1)
                    for g in range(PAIRS):
                        r = slice(32 * g, 32 * g + 32)
                        for b in range(2):
                            keys = kT[r, w, :].rearrange("p (j b s) -> p j b s", j=2, b=2)[:, :, b, :]
                            mm = nc.tensor.matmul(S[b * SEQ:(b + 1) * SEQ, g, 0:2 * SEQ],
                                                  qT[r, w, b * SEQ:(b + 1) * SEQ], keys, start=False, stop=True,
                                                  skip_group_check=True)
                    mm.then_inc(s["scores"], 1)
                t, w = k - 2, (v - 2) % 2
                if exists(t):
                    pe.wait_ge(s["updT"], t + 1)
                    nc.tensor.matmul(proj, updT[:, w, :], wo[:, P:2 * P], start=False,
                                     stop=True).then_inc(s["proj"], 1)
                t, w = k - 1, (v - 1) % 2
                if exists(t):
                    pe.wait_ge(s["PT"], t + 1)
                    pe.wait_ge(s["v"], 2 * t + 2)
                    for b in range(2):
                        for g in range(PAIRS):
                            mm = nc.tensor.matmul(O[b * SEQ:(b + 1) * SEQ, g * 34:(g + 1) * 34],
                                                  PT[:, w, g, b * SEQ:(b + 1) * SEQ],
                                                  V[:, w, b, g, :, :], start=True, stop=True)
                    mm.then_inc(s["pv"], 1)
            staggered(pe, step, TILES, 2 * RING, RING)

        @block.scalar
        def _(act):
            act.wait_ge(consts_landed, 16 * (n_consts + 1))

            zeroed = list(io["zeroed"])

            def step(k, v):
                if isinstance(k, int) and 1 <= k < 2 * RING:
                    act.wait_ge(zeros_out, 16)
                    for dst in zeroed[3 * (k - 1):3 * k]:
                        act.dma_start(dst, zero[:, 0:dst.shape[1]]).then_inc(zeros_out, 16)
                if isinstance(k, int) and k == 2 * RING - 1:
                    for e in range(E0):
                        act.dma_start(keep["WE"][:, e, :], io["expert_w"][e]).then_inc(experts_landed, 16)
                lo, hi = 0 if exists(k) else 1, 2 if exists(k - 4) else 1
                if lo < hi:
                    act.wait_ge(s["xTp"], k + 1)
                    at_least(act, s["keptT"], least(k - 7, TILES))
                    at_least(act, s["lgp"], least(k - 7, TILES))
                    at_least(act, s["proj"], least(k - 3, TILES))
                    nc.scalar.copy(xT[:, v, lo:hi, :], turned[:, lo:hi, :]).then_inc(s["xT"], 1)
                t, w = k - 1, (v - 1) % 2
                if exists(t):
                    act.wait_ge(s["shifted"], t + 1)
                    at_least(act, s["PTp"], t - 1)
                    nc.scalar.activation(PR[:, w].rearrange("p g c -> p (g c)"),
                                         D[:, w].rearrange("p g j c -> p (g j c)"), ACT.Exp,
                                         scale=SCALE).then_inc(s["probs"], 1)
                if exists(k):
                    act.wait_ge(c_landed[v], slot_wait(k, v, 48))
                    at_least(act, s["k"], k - RING + 1)
                    for j in range(2):
                        a = nc.scalar.activation(mhalf[:, v, j * P:(j + 1) * P], mrow[:, v, :], ACT.Copy,
                                                 scale=C[:, C_HALF + j:C_HALF + j + 1])
                    a.then_inc(s["halves"], 1)
                if exists(t):
                    act.wait_ge(s["PTp"], t + 1)
                    at_least(act, s["pv"], t - 1)
                    nc.scalar.copy(PT[:, w], PTp[:]).then_inc(s["PT"], 1)
                t, w = k - 2, (v - 2) % 2
                if exists(t):
                    act.wait_ge(s["updTp"], t + 1)
                    at_least(act, s["proj"], t - 1)
                    nc.scalar.activation(updT[:, w, :], turned[:, 2, :], ACT.Identity,
                                         bias=cols[:, 2:3]).then_inc(s["updT"], 1)
            staggered(act, step, TILES, 2 * RING, RING)
            act.wait_ge(zeros_out, 16 + 16 * len(io["zeroed"]))
            act.wait_ge(experts_landed, 16 * E0)


def route(nc, dve, link, LOG, C, w, rank_ps, total_ps, pe_needs, pe_done, act_needs, act_done):
    TE = [P, TILES, E0]

    def over_e(a):
        return a.unsqueeze(2).broadcast_to(TE)

    iota = C[:, C_IOTA:C_IOTA + E0].unsqueeze(1).broadcast_to(TE)
    rest = LOG
    for n in range(2):
        top, hot = w["top"][:, n, :], w["hot"][:, n]
        link(nc.vector.tensor_reduce(top, rest[:], AX.X, ALU.max))
        link(nc.vector.tensor_tensor(w["a"][:], rest[:], over_e(top), ALU.is_equal))
        link(nc.vector.scalar_tensor_tensor(w["b"][:], w["a"][:], -float(E0), iota, ALU.mult, ALU.add))
        link(nc.vector.tensor_reduce(w["t"][:], w["b"][:], AX.X, ALU.min))
        link(nc.vector.tensor_tensor(hot, w["b"][:], over_e(w["t"][:]), ALU.is_equal))
        if n == 0:
            link(nc.vector.scalar_tensor_tensor(w["rest"][:], hot, NEG, LOG[:], ALU.mult, ALU.add))
            rest = w["rest"]
    link(nc.vector.tensor_tensor(w["a"][:], LOG[:], over_e(w["top"][:, 0, :]), ALU.subtract))
    link(nc.vector.tensor_tensor(w["t"][:], w["top"][:, 1, :], w["top"][:, 0, :], ALU.subtract), act_needs)
    link(nc.vector.tensor_tensor(w["chosen"][:], w["hot"][:, 0], w["hot"][:, 1], ALU.add), pe_needs)
    dve.wait_ge(act_done, 1)
    dve.wait_ge(pe_done, 1)
    link(nc.vector.tensor_tensor_scan(w["upto"][:], C[:, C_KEEP:C_KEEP + TILES * E0], total_ps[:], 0.0,
                                      ALU.mult, ALU.add))
    link(nc.vector.tensor_tensor(w["rank"][:], w["upto"][:], total_ps[:], ALU.subtract))
    link(nc.vector.tensor_tensor(w["rank"][:], w["rank"][:], rank_ps[:], ALU.add))
    rank = w["rank"][:].rearrange("p (e t) -> p e t", e=E0)
    count = w["upto"][:].rearrange("p (e t) -> p e t", e=E0)[:, :, TILES - 1]
    full = TOKENS // BLOCK
    link(nc.vector.tensor_scalar(w["steps"][:], C[:, C_IOTA:C_IOTA + full], float(BLOCK), None, ALU.mult))
    link(nc.vector.tensor_tensor(w["over"][:], count.unsqueeze(2).broadcast_to([P, E0, full]),
                                 w["steps"][:].unsqueeze(1).broadcast_to([P, E0, full]), ALU.is_gt))
    link(nc.vector.tensor_reduce(w["blocks"][:], w["over"][:], AX.X, ALU.add))
    link(nc.vector.tensor_tensor_scan(w["last"][:], C[:, C_ONES:C_ONES + E0], w["blocks"][:], 0.0,
                                      ALU.mult, ALU.add))
    link(nc.vector.tensor_tensor(w["first"][:], w["last"][:], w["blocks"][:], ALU.subtract))
    link(nc.vector.tensor_scalar(w["base"][:], w["first"][:], float(BLOCK), None, ALU.mult))
    link(nc.vector.tensor_tensor(rank, rank, w["base"][:].unsqueeze(2).broadcast_to([P, E0, TILES]), ALU.add))
    for n in range(2):
        link(nc.vector.tensor_tensor(w["a"][:], w["hot"][:, n], rank.rearrange("p e t -> p t e"), ALU.mult))
        slot = w["slot_f"][:, n, :]
        link(nc.vector.tensor_reduce(slot, w["a"][:], AX.X, ALU.add))
    return nc.vector.tensor_copy(w["slot"][:].rearrange("p t n -> p n t"), w["slot_f"][:])


def route_weights(nc, link, C, w):
    link(nc.vector.tensor_reduce(w["sum"][:], w["b"][:], AX.X, ALU.add))
    link(nc.vector.reciprocal(w["w"][:, 0, :], w["sum"][:]))
    link(nc.vector.tensor_tensor(w["w"][:, 1, :], w["exp2"][:], w["w"][:, 0, :], ALU.mult))
    one = [1, BLOCKS, E0]
    link(nc.vector.tensor_tensor(w["owns"][:], w["first"][0:1, :].unsqueeze(1).broadcast_to(one),
                                 C[0:1, C_IOTA:C_IOTA + BLOCKS].unsqueeze(2).broadcast_to(one), ALU.is_le))
    link(nc.vector.tensor_reduce(w["owner_f"][:], w["owns"][:], AX.X, ALU.add))
    link(nc.vector.tensor_scalar(w["owner"][:], w["owner_f"][:], -1.0, None, ALU.add))


def route_buffers(m, keep, tag):
    sb = m.sb
    w = {n: sb(tag + n, [P, TILES, E0]) for n in ("a", "b", "rest")}
    w.update({n: sb(tag + n, [P, E0 * TILES]) for n in ("upto", "rank")})
    w.update({n: sb(tag + n, [P, TILES]) for n in ("t", "sum", "exp2")})
    w.update({n: sb(tag + n, [P, E0]) for n in ("blocks", "last", "first", "base")})
    w.update(hot=sb(tag + "hot", [P, 2, TILES, E0]), chosen=sb(tag + "chosen", [P, TILES, E0], BF16),
             top=sb(tag + "top", [P, 2, TILES]), slot_f=sb(tag + "slot_f", [P, 2, TILES]),
             steps=sb(tag + "steps", [P, TOKENS // BLOCK]), over=sb(tag + "over", [P, E0, TOKENS // BLOCK]),
             owns=sb(tag + "owns", [1, BLOCKS, E0]), owner_f=sb(tag + "owner_f", [1, BLOCKS]),
             owner=keep["OWNER"], w=keep["W"], slot=keep["SLOT"],
             before=sb(tag + "before", [P, P], BF16), ones=sb(tag + "ones", [P, P], BF16))
    return w


def route_exps(nc, act, w, needs, done):
    act.wait_ge(needs, 1)
    nc.scalar.activation(w["b"][:], w["a"][:], ACT.Exp)
    nc.scalar.activation(w["exp2"][:], w["t"][:], ACT.Exp).then_inc(done, 1)


def route_counts(nc, pe, w, rank_ps, total_ps, tables, needs, done):
    pe.wait_ge(tables, 2)
    pe.wait_ge(needs, 1)
    chosen = w["chosen"][:].rearrange("p t e -> p e t")
    nc.tensor.matmul(rank_ps[:], w["before"][:], chosen, start=True, stop=True)
    nc.tensor.matmul(total_ps[:], w["ones"][:], chosen, start=True, stop=True).then_inc(done, 1)


GROUP = 4
GROUPS = TILES // GROUP


def group_wait(g, v, each):
    return each * (g // 2 + 1) if isinstance(g, int) else (g - v) * (each // 2) + each


def copy_group(nc, dve, keep, rows, index, g, v, copied, sent):
    if not isinstance(g, int) or g >= 2:
        dve.wait_ge(sent[v], group_wait(g - 2, v, 32 * GROUP) if isinstance(g, int) else (g - v) * 16 * GROUP)
    xn = tile_of(keep["XN"][:].rearrange("p (g t) c -> p g (t c)", t=GROUP), g).rearrange("p (t c) -> p t c", t=GROUP)
    nc.vector.tensor_copy(rows[:, v, :, :, 0:H], xn.unsqueeze(2).broadcast_to([P, GROUP, CHOICES, H])
                          ).then_inc(copied, 1)
    places = keep["C"][:, C_PLACE:].rearrange("p (g n) -> p g n", g=GROUPS)
    nc.vector.tensor_copy(rows[:, v, :, :, H].rearrange("p t n -> p (t n)"), tile_of(places, g)).then_inc(copied, 1)
    nc.vector.tensor_copy(index[:, v], tile_of(keep["SLOT"][:].rearrange("p (g t) n -> p g (t n)", t=GROUP), g)
                          ).then_inc(copied, 1)


def scatter_rows(nc, pool, rows, index, copied, sent, dst, most):
    def step(g, v):
        wait_alone(pool, copied, 3 * g + 3, copied, 3)
        for t in range(GROUP):
            for n in range(2):
                slot = index[:, v, 2 * t + n:2 * t + n + 1]
                nc.gpsimd.indirect_dma_start(dst, bass.IndirectOffsetOnAxis(ap=slot, axis=0),
                                             rows[:, v, t, n, :], None, bounds_check=most - 1,
                                             oob_is_err=False).then_inc(sent[v], 16)
    with pool.Fori(0, GROUPS // 2) as i:
        step(2 * i, 0)
        step(2 * i + 1, 1)
    for v in range(2):
        pool.wait_ge(sent[v], 16 * GROUP * GROUPS)


def shared_phase(nc, io, keep):
    X, XNT, C = keep["X"], keep["XNT"], keep["C"]
    SUB = WIDE // P
    assert WIDE == GROUP * P
    with ExitStack() as ctx:
        m = Mem(nc, ctx)
        sb, ps, sem = m.sb, m.ps, m.sem
        w = route_buffers(m, keep, "b_")
        rows, index = sb("b_rows", [P, 2, GROUP, CHOICES, ROW]), sb("b_index", [P, 2, 2 * GROUP], U32)

        WS = sb("b_W", [P, W_COLS])
        up, upb = WS[:, W_UP:W_UP + F0], WS[:, W_UPB:W_UPB + CHUNKS0]
        down = WS[:, W_DOWN:W_DOWN + F0].rearrange("p (c h) -> p c h", c=CHUNKS0)
        G = sb("b_G", [P, 2, CHUNKS0, WIDE])
        lens_i, lens = sb("b_lens_i", [P, PATCHES], I32), sb("b_lens", [P, PATCHES])
        ends, neg, mark = sb("b_ends", [P, PATCHES]), sb("b_neg", [P, PATCHES]), sb("b_mark", [P, SEQ])
        plug = sb("b_plug", [P, SEQ])
        hits = G[:].rearrange("p v c w -> p (v c w)")[:, 0:SEQ * PATCHES].rearrange("p (a b) -> p a b", a=SEQ)
        hid = ps("b_hid", [P, CHUNKS0, WIDE])
        y = ps("b_y", [P, 2, WIDE])
        rank_ps, total_ps = ps("b_rank_ps", [P, WIDE]), ps("b_total_ps", [P, WIDE])
        s = {n: sem("b_" + n) for n in ("landed chain exps_wanted exps counts_wanted counts tables slots hid gelu y "
                                        "biased added plugged copied").split()}
        sent = [sem(f"b_sent{v}") for v in range(2)]
        block = ctx.enter_context(nc.Block())

        @block.sync
        def _(sp):
            sp.dma_start(WS[:], io["shared_w"]).then_inc(s["landed"], 16)
            sp.dma_start(lens_i[:], io["mask_BxS2_if0"]).then_inc(s["landed"], 16)
            sp.wait_ge(s["plugged"], 1)
            sp.dma_start(io["plug"], plug[:]).then_inc(s["landed"], 16)
            sp.wait_ge(s["landed"], 48)

        @block.gpsimd
        def _(pool):
            nc.gpsimd.tensor_copy(w["before"][:], C[:, C_BEFORE:C_BEFORE + P]).then_inc(s["tables"], 1)
            nc.gpsimd.tensor_copy(w["ones"][:], C[:, C_ONES:C_ONES + P]).then_inc(s["tables"], 1)
            scatter_rows(nc, pool, rows, index, s["copied"], sent, io["xg0"], SLOTS)

        @block.scalar
        def _(act):
            route_exps(nc, act, w, s["exps_wanted"], s["exps"])
            act.wait_ge(s["landed"], 32)

            def step(k, v):
                for c in range(CHUNKS0):
                    act.wait_ge(s["hid"], CHUNKS0 * k + c + 1)
                    if c == 0:
                        at_least(act, s["y"], k - 1)
                    nc.scalar.activation(G[:, v, c, :], hid[:, c, :], ACT.Gelu,
                                         bias=upb[:, c:c + 1]).then_inc(s["gelu"], 1)
            step(0, 0)
            step(1, 1)
            with act.Fori(1, GROUPS // 2) as i:
                step(2 * i, 0)
                step(2 * i + 1, 1)

        @block.tensor
        def _(pe):
            pe.wait_ge(s["landed"], 32)
            xt = XNT[:].rearrange("p (g t) c -> p g (t c)", g=GROUPS)

            def step(k, v):
                if not isinstance(k, int) or k < GROUPS:
                    for c in range(CHUNKS0):
                        at_least(pe, s["gelu"], CHUNKS0 * (k - 1) + c + 1)
                        nc.tensor.matmul(hid[:, c, :], up[:, c * P:(c + 1) * P], tile_of(xt, k), start=True,
                                         stop=True).then_inc(s["hid"], 1)
                k, v = k - 1, (v - 1) % 2
                if not isinstance(k, int) or k >= 0:
                    pe.wait_ge(s["gelu"], CHUNKS0 * (k + 1))
                    at_least(pe, s["added"], k - 1)
                    for t in range(SUB):
                        for c in range(CHUNKS0):
                            mm = nc.tensor.matmul(y[:, v, t * P:(t + 1) * P], G[:, v, c, t * P:(t + 1) * P],
                                                  down[:, c, :], start=c == 0, stop=c == CHUNKS0 - 1)
                    mm.then_inc(s["y"], 1)
            step(0, 0)
            route_counts(nc, pe, w, rank_ps, total_ps, s["tables"], s["counts_wanted"], s["counts"])
            step(1, 1)
            with pe.Fori(1, GROUPS // 2) as i:
                step(2 * i, 0)
                step(2 * i + 1, 1)
            step(GROUPS, 0)

        @block.vector
        def _(dve):
            count = [0]

            def link(ins, also=None):
                count[0] += 1
                ins.then_inc(s["chain"], 1)
                dve.wait_ge(s["chain"], count[0])
                if also is not None:
                    dve.sem_inc(also, 1)

            route(nc, dve, link, keep["LOG"], C, w, rank_ps, total_ps, s["counts_wanted"], s["counts"],
                  s["exps_wanted"], s["exps"]).then_inc(s["slots"], 1)
            dve.wait_ge(s["slots"], 1)
            for g in range(2):
                copy_group(nc, dve, keep, rows, index, g, g, s["copied"], sent)
            route_weights(nc, link, C, w)
            xv = X[:].rearrange("p (g t) c -> p g (t c)", g=GROUPS)

            dve.wait_ge(s["landed"], 32)

            def step(k, v, more):
                bias = WS[:, W_DNB:W_DNB + H].unsqueeze(1).broadcast_to([P, SUB, H])
                x4 = tile_of(xv, k)
                nc.vector.tensor_tensor(x4.rearrange("p (t c) -> p t c", t=SUB), x4.rearrange("p (t c) -> p t c", t=SUB),
                                        bias, ALU.add).then_inc(s["biased"], 1)
                dve.wait_ge(s["biased"], k + 1)
                dve.wait_ge(s["y"], k + 1)
                nc.vector.tensor_tensor(x4, x4, y[:, v, :], ALU.add).then_inc(s["added"], 1)
                if more:
                    copy_group(nc, dve, keep, rows, index, k + 2, v, s["copied"], sent)
            with dve.Fori(0, GROUPS // 2 - 1) as i:
                step(2 * i, 0, True)
                step(2 * i + 1, 1, True)
            step(GROUPS - 2, 0, False)
            step(GROUPS - 1, 1, False)
            dve.wait_ge(s["landed"], 32)
            link(nc.vector.tensor_copy(lens[:], lens_i[:]))
            ones = C[:, C_ONES:C_ONES + PATCHES]
            link(nc.vector.tensor_tensor_scan(ends[:], ones, lens[:], 0.0, ALU.mult, ALU.add))
            link(nc.vector.tensor_scalar(ends[:], ends[:], -1.0, None, ALU.add))
            link(nc.vector.tensor_scalar(neg[:], ends[:], 0.0, float(SEQ), ALU.is_lt, ALU.mult))
            link(nc.vector.tensor_tensor(ends[:], ends[:], neg[:], ALU.add))
            box = [P, SEQ, PATCHES]
            link(nc.vector.tensor_tensor(hits, ends[:].unsqueeze(1).broadcast_to(box),
                                         C[:, C_IOTA:C_IOTA + SEQ].unsqueeze(2).broadcast_to(box), ALU.is_equal))
            link(nc.vector.tensor_reduce(mark[:], hits, AX.X, ALU.max))
            link(nc.vector.tensor_tensor_scan(plug[:], ones, mark[:], 0.0, ALU.mult, ALU.add))
            link(nc.vector.tensor_scalar(plug[:], plug[:], -1.0, 0.0, ALU.add, ALU.max))
            nc.vector.tensor_scalar(plug[:], plug[:], float(PATCHES - 1), C[:, C_ROW:C_ROW + 1], ALU.min,
                                    ALU.add).then_inc(s["plugged"], 1)


def places_of(nc, rows, place):
    return nc.vector.tensor_scalar(place, rows[:, :, H], float(OUT_OF_RANGE), None, ALU.add)


def scatter_results(nc, pool, Y, place, dst, done):
    for n in range(Y.shape[1]):
        nc.gpsimd.indirect_dma_start(dst, bass.IndirectOffsetOnAxis(ap=place[:, n:n + 1], axis=0), Y[:, n, :], None,
                                     bounds_check=CHOICES * TOKENS - 1, oob_is_err=False).then_inc(done, 16)


def experts_phase(nc, io, keep):
    C, OWNER = keep["C"], keep["OWNER"]
    SUB = BLOCK // P
    with ExitStack() as ctx:
        m = Mem(nc, ctx)
        sb, ps, sem = m.sb, m.ps, m.sem
        WE = keep["WE"]
        W = sb("e_w", [P, RING, W_COLS])
        rows, place = sb("e_rows", [P, RING, SUB, ROW]), sb("e_place", [P, RING, SUB], U32)
        xT = sb("e_xT", [P, 2, BLOCK])
        G = sb("e_G", [P, 2, CHUNKS0, BLOCK])
        Y = sb("e_Y", [P, RING, SUB, P])
        xTp = ps("e_xTp", [P, 2, 512])
        hid = ps("e_hid", [P, 2, CHUNKS0, BLOCK])
        yp = ps("e_yp", [P, 2, 512])
        s = {n: sem("e_" + n) for n in "w xTp xT place hid gelu yp y".split()}
        landed = [sem(f"e_landed{u}") for u in range(RING)]
        stored = [sem(f"e_stored{u}") for u in range(RING)]
        src = io["xg0"].rearrange("(k n p) c -> k p n c", p=P, n=SUB)
        block = ctx.enter_context(nc.Block())

        def blk(a, k):
            return a[k] if isinstance(k, int) else a[bass.ds(k, 1)].rearrange("a p n c -> (a p) n c")

        def real(k):
            return not isinstance(k, int) or 0 <= k < BLOCKS

        @block.sync
        def _(sp):
            def step(k, v):
                if real(k):
                    at_least(sp, s["xTp"], k - RING + 1)
                    at_least(sp, s["place"], k - RING + 1)
                    sp.dma_start(rows[:, v], blk(src, k)).then_inc(landed[v], 16)
            staggered(sp, step, BLOCKS, RING, RING)

        @block.gpsimd
        def _(pool):
            pool.wait_ge(s["y"], 1)

            def step(k, v):
                if real(k):
                    wait_alone(pool, s["y"], k + 1, s["y"], 1)
                    scatter_results(nc, pool, Y[:, v], place[:, v], io["results0"], stored[v])
            staggered(pool, step, BLOCKS, RING, RING)
            for u in range(RING):
                pool.wait_ge(stored[u], 16 * SUB * (BLOCKS // RING))

        @block.tensor
        def _(pe):
            ident = C[:, C_ID:C_ID + P]

            def step(k, v):
                if real(k):
                    pe.wait_ge(landed[v], 16 * (k // RING + 1) if isinstance(k, int) else (k - v) * 4 + 16)
                    at_least(pe, s["xT"], k - 1)
                    for n in range(SUB):
                        mm = nc.tensor.transpose(xTp[:, v % 2, n * P:(n + 1) * P], rows[:, v, n, 0:H], ident)
                    mm.then_inc(s["xTp"], 1)
                k, v = k - 1, (v - 1) % RING
                if real(k):
                    pe.wait_ge(s["w"], k + 1)
                    pe.wait_ge(s["xT"], k + 1)
                    at_least(pe, s["gelu"], 2 * k - 2)
                    for c in range(CHUNKS0):
                        mm = nc.tensor.matmul(hid[:, v % 2, c, :], W[:, v, W_UP + c * P:W_UP + (c + 1) * P], xT[:, v % 2, :],
                                              start=True, stop=True)
                        if c % 2 == 1:
                            mm.then_inc(s["hid"], 1)
                k, v = k - 1, (v - 1) % RING
                if real(k):
                    pe.wait_ge(s["gelu"], 2 * k + 2)
                    at_least(pe, s["y"], k - 1)
                    for n in range(SUB):
                        for c in range(CHUNKS0):
                            mm = nc.tensor.matmul(yp[:, v % 2, n * P:(n + 1) * P], G[:, v % 2, c, n * P:(n + 1) * P],
                                                  W[:, v, W_DOWN + c * P:W_DOWN + (c + 1) * P], start=c == 0,
                                                  stop=c == CHUNKS0 - 1)
                    mm.then_inc(s["yp"], 1)
            staggered(pe, step, BLOCKS, RING, RING)

        @block.scalar
        def _(act):
            def step(k, v):
                if not real(k):
                    return
                at_least(act, s["yp"], k - 1)
                for c in range(CHUNKS0):
                    if c % 2 == 0:
                        act.wait_ge(s["hid"], 2 * k + c // 2 + 1)
                    a = nc.scalar.activation(G[:, v % 2, c, :], hid[:, v % 2, c, :], ACT.Gelu,
                                             bias=W[:, v, W_UPB + c:W_UPB + c + 1])
                    if c % 2 == 1:
                        a.then_inc(s["gelu"], 1)
            staggered(act, step, BLOCKS, RING, RING)

        @block.vector
        def _(dve):
            def step(k, v):
                if real(k):
                    dve.wait_ge(s["xTp"], k + 1)
                    at_least(dve, s["hid"], 2 * k - 2)
                    nc.vector.tensor_copy(xT[:, v % 2, :], xTp[:, v % 2, 0:BLOCK]).then_inc(s["xT"], 1)
                    at_least(dve, s["y"], k - RING + 1)
                    if not isinstance(k, int) or k >= RING:
                        dve.wait_ge(stored[v], 16 * SUB * (k // RING) if isinstance(k, int) else (k - v) * 4 * SUB)
                    places_of(nc, rows[:, v], place[:, v]).then_inc(s["place"], 1)
                    e = dve.value_load(OWNER[0:1, bass.ds(k, 1)], min_val=0, max_val=E0 - 1)
                    nc.vector.tensor_copy(W[:, v, :], tile_of(WE, e)).then_inc(s["w"], 1)
                k, v = k - 2, (v - 2) % RING
                if real(k):
                    dve.wait_ge(s["yp"], k + 1)
                    nc.vector.tensor_tensor(Y[:, v], yp[:, v % 2, 0:BLOCK].rearrange("p (n c) -> p n c", n=SUB),
                                            W[:, v, W_DNB:W_DNB + H].unsqueeze(1).broadcast_to([P, SUB, H]),
                                            ALU.add).then_inc(s["y"], 1)
            staggered(dve, step, BLOCKS, 2 * RING, RING)


def depool_phase(nc, io, keep):
    X, XN, LOG, C = keep["X"], keep["XN"], keep["LOG"], keep["C"]
    with ExitStack() as ctx:
        m = Mem(nc, ctx)
        sb, ps, sem = m.sb, m.ps, m.sem
        cr = sb("d_ctx", [P, RING, CTX])
        plug = sb("d_plug", [P, RING, P])
        Y = sb("d_Y", [P, RING, CHOICES, H])
        win, g_res = sb("d_win", [P, P]), sb("d_g_res", [P, 1])
        winG = sb("d_winG", [P, P])
        g_init, b_in = sb("d_g_init", [P, P]), sb("d_b_in", [1, P])
        rw = sb("d_rw", [P, E1])
        power_of = sb("d_power_of", [P, 3])
        square = sb("d_square", [P, CTX])
        hot, cg, GT = (sb("d_" + n, [P, RING, P]) for n in ("hot", "cg", "GT"))
        stat, stat2 = sb("d_stat", [P, RING, 6]), sb("d_stat2", [P, RING, 6])
        mv = sb("d_mv", [P, RING, 3, 2])
        ve = sb("d_ve", [P, RING, 3])
        factor = sb("d_factor", [P, RING, 3])
        z, xn = sb("d_z", [P, RING, P]), sb("d_xn", [P, RING, P])
        xT = sb("d_xT", [P, RING, 2, P])
        turned, Gp, lgp = (ps("d_" + n, [P, 512]) for n in ("turned", "Gp", "lgp"))
        Hp = ps("d_Hp", [P, 2, 512])
        s = {n: sem("d_" + n) for n in (
            "weights setup ss hot cg y1 x2 stat mv x3 stat2 mv2 ve factor z xn xTp xT Gp GT H kept lgp "
            "lg").split()}
        y_landed = [sem(f"d_y_landed{u}") for u in range(RING)]
        c_landed = [sem(f"d_c_landed{u}") for u in range(RING)]
        n_w = 16 * 5
        TE = [P, GROUP, E1]
        r = {n: sb("d_r_" + n, TE) for n in ("L", "a", "b", "rest", "rank", "full")}
        r.update({n: sb("d_r_" + n, [P, GROUP]) for n in ("t", "diff", "exp", "sum")})
        r.update({n: sb("d_r_" + n, [P, CHOICES, GROUP]) for n in ("top", "w", "none", "keep", "slot0", "slot")})
        r_hot, r_picked = sb("d_r_hot", [P, CHOICES, GROUP, E1]), sb("d_r_picked", [P, CHOICES, GROUP, E1])
        r_chosen, r_before = sb("d_r_chosen", TE, BF16), sb("d_r_earlier", [P, E1], BF16)
        r_group, r_base = sb("d_r_group", [P, E1]), sb("d_r_base", [P, E1])
        before, ones = sb("d_before", [P, P], BF16), sb("d_ones", [P, P], BF16)
        rank_ps = ps("d_rank_ps", [P, 512])
        rank = rank_ps[:, 0:GROUP * E1].rearrange("p (t e) -> p t e", t=GROUP)
        rows, index = sb("d_rows", [P, RING, CHOICES, ROW]), sb("d_index", [P, RING, CHOICES], U32)
        LINKS = 8 * GROUP
        assert GROUP == RING

        def group_real(k, v):
            return not isinstance(k, int) or 0 <= k - v - 3 * GROUP < TILES
        s.update({n: sem("d_" + n) for n in "chain exps_wanted exps counts_wanted counts ready weights1".split()})
        sent = [sem(f"d_sent{v}") for v in range(RING)]
        met = (s["setup"], 6)
        block = ctx.enter_context(nc.Block())

        @block.sync
        def _(sp):
            sp.dma_start(win[:], io["winT"]).then_inc(s["weights"], 16)
            sp.dma_start(rw[:], io["embT"]).then_inc(s["weights"], 16)
            sp.dma_start(g_res[:], io["L1_xattn_g_res"].rearrange("(p o) -> p o", o=1)).then_inc(s["weights"], 16)
            sp.dma_start(g_init[:], io["g_init"].partition_broadcast(P)).then_inc(s["weights"], 16)
            sp.dma_start(b_in[:], io["L1_xattn_b_in"].rearrange("(o d) -> o d", o=1)).then_inc(s["weights"], 16)

            def step(t, u):
                if not exists(t):
                    return
                at_least(sp, s["ss"], t - RING + 1)
                at_least(sp, s["cg"], t - RING + 1)
                at_least(sp, s["hot"], t - RING + 1)
                at_least(sp, s["x2"], t - RING + 1)
                sp.dma_start(Y[:, u].rearrange("p n c -> p (n c)"), row_of(io["result_tiles0"], t)
                             ).then_inc(y_landed[u], 16)
                sp.dma_start(cr[:, u, :], row_of(io["ctx_tiles"], t)).then_inc(c_landed[u], 16)
                sp.dma_start(plug[:, u, :], io["plug_rows"][bass.ds(t, 1)].rearrange("a c -> (a c)")
                             .partition_broadcast(P)).then_inc(c_landed[u], 16)
            staggered(sp, step, TILES, RING, RING)
            for e in range(E1):
                sp.dma_start(keep["WE1"][:, e, :], io["expert1_w"][e]).then_inc(s["weights1"], 16)
            sp.wait_ge(s["weights1"], 16 * E1)

        @block.gpsimd
        def _(pool):
            nc.gpsimd.memset(power_of[:], -0.5).then_inc(s["setup"], 1)
            nc.gpsimd.memset(r_before[:], 0.0).then_inc(s["setup"], 1)
            nc.gpsimd.tensor_copy(before[:], C[:, C_BEFORE:C_BEFORE + P]).then_inc(s["setup"], 1)
            nc.gpsimd.tensor_copy(ones[:], C[:, C_ONES:C_ONES + P]).then_inc(s["setup"], 1)
            nc.gpsimd.tensor_scalar(r_base[:], C[:, C_IOTA:C_IOTA + E1], float(CAPACITY), None,
                                    ALU.mult).then_inc(s["setup"], 1)
            pool.wait_ge(s["weights"], n_w)
            nc.gpsimd.tensor_scalar(winG[:], win[:], g_res[:], None, ALU.mult).then_inc(s["setup"], 1)
            pool.wait_ge(*met)

            def step(k, v):
                t = k - 4 * RING
                if exists(t):
                    wait_alone(pool, s["ready"], 3 * t + 3, *met)
                    for n in range(CHOICES):
                        nc.gpsimd.indirect_dma_start(io["xg1"], bass.IndirectOffsetOnAxis(ap=index[:, v, n:n + 1], axis=0),
                                                     rows[:, v, n, :], None, bounds_check=TOKENS - 1,
                                                     oob_is_err=False).then_inc(sent[v], 16)
                lo, hi = 0 if exists(k - 1) else 2, 3 if exists(k - 4) else 2
                if lo < hi:
                    if lo == 0:
                        wait_alone(pool, s["mv"], k, *met)
                        nc.gpsimd.tensor_scalar(ve[:, v, 0:1], mv[:, v, 0, 1:2], 1.0 + LN_EPS, LN_EPS * LN_EPS,
                                                ALU.mult, ALU.add).then_inc(s["ve"], 1)
                        wait_alone(pool, s["ss"], k, *met)
                    wait_alone(pool, s["mv2"], least(k - 3, TILES), *met)
                    lo1 = max(lo, 1)
                    nc.gpsimd.tensor_scalar(ve[:, v, lo1:hi], mv[:, v, lo1:hi, 1], LN_EPS, None,
                                            ALU.add).then_inc(s["ve"], 1)
                    wait_alone(pool, s["ve"], 2 * k if exists(k - 1) else k + TILES, *met)
                    nc.gpsimd.tensor_tensor(factor[:, v, lo:hi], ve[:, v, lo:hi], power_of[:, lo:hi],
                                            ALU.pow).then_inc(s["factor"], 1)
            staggered(pool, step, TILES, 5 * RING, RING, peel=RING)
            for v in range(RING):
                pool.wait_ge(sent[v], 16 * CHOICES * TILES // RING)

        @block.vector
        def _(dve):
            dve.wait_ge(s["weights"], n_w)
            dve.wait_ge(*met)
            W = keep["W"]

            def add_choice(t, u, n, name):
                nc.vector.scalar_tensor_tensor(tile_of(X, t), Y[:, u, n, :], W[:, n, bass.ds(t, 1)],
                                               tile_of(X, t), ALU.mult, ALU.add).then_inc(s[name], 1)

            def over_e(a):
                return a.unsqueeze(2).broadcast_to(TE)
            iota = C[:, C_IOTA:C_IOTA + E1].unsqueeze(1).broadcast_to(TE)
            links = [0]

            def after_link(k, v):
                if links[0] or not isinstance(k, int) or k - v > 3 * GROUP:
                    dve.wait_ge(s["chain"], (k - v - 3 * GROUP) * (LINKS // GROUP) + links[0])

            def link(ins, n=1):
                links[0] += n
                return ins.then_inc(s["chain"], n)

            def choose(k, v, values, n, part):
                after_link(k, v)
                if part == 0:
                    link(nc.vector.tensor_reduce(r["top"][:, n, :], values, AX.X, ALU.max))
                elif part == 1:
                    link(nc.vector.tensor_tensor(r["a"][:], values, over_e(r["top"][:, n, :]), ALU.is_equal))
                elif part == 2:
                    link(nc.vector.scalar_tensor_tensor(r["b"][:], r["a"][:], -float(E1), iota, ALU.mult, ALU.add))
                elif part == 3:
                    link(nc.vector.tensor_reduce(r["t"][:], r["b"][:], AX.X, ALU.min))
                elif part == 4:
                    link(nc.vector.tensor_tensor(r_hot[:, n], r["b"][:], over_e(r["t"][:]), ALU.is_equal))

            def first_choice(k, v, part):
                if part == 0:
                    links[0] = 0
                    wait_alone(dve, s["lg"], k - v - 2 * GROUP, *met)
                    link(nc.vector.tensor_copy(r["L"][:], LOG[:, bass.ds(k - v - 3 * GROUP, GROUP), :]))
                elif part < 6:
                    choose(k, v, r["L"][:], 0, part - 1)
                elif part == 6:
                    after_link(k, v)
                    link(nc.vector.scalar_tensor_tensor(r["rest"][:], r_hot[:, 0], NEG, r["L"][:], ALU.mult, ALU.add))

            def second_choice(k, v, part):
                if part < 5:
                    choose(k, v, r["rest"][:], 1, part)
                elif part == 5:
                    after_link(k, v)
                    link(nc.vector.tensor_tensor(r["diff"][:], r["top"][:, 1, :], r["top"][:, 0, :], ALU.subtract))
                elif part == 6:
                    after_link(k, v)
                    dve.sem_inc(s["exps_wanted"], GROUP)

            def weights_and_chosen(k, v, part):
                if part == 0:
                    dve.wait_ge(s["exps"], k - v - 2 * GROUP)
                    link(nc.vector.tensor_scalar(r["sum"][:], r["exp"][:], 1.0, None, ALU.add))
                elif part < 7:
                    after_link(k, v)
                if part == 1:
                    link(nc.vector.reciprocal(r["w"][:, 0, :], r["sum"][:]))
                elif part == 2:
                    link(nc.vector.tensor_tensor(r["w"][:, 1, :], r["exp"][:], r["w"][:, 0, :], ALU.mult))
                elif part == 3:
                    link(nc.vector.tensor_scalar(r["t"][:], r["w"][:, 1, :], 0.0, None, ALU.is_gt))
                elif part == 4:
                    link(nc.vector.tensor_tensor(r["a"][:], r_hot[:, 1], over_e(r["t"][:]), ALU.mult))
                elif part == 5:
                    link(nc.vector.tensor_tensor(r_chosen[:], r["a"][:], r_hot[:, 0], ALU.add))
                elif part == 6:
                    dve.sem_inc(s["counts_wanted"], GROUP)

            def slots_and_kept(k, v, part):
                if part == 0:
                    dve.wait_ge(s["counts"], k - v - 2 * GROUP)
                    link(nc.vector.tensor_tensor(r["rank"][:], rank, r_base[:].unsqueeze(1).broadcast_to(TE), ALU.add))
                    link(nc.vector.tensor_scalar(r["full"][:], rank, float(CAPACITY), float(OUT_OF_RANGE),
                                                 ALU.is_ge, ALU.mult))
                    link(nc.vector.tensor_reduce(r_group[:], r_chosen[:].rearrange("p t e -> p e t"), AX.X, ALU.add))
                    link(nc.vector.tensor_scalar(r["none"][:], r["w"][:], 0.0, float(OUT_OF_RANGE), ALU.is_le,
                                                 ALU.mult))
                else:
                    after_link(k, v)
                if part == 1:
                    link(nc.vector.tensor_tensor(r["rank"][:], r["rank"][:], r["full"][:], ALU.add))
                    link(nc.vector.tensor_tensor(r_before[:], r_before[:], r_group[:], ALU.add))
                elif part == 2:
                    four = [P, CHOICES, GROUP, E1]
                    link(nc.vector.tensor_tensor(r_picked[:], r_hot[:], r["rank"][:].unsqueeze(1).broadcast_to(four),
                                                 ALU.mult))
                elif part == 3:
                    link(nc.vector.tensor_reduce(r["slot0"][:], r_picked[:], AX.X, ALU.add))
                elif part == 4:
                    if not isinstance(k, int) or k - v > 3 * GROUP:
                        dve.wait_ge(s["ready"], (k - v - 3 * GROUP) * 3)
                    link(nc.vector.tensor_tensor(r["slot"][:], r["slot0"][:], r["none"][:], ALU.add))
                elif part == 5:
                    link(nc.vector.tensor_scalar(r["keep"][:], r["slot"][:], float(TOKENS), None, ALU.is_lt))
                elif part == 6:
                    assert 0 < LINKS - links[0]
                    link(nc.vector.tensor_tensor(W[:, :, bass.ds(k - v - 3 * GROUP, GROUP)], r["w"][:], r["keep"][:],
                                                 ALU.mult), LINKS - links[0])

            def route_part(k, v, part):
                if not group_real(k, v):
                    return
                if v < 3:
                    (first_choice, second_choice, weights_and_chosen)[v](k, v, part)
                elif part >= 2:
                    for late in range(part - 2, 7 if part == 6 else part - 1):
                        slots_and_kept(k, v, late)

            def step(k, v):
                w = (v - 2) % RING
                t, u = k - 3, (v - 3) % RING
                if exists(k - 3) or exists(k - 6):
                    dve.wait_ge(s["factor"], k - 2)
                if exists(t):
                    nc.vector.tensor_scalar(z[:, u, :], tile_of(X, t), mv[:, w, 0, 0:1], factor[:, w, 0:1],
                                            ALU.subtract, ALU.mult).then_inc(s["z"], 1)
                route_part(k, v, 0)
                old, new = k - 4, k - 1
                uo, un = v, (v - 1) % RING
                if exists(new):
                    dve.wait_ge(y_landed[un], slot_wait(new, un, 16))
                    add_choice(new, un, 0, "y1")
                route_part(k, v, 1)
                t, u = k - 6, (v - 6) % RING
                if exists(t):
                    at_least(dve, s["kept"], t - RING + 1)
                    nc.vector.tensor_scalar(xn[:, u, :], tile_of(X, t), mv[:, w, 2, 0:1], factor[:, w, 2:3],
                                            ALU.subtract, ALU.mult).then_inc(s["xn"], 1)
                route_part(k, v, 2)
                if exists(new):
                    dve.wait_ge(c_landed[un], slot_wait(new, un, 32))
                    at_least(dve, s["Gp"], new - RING + 1)
                    nc.vector.tensor_scalar(hot[:, un, :], plug[:, un, :], C[:, C_PART:C_PART + 1], None,
                                            ALU.is_equal).then_inc(s["hot"], 1)
                    wait_alone(dve, s["y1"], new + 1, *met)
                    add_choice(new, un, 1, "x2")
                route_part(k, v, 3)
                if exists(old):
                    dve.wait_ge(s["H"], old + 1)
                    nc.vector.tensor_tensor(tile_of(X, old), tile_of(X, old), Hp[:, v % 2, 0:P],
                                            ALU.add).then_inc(s["x3"], 1)
                if exists(new):
                    wait_alone(dve, s["x2"], new + 1, *met)
                    nc.vector.bn_stats(stat[:, un, :], tile_of(X, new)).then_inc(s["stat"], 1)
                route_part(k, v, 4)
                if exists(old):
                    wait_alone(dve, s["x3"], old + 1, *met)
                    nc.vector.bn_stats(stat2[:, uo, :], tile_of(X, old)).then_inc(s["stat2"], 1)
                if exists(new):
                    wait_alone(dve, s["stat"], new + 1, *met)
                    nc.vector.bn_aggr(mv[:, v, 0, :], stat[:, un, :]).then_inc(s["mv"], 1)
                route_part(k, v, 5)
                if exists(old):
                    wait_alone(dve, s["stat2"], old + 1, *met)
                    nc.vector.bn_aggr(mv[:, v, 2, :], stat2[:, uo, :]).then_inc(s["mv2"], 1)
                if exists(k - 7):
                    dve.wait_ge(s["lgp"], k - 6)
                    nc.vector.tensor_copy(tile_of(LOG, k - 7), lgp[:, 0:E1]).then_inc(s["lg"], 1)
                if exists(new):
                    at_least(dve, s["H"], new - RING + 1)
                    nc.vector.tensor_tensor(cg[:, un, :], cr[:, un, 0:H], g_init[:], ALU.mult).then_inc(s["cg"], 1)
                route_part(k, v, 6)
            staggered(dve, step, TILES, 5 * RING, RING, peel=RING)

        @block.tensor
        def _(pe):
            ident, decay = C[:, C_ID:C_ID + P], C[:, C_DECAY:C_DECAY + P]
            pe.wait_ge(s["weights"], n_w)
            pe.wait_ge(*met)

            def step(k, v):
                if v == 3 and group_real(k, v):
                    pe.wait_ge(s["counts_wanted"], k - v - 2 * GROUP)
                    nc.tensor.matmul(rank, before[:], r_chosen[:], start=True, stop=False)
                    for i in range(GROUP - 1):
                        nc.tensor.matmul(rank[:, i + 1:, :], ones[:], r_chosen[:, i, :].unsqueeze(1)
                                         .broadcast_to([P, GROUP - 1 - i, E1]), start=False, stop=False)
                    nc.tensor.matmul(rank, ones[:], r_before[:].unsqueeze(1).broadcast_to([P, GROUP, E1]), start=False,
                                     stop=True).then_inc(s["counts"], GROUP)
                t, u = k - 3, (v - 3) % RING
                mm = None
                at_least(pe, s["xT"], least(k - 3, TILES + 3))
                if exists(k - 6):
                    pe.wait_ge(s["xn"], k - 5)
                    mm = nc.tensor.transpose(turned[:, P:2 * P], xn[:, (v - 6) % RING, :], ident)
                if exists(t):
                    pe.wait_ge(s["z"], t + 1)
                    mm = nc.tensor.transpose(turned[:, 0:P], z[:, u, :], ident)
                if mm is not None:
                    mm.then_inc(s["xTp"], 1)
                if exists(k - 2):
                    pe.wait_ge(s["hot"], k - 1)
                    at_least(pe, s["GT"], k - 2)
                    nc.tensor.matmul(Gp[:, 0:P], decay, hot[:, (v - 2) % RING, :], start=True,
                                     stop=True).then_inc(s["Gp"], 1)
                if exists(t):
                    pe.wait_ge(s["xT"], k - 2)
                    at_least(pe, s["x3"], t - 1)
                    nc.tensor.matmul(Hp[:, u % 2, 0:P], C[0:1, C_ONES:C_ONES + P], b_in[:], start=True, stop=False)
                    nc.tensor.matmul(Hp[:, u % 2, 0:P], xT[:, v, 0, :], winG[:], start=False, stop=False)
                    pe.wait_ge(s["cg"], t + 1)
                    pe.wait_ge(s["GT"], t + 1)
                    nc.tensor.matmul(Hp[:, u % 2, 0:P], GT[:, u, :], cg[:, u, :], start=False, stop=True).then_inc(s["H"], 1)
                t = k - 6
                if exists(t):
                    pe.wait_ge(s["xT"], k - 2)
                    at_least(pe, s["lg"], t)
                    nc.tensor.matmul(lgp[:, 0:E1], xT[:, v, 1, :], rw[:], start=True, stop=True).then_inc(s["lgp"], 1)
            staggered(pe, step, TILES, 5 * RING, RING)

        @block.scalar
        def _(act):
            act.wait_ge(*met)

            def step(k, v):
                if v == 2 and group_real(k, v):
                    act.wait_ge(s["exps_wanted"], k - v - 2 * GROUP)
                    nc.scalar.activation(r["exp"][:], r["diff"][:], ACT.Exp).then_inc(s["exps"], GROUP)
                t = k - 4 * RING
                if exists(t):
                    act.wait_ge(s["chain"], (t - v) * (LINKS // GROUP) + LINKS)
                    at_least(act, sent[v], (t - v) * (16 * CHOICES // RING))
                    nc.scalar.copy(index[:, v, :], r["slot"][:, :, v]).then_inc(s["ready"], 1)
                    act.wait_ge(s["kept"], t + 1)
                    nc.scalar.copy(rows[:, v, :, 0:H], tile_of(XN, t).unsqueeze(1).broadcast_to([P, CHOICES, H])
                                   ).then_inc(s["ready"], 1)
                    places = C[:, C_PLACE:].rearrange("p (t n) -> p t n", n=CHOICES)
                    nc.scalar.copy(rows[:, v, :, H], tile_of(places, t)).then_inc(s["ready"], 1)
                t, u = k - 3, (v - 3) % RING
                if exists(t):
                    act.wait_ge(s["Gp"], t + 1)
                    act.wait_ge(s["factor"], k - 2)
                    at_least(act, s["H"], t - RING + 1)
                    nc.scalar.activation(GT[:, u, :], Gp[:, 0:P], ACT.Copy, 
                                         scale=factor[:, (v - 2) % RING, 1:2]).then_inc(s["GT"], 1)
                lo, hi = 0 if exists(k - 3) else 1, 2 if exists(k - 6) else 1
                if lo < hi:
                    act.wait_ge(s["xTp"], k - 2)
                    at_least(act, s["H"], least(k - 6, TILES))
                    at_least(act, s["lgp"], least(k - 9, TILES))
                    nc.scalar.copy(xT[:, v, lo:hi, :].rearrange("p a c -> p (a c)"),
                                   turned[:, lo * P:hi * P]).then_inc(s["xT"], 1)
                t, u = k - 1, (v - 1) % RING
                if exists(t):
                    act.wait_ge(c_landed[u], slot_wait(t, u, 32))
                    at_least(act, s["ss"], t)
                    at_least(act, s["factor"], k - RING)
                    nc.scalar.activation(square[:], cr[:, u, :], ACT.Square, scale=CTX ** -0.5,
                                         accum_out=mv[:, v, 1, 1:2]).then_inc(s["ss"], 1)
                t = k - 6
                if exists(t):
                    nc.scalar.copy(tile_of(XN, t), xn[:, (v - 6) % RING, :]).then_inc(s["kept"], 1)
            staggered(act, step, TILES, 5 * RING, RING)


def second_experts_phase(nc, io, keep):
    C = keep["C"]
    SUB, STEPS, PER = WIDE // P, TOKENS // WIDE, CAPACITY // WIDE
    with ExitStack() as ctx:
        m = Mem(nc, ctx)
        sb, ps, sem = m.sb, m.ps, m.sem
        WE = keep["WE1"]
        W = sb("f_w", [P, 2, 2 * F1])
        rows, place = sb("f_rows", [P, RING, SUB, ROW]), sb("f_place", [P, RING, SUB], U32)
        Y = sb("f_Y", [P, RING, SUB, P])
        xT, G = sb("f_xT", [P, 2, WIDE]), sb("f_G", [P, 2, CHUNKS1, WIDE])
        xTp, hid, yp = ps("f_xTp", [P, 2, WIDE]), ps("f_hid", [P, 2, CHUNKS1, WIDE]), ps("f_yp", [P, 2, WIDE])
        s = {n: sem("f_" + n) for n in "w xTp xT place hid relu yp y".split()}
        landed = [sem(f"f_landed{u}") for u in range(RING)]
        stored = [sem(f"f_stored{u}") for u in range(RING)]
        src = io["xg1"].rearrange("(k n p) c -> k p n c", p=P, n=SUB)
        block = ctx.enter_context(nc.Block())

        def blk(a, k):
            return a[k] if isinstance(k, int) else a[bass.ds(k, 1)].rearrange("a p n c -> (a p) n c")

        def real(k):
            return not isinstance(k, int) or 0 <= k < STEPS

        @block.sync
        def _(sp):
            def step(k, v):
                if real(k):
                    at_least(sp, s["xTp"], k - RING + 1)
                    at_least(sp, s["place"], k - RING + 1)
                    sp.dma_start(rows[:, v], blk(src, k)).then_inc(landed[v], 16)
            staggered(sp, step, STEPS, RING, RING)

        @block.gpsimd
        def _(pool):
            pool.wait_ge(s["y"], 1)

            def step(k, v):
                if real(k):
                    wait_alone(pool, s["y"], k + 1, s["y"], 1)
                    scatter_results(nc, pool, Y[:, v], place[:, v], io["results1"], stored[v])
            staggered(pool, step, STEPS, RING, RING)
            for u in range(RING):
                pool.wait_ge(stored[u], 16 * SUB * (STEPS // RING))

        @block.tensor
        def _(pe):
            ident = C[:, C_ID:C_ID + P]

            def step(k, v):
                if real(k):
                    pe.wait_ge(landed[v], slot_wait(k, v, 16))
                    at_least(pe, s["xT"], k - 1)
                    for n in range(SUB):
                        mm = nc.tensor.transpose(xTp[:, v % 2, n * P:(n + 1) * P], rows[:, v, n, 0:H], ident)
                    mm.then_inc(s["xTp"], 1)
                k, v = k - 1, (v - 1) % RING
                if real(k):
                    pe.wait_ge(s["w"], k - v % PER + PER)
                    pe.wait_ge(s["xT"], k + 1)
                    at_least(pe, s["relu"], k - 1)
                    for c in range(CHUNKS1):
                        mm = nc.tensor.matmul(hid[:, v % 2, c, :], W[:, v // PER, c * P:(c + 1) * P], xT[:, v % 2, :],
                                              start=True, stop=True)
                    mm.then_inc(s["hid"], 1)
                k, v = k - 1, (v - 1) % RING
                if real(k):
                    pe.wait_ge(s["relu"], k + 1)
                    at_least(pe, s["y"], k - 1)
                    for n in range(SUB):
                        for c in range(CHUNKS1):
                            mm = nc.tensor.matmul(yp[:, v % 2, n * P:(n + 1) * P], G[:, v % 2, c, n * P:(n + 1) * P],
                                                  W[:, v // PER, F1 + c * P:F1 + (c + 1) * P], start=c == 0,
                                                  stop=c == CHUNKS1 - 1)
                    mm.then_inc(s["yp"], 1)
            staggered(pe, step, STEPS, RING, RING)

        @block.scalar
        def _(act):
            def weights_of(e, slot):
                at_least(act, s["yp"], PER * (e - 1))
                nc.scalar.copy(W[:, slot, :], tile_of(WE, e)).then_inc(s["w"], PER)

            def step(k, v, e):
                at_least(act, s["yp"], k - 1)
                if v % PER == 0 and e is not None:
                    weights_of(e, (v // PER + 1) % 2)
                act.wait_ge(s["hid"], k + 1)
                nc.scalar.activation(G[:, v % 2], hid[:, v % 2], ACT.Relu).then_inc(s["relu"], 1)
            weights_of(0, 0)
            for k in range(RING):
                step(k, k, k // PER + 1)
            with act.Fori(1, STEPS // RING - 1) as i:
                for v in range(RING):
                    step(i * RING + v, v, i * (RING // PER) + (v // PER + 1))
            for k in range(STEPS - RING, STEPS):
                step(k, k % RING, k // PER + 1 if k // PER + 1 < E1 else None)

        @block.vector
        def _(dve):
            def step(k, v):
                if real(k):
                    dve.wait_ge(s["xTp"], k + 1)
                    at_least(dve, s["hid"], k - 1)
                    nc.vector.tensor_copy(xT[:, v % 2, :], xTp[:, v % 2, :]).then_inc(s["xT"], 1)
                    if not isinstance(k, int) or k >= RING:
                        dve.wait_ge(stored[v], 16 * SUB * (k // RING) if isinstance(k, int) else (k - v) * 4 * SUB)
                    places_of(nc, rows[:, v], place[:, v]).then_inc(s["place"], 1)
                k, v = k - 2, (v - 2) % RING
                if real(k):
                    dve.wait_ge(s["yp"], k + 1)
                    nc.vector.tensor_copy(Y[:, v].rearrange("p n c -> p (n c)"), yp[:, v % 2, :]).then_inc(s["y"], 1)
            staggered(dve, step, STEPS, RING, RING)


def output_phase(nc, io, keep):
    with ExitStack() as ctx:
        m = Mem(nc, ctx)
        Y = m.sb("o_Y", [P, RING, GROUP, CHOICES, H])
        landed = [m.sem(f"o_landed{u}") for u in range(RING)]
        added, out_done = m.sem("o_added"), m.sem("o_out_done")
        X, grouped = keep["X"], keep["X"][:].rearrange("p (g t) c -> p g (t c)", t=GROUP)
        W = keep["W"]
        results = io["result_tiles1"].rearrange("(g t) p c -> g p t c", t=GROUP)
        out = io["out_tiles"].rearrange("(g t) p c -> g p t c", t=GROUP)
        block = ctx.enter_context(nc.Block())

        def over_groups(eng, step):
            for g in range(RING):
                step(g, g)
            with eng.Fori(1, GROUPS // RING) as i:
                for v in range(RING):
                    step(i * RING + v, v)

        def group_of(a, g):
            return a[g] if isinstance(g, int) else a[bass.ds(g, 1)].rearrange("a p t c -> (a p) t c")

        @block.sync
        def _(sp):
            def step(g, v):
                at_least(sp, added, CHOICES * GROUP * (g - RING + 1))
                sp.dma_start(Y[:, v].rearrange("p t n c -> p t (n c)"), group_of(results, g)).then_inc(landed[v], 16)
            over_groups(sp, step)

        @block.vector
        def _(dve):
            def step(g, v):
                dve.wait_ge(landed[v], slot_wait(g, v, 16))
                for n in range(CHOICES):
                    for i in range(GROUP):
                        t = g * GROUP + i
                        if n == 1:
                            dve.wait_ge(added, g * (CHOICES * GROUP) + i + 1)
                        nc.vector.scalar_tensor_tensor(tile_of(X, t), Y[:, v, i, n, :], W[:, n, bass.ds(t, 1)],
                                                       tile_of(X, t), ALU.mult, ALU.add).then_inc(added, 1)
            over_groups(dve, step)

        @block.scalar
        def _(act):
            def step(g, v):
                act.wait_ge(added, (g + 1) * (CHOICES * GROUP))
                act.dma_start(group_of(out, g), tile_of(grouped, g).rearrange("p (t c) -> p t c", t=GROUP)
                              ).then_inc(out_done, 16)
            over_groups(act, step)
            act.wait_ge(out_done, 16 * GROUPS)


def build(nc, io, out):
    zeroed = []
    io = dict(io)
    for name, rows, cols in (("xg0", SLOTS, ROW), ("xg1", TOKENS, ROW), ("results0", CHOICES * TOKENS, H),
                             ("results1", CHOICES * TOKENS, H)):
        io[name] = nc.dram_tensor(name, [rows, cols], F32).ap()
    io["plug"] = nc.dram_tensor("plug", [BATCH, SEQ], F32).ap()
    for name, n in (("xg0", ZEROS), ("xg1", ZEROS), ("results1", 2048)):
        flat = io[name].rearrange("r c -> (r c)").rearrange("(k p n) -> k p n", p=P, n=n)
        zeroed += [flat[i] for i in range(flat.shape[0])]
    assert len(zeroed) <= 3 * (2 * RING - 1)
    for n in range(2):
        io[f"result_tiles{n}"] = io[f"results{n}"].rearrange("(t p n) c -> t p (n c)", p=P, n=CHOICES)
    io["zeroed"] = zeroed
    io["x_tiles"] = io["x"].rearrange("(t b) s d -> t (b s) d", b=2)
    io["out_tiles"] = out.rearrange("(t b) s d -> t (b s) d", b=2)
    io["plug_rows"] = io["plug"].rearrange("(t b) s -> t (b s)", b=2)
    io["ctx_tiles"] = io["ctx_2048"].rearrange("(t b) s d -> t (b s) d", b=2)
    io["mask_rows"] = io["mask_BxS2_fk1"].rearrange("(t b) s -> t (b s)", b=2)
    io["mask_pairs"] = io["mask_BxS2_fk1"].rearrange("(t b) s -> t b s", b=2)
    with ExitStack() as ctx:
        m = Mem(nc, ctx)
        keep = {
            "X": m.sb("X", [P, TILES, H]), "XN": m.sb("XN", [P, TILES, H]),
            "LOG": m.sb("LOG", [P, TILES, E0]), "C": m.sb("C", [P, C_COLS]),
            "W": m.sb("WEIGHT", [P, 2, TILES]), "SLOT": m.sb("SLOT", [P, TILES, 2], U32),
            "OWNER": m.sb("OWNER", [1, BLOCKS], I32),
        }
        with ExitStack() as weights:
            keep["WE"] = Mem(nc, weights).sb("WE", [P, E0, W_COLS])
            with ExitStack() as inner:
                keep["XNT"] = Mem(nc, inner).sb("XNT", [P, TILES, P])
                attention_phase(nc, io, keep)
                shared_phase(nc, io, keep)
            experts_phase(nc, io, keep)
        keep["WE1"] = m.sb("WE1", [P, E1, 2 * F1])
        depool_phase(nc, io, keep)
        second_experts_phase(nc, io, keep)
        output_phase(nc, io, keep)


def kernel(**inputs):
    import numpy as _np
    import concourse.bacc as _bacc
    from concourse import mybir as _mybir
    from concourse.bass_utils import run_bass_kernel_spmd as _run

    a = {k: _np.asarray(v) for k, v in inputs.items()}
    T, ctx = _np.transpose, a["ctx_2048"].reshape(TILES, P, 2, P)
    a["consts"] = constants()
    ctx = T(ctx, (0, 3, 2, 1)).reshape(TILES, P, 2, 2, 1, SEQ)
    a["ctxT"] = _np.broadcast_to(ctx, (TILES, P, 2, 2, 2, SEQ)).reshape(TILES, P, 4 * P)
    a["maskT"] = a["mask_BxS2_fk1"].T
    wsrc = a["L0_xattn_W_src"].reshape(2, H, 2, P)
    a["wkT"] = T(wsrc[0], (2, 1, 0)).reshape(P, 2 * P)
    a["wvT"] = T(wsrc[1], (2, 1, 0)).reshape(P, 2 * P)
    a["b_k"], a["b_v"] = a["L0_xattn_b_src"][:H], a["L0_xattn_b_src"][H:]
    a["wqT"] = a["L0_xattn_W_tgt"].T
    a["woT"] = T(a["L0_xattn_W_out"].reshape(H, 2, P), (2, 1, 0)).reshape(P, 2 * P)

    def ffn(up, down, up_b, down_b):
        n = up.shape[0]
        return _np.concatenate([up, T(down.reshape(n, CHUNKS0, P, H), (0, 2, 1, 3)).reshape(n, P, F0),
                                T(up_b.reshape(n, CHUNKS0, P), (0, 2, 1)),
                                _np.broadcast_to(down_b[:, None, :], (n, P, H))], axis=2)
    a["expert_w"] = ffn(a["L0_ffn_up_w"], a["L0_ffn_down_w"], a["L0_ffn_up_b"], a["L0_ffn_down_b"])
    a["shared_w"] = ffn(a["L0_ffn_sh_up_w"][None], a["L0_ffn_sh_down_w"][None], a["L0_ffn_sh_up_b"][None],
                        a["L0_ffn_sh_down_b"][None])[0]
    a["winT"] = a["L1_xattn_W_in"].T
    a["embT"] = a["L1_ffn_expert_embeddings"].T
    a["g_init"] = a["L1_xattn_g_init"][:H]
    first, second = a["L1_ffn_first_linear"], a["L1_ffn_second_linear"]
    a["expert1_w"] = _np.concatenate([T(first, (0, 2, 1)),
                                      T(second.reshape(E1, H, CHUNKS1, P), (0, 3, 2, 1)).reshape(E1, P, F1)], axis=2)
    names = ["ctx_2048", "winT", "embT", "g_init", "L1_xattn_g_res", "L1_xattn_b_in", "expert1_w", "x", "mask_BxS2_fk1", "consts", "ctxT", "maskT", "wkT", "wvT", "b_k", "b_v", "wqT", "woT",
             "L0_xattn_b_tgt", "L0_xattn_b_out", "L0_ffn_router_b", "L0_ffn_router_w",
             "mask_BxS2_if0", "expert_w", "shared_w"]
    nc = _bacc.Bacc("TRN2", target_bir_lowering=False, num_devices=1)
    arrays, io = {}, {}
    for name in names:
        v = _np.ascontiguousarray(a[name])
        arrays["in_" + name] = v
        io[name] = nc.dram_tensor("in_" + name, v.shape, _mybir.dt.from_np(v.dtype), kind="ExternalInput").ap()
    out = nc.dram_tensor("out_0", (BATCH, SEQ, H), _mybir.dt.float32, kind="ExternalOutput").ap()
    build(nc, io, out)
    r = _run(nc, [arrays], core_ids=[0])
    return r.results[0]["out_0"]
```
